# Optimizing a Trainium2 kernel written in Bass

```python
import numpy as np
import jax
import jax.numpy as jnp

def _softmax(x, axis=-1):
    return jax.nn.softmax(x, axis=axis)

def _gelu(x):
    return jax.nn.gelu(x, approximate=True)

def _silu(x):
    return jax.nn.silu(x)

def _sigmoid(x):
    return jax.nn.sigmoid(x)

def _layernorm(x, axis=-1, eps=1e-05):
    m = jnp.mean(x, axis=axis, keepdims=True)
    v = jnp.var(x, axis=axis, keepdims=True)
    return (x - m) / jnp.sqrt(v + eps)

def _scatter_add(tgt, idx, src, axis=0):
    return tgt.at[idx].add(src)

def _segment_sum(src, seg, n):
    return jax.ops.segment_sum(src, seg, n)
kernel_name = 'mk_lm_tower_d1_tok_ids2048_r4_52a10f'

def setup_inputs(seed: int=0):
    np.random.seed(seed)
    _w = jnp.asarray

    def _rec_inputs():
        import jax
        import jax.numpy as jnp
        _rk = jax.random.key(seed)
        x = jax.random.randint(jax.random.fold_in(_rk, 1), (8, 256), 0, 12564, jnp.int32)
        return x
    x = _rec_inputs()

    def _L0_tok_setup():
        import jax, jax.numpy as jnp
        import numpy as np
        VOCAB = 50257
        D_MODEL = 512
        RANK = max(64, int(D_MODEL * 0.125))
        key = jax.random.key(seed)
        k1, k2, k3 = jax.random.split(key, 3)
        x = jax.random.randint(k1, (8, 1024), 0, VOCAB, dtype=jnp.int64)
        embed_low = jax.random.normal(k2, (VOCAB, RANK), dtype=jnp.float32)
        bound = 1.0 / np.sqrt(RANK)
        project_up = jax.random.uniform(k3, (D_MODEL, RANK), minval=-bound, maxval=bound, dtype=jnp.float32)
        return {'x': x, 'embed_low': embed_low, 'project_up': project_up}
    _L0_tok_all = _L0_tok_setup()
    _L0_tok_in = {k: v for k, v in _L0_tok_all.items() if k in ('embed_low', 'project_up')}
    del _L0_tok_all

    def _L0_attn_setup():
        import jax, jax.numpy as jnp
        import numpy as np
        B, S, H = (2, 512, 512)
        N_HEADS = 16
        HEAD_DIM = H // N_HEADS
        key = jax.random.key(seed)
        k1, k2, k3 = jax.random.split(key, 3)
        lim_in = float(np.sqrt(6.0 / (H + 3 * H)))
        lim_out = float(np.sqrt(6.0 / (H + H)))
        return {'hidden_states': jax.random.normal(k1, (B, S, H), dtype=jnp.float32), 'W_in': jax.random.uniform(k2, (3 * H, H), jnp.float32, -lim_in, lim_in), 'b_in': jnp.zeros((3 * H,), jnp.float32), 'W_out': jax.random.uniform(k3, (H, H), jnp.float32, -lim_out, lim_out), 'b_out': jnp.zeros((H,), jnp.float32)}
    _L0_attn_all = _L0_attn_setup()
    _L0_attn_in = {k: v for k, v in _L0_attn_all.items() if k in ('W_in', 'b_in', 'W_out', 'b_out')}
    del _L0_attn_all

    def _L0_ffn_setup():
        import jax, jax.numpy as jnp
        import numpy as np
        HIDDEN = 512
        INTER = 2048
        COMPRESSION = 128.9

        def _n_ctrl(out_size, in_size):
            return max(16, int(out_size * in_size / COMPRESSION))

        def _catmull_rom_grid(n_ctrl, n_samples):
            t = np.linspace(0.0, n_ctrl - 1.0, n_samples, dtype=np.float64)
            i = np.clip(np.floor(t).astype(np.int64), 0, n_ctrl - 2)
            f = (t - i).astype(np.float32)
            idx = np.stack([np.clip(i + k, 0, n_ctrl - 1) for k in (-1, 0, 1, 2)], axis=0)
            return (jnp.asarray(idx.astype(np.int32)), jnp.asarray(f))

        def spline_reconstruct(control_points, out_size, in_size):
            n = out_size * in_size
            idx, f = _catmull_rom_grid(control_points.shape[0], n)
            p0, p1, p2, p3 = (control_points[idx[0]], control_points[idx[1]], control_points[idx[2]], control_points[idx[3]])
            f2 = f * f
            f3 = f2 * f
            w = 0.5 * (2.0 * p1 + (p2 - p0) * f + (2.0 * p0 - 5.0 * p1 + 4.0 * p2 - p3) * f2 + (3.0 * p1 - p0 - 3.0 * p2 + p3) * f3)
            return w.reshape(out_size, in_size)
        key = jax.random.key(seed)
        k0, k1, k2, k3 = jax.random.split(key, 4)
        hidden_states = jax.random.normal(k0, (4, 512, HIDDEN), dtype=jnp.float32)
        gate_cp = jax.random.normal(k1, (_n_ctrl(INTER, HIDDEN),), dtype=jnp.float32) * 0.02
        up_cp = jax.random.normal(k2, (_n_ctrl(INTER, HIDDEN),), dtype=jnp.float32) * 0.02
        down_cp = jax.random.normal(k3, (_n_ctrl(HIDDEN, INTER),), dtype=jnp.float32) * 0.02
        return {'hidden_states': hidden_states, 'gate_cp': gate_cp, 'up_cp': up_cp, 'down_cp': down_cp}
    _L0_ffn_all = _L0_ffn_setup()
    _L0_ffn_in = {k: v for k, v in _L0_ffn_all.items() if k in ('gate_cp', 'up_cp', 'down_cp')}
    del _L0_ffn_all
    return {'x': x, 'L0_tok_embed_low': _L0_tok_in['embed_low'], 'L0_tok_project_up': _L0_tok_in['project_up'], 'L0_attn_W_in': _L0_attn_in['W_in'], 'L0_attn_b_in': _L0_attn_in['b_in'], 'L0_attn_W_out': _L0_attn_in['W_out'], 'L0_attn_b_out': _L0_attn_in['b_out'], 'L0_ffn_gate_cp': _L0_ffn_in['gate_cp'], 'L0_ffn_up_cp': _L0_ffn_in['up_cp'], 'L0_ffn_down_cp': _L0_ffn_in['down_cp']}

def reference(x, L0_tok_embed_low, L0_tok_project_up, L0_attn_W_in, L0_attn_b_in, L0_attn_W_out, L0_attn_b_out, L0_ffn_gate_cp, L0_ffn_up_cp, L0_ffn_down_cp):
    import jax
    import jax.numpy as jnp

    def _L0_tok_ref(x, embed_low, project_up):
        import jax, jax.numpy as jnp
        import numpy as np
        VOCAB = 50257
        D_MODEL = 512
        RANK = max(64, int(D_MODEL * 0.125))
        low = embed_low[x]
        return jnp.einsum('bsr,dr->bsd', low, project_up)

    def _L0_attn_ref(hidden_states, W_in, b_in, W_out, b_out):
        import jax, jax.numpy as jnp
        import numpy as np
        B, S, H = (2, 512, 512)
        N_HEADS = 16
        HEAD_DIM = H // N_HEADS
        b, s, h = hidden_states.shape
        qkv = hidden_states @ W_in.T + b_in
        q, k, v = jnp.split(qkv, 3, axis=-1)

        def to_heads(x):
            return x.reshape(b, s, N_HEADS, HEAD_DIM).transpose(0, 2, 1, 3)
        q, k, v = (to_heads(q), to_heads(k), to_heads(v))
        scale = HEAD_DIM ** (-0.5)
        scores = jnp.einsum('bnqd,bnkd->bnqk', q, k) * scale
        causal = jnp.triu(jnp.ones((s, s), dtype=bool), k=1)
        scores = jnp.where(causal, -jnp.inf, scores)
        weights = jax.nn.softmax(scores, axis=-1)
        attn = jnp.einsum('bnqk,bnkd->bnqd', weights, v)
        attn = attn.transpose(0, 2, 1, 3).reshape(b, s, h)
        return attn @ W_out.T + b_out

    def _L0_ffn_ref(hidden_states, gate_cp, up_cp, down_cp):
        import jax, jax.numpy as jnp
        import numpy as np
        HIDDEN = 512
        INTER = 2048
        COMPRESSION = 128.9

        def _n_ctrl(out_size, in_size):
            return max(16, int(out_size * in_size / COMPRESSION))

        def _catmull_rom_grid(n_ctrl, n_samples):
            t = np.linspace(0.0, n_ctrl - 1.0, n_samples, dtype=np.float64)
            i = np.clip(np.floor(t).astype(np.int64), 0, n_ctrl - 2)
            f = (t - i).astype(np.float32)
            idx = np.stack([np.clip(i + k, 0, n_ctrl - 1) for k in (-1, 0, 1, 2)], axis=0)
            return (jnp.asarray(idx.astype(np.int32)), jnp.asarray(f))

        def spline_reconstruct(control_points, out_size, in_size):
            n = out_size * in_size
            idx, f = _catmull_rom_grid(control_points.shape[0], n)
            p0, p1, p2, p3 = (control_points[idx[0]], control_points[idx[1]], control_points[idx[2]], control_points[idx[3]])
            f2 = f * f
            f3 = f2 * f
            w = 0.5 * (2.0 * p1 + (p2 - p0) * f + (2.0 * p0 - 5.0 * p1 + 4.0 * p2 - p3) * f2 + (3.0 * p1 - p0 - 3.0 * p2 + p3) * f3)
            return w.reshape(out_size, in_size)
        gate_w = spline_reconstruct(gate_cp, INTER, HIDDEN)
        up_w = spline_reconstruct(up_cp, INTER, HIDDEN)
        down_w = spline_reconstruct(down_cp, HIDDEN, INTER)
        gate = jnp.einsum('bsh,ih->bsi', hidden_states, gate_w)
        up = jnp.einsum('bsh,ih->bsi', hidden_states, up_w)
        inter = jax.nn.silu(gate) * up
        return jnp.einsum('bsi,hi->bsh', inter, down_w)
    h = _L0_tok_ref(x, L0_tok_embed_low, L0_tok_project_up)
    h = h + _L0_attn_ref(_layernorm(h, axis=-1), L0_attn_W_in, L0_attn_b_in, L0_attn_W_out, L0_attn_b_out)
    h = h + _L0_ffn_ref(_layernorm(h, axis=-1), L0_ffn_gate_cp, L0_ffn_up_cp, L0_ffn_down_cp)
    return h

_drawn_inputs = setup_inputs


def setup_inputs(seed=0):
    import zlib

    import numpy as np

    out = dict(_drawn_inputs(seed))
    spreads = {'L0_attn_b_in': (0.0, 0.1), 'L0_attn_b_out': (0.0, 0.1)}
    factors = {}
    for name, (base, spread) in spreads.items():
        noise = np.random.default_rng([zlib.crc32(name.encode()), seed]).standard_normal(out[name].shape)
        drawn = base * np.exp(spread * noise) if base else spread * noise
        out[name] = jnp.asarray(drawn.astype(out[name].dtype))
    for name, factor in factors.items():
        out[name] = (out[name] * factor).astype(out[name].dtype)
    return out
```

```python
from contextlib import ExitStack
from math import comb

import numpy as np

import concourse.bass as bass
from concourse import mybir

F32 = mybir.dt.float32
F32R = mybir.dt.float32r
U32 = mybir.dt.uint32
U8 = mybir.dt.uint8
ALU = mybir.AluOpType
ACT = mybir.ActivationFunctionType

P = 128
HID = 512
INTER = 2048
BATCH, SEQ = 8, 256
TOKENS = BATCH * SEQ
RANK = 64
HEADS, HEAD_DIM = 16, 32
EPS = 1e-5
SCALE = float(HEAD_DIM) ** -0.5
MASKED = -1e30
LOWEST = -3e38

BLOCK_TILES = 4
BLOCK = BLOCK_TILES * P
STEPS = TOKENS // BLOCK
TILES = TOKENS // P
KT = HID // P
MT = INTER // P
BLOCK_SEQS = BLOCK // SEQ
PAIRS = BLOCK_SEQS * HEADS

N_WEIGHTS = HID * INTER
N_CTRL = max(16, int(N_WEIGHTS / 128.9))
DEG = 4
WINDOWS = 4
GROUPS = 4
WIN = 32
PITCH = 129
SEGS = WINDOWS + 1
MOM = SEGS * DEG
FEAT = 32
STACK = 3 * FEAT
U_SCALE = 64.0
D_SEGS = 17
D_K = D_SEGS * DEG
D_SCALE = 128.0
G_WIN = SEGS + 3
D_WIN = D_SEGS + 3



def _grid():
    t = np.linspace(0.0, N_CTRL - 1.0, N_WEIGHTS, dtype=np.float64)
    return np.clip(np.floor(t).astype(np.int64), 0, N_CTRL - 2), (N_CTRL - 1.0) / (N_WEIGHTS - 1)


_CR = 0.5 * np.array([[0, 2, 0, 0], [-1, 0, 1, 0], [2, -5, 4, -1], [-1, 3, -3, 1]], np.float64)


def _psi(center, scale):
    out = np.zeros((4,) + center.shape + (DEG,))
    for d in range(DEG):
        for e in range(d, DEG):
            out[..., d] += np.multiply.outer(_CR[e], comb(e, d) * center ** (e - d) * scale ** d)
    return out


def _tables():
    interval, step = _grid()
    rows = interval.reshape(INTER, HID)
    first = rows[:, 0]
    ends = np.array([[np.searchsorted(r, r[0] + 1 + c) for c in range(WINDOWS)] for r in rows])
    start = PITCH * np.arange(WINDOWS)[None] + WIN * np.arange(GROUPS)[:, None]
    fits = ((ends[:, None] >= start) & (ends[:, None] <= start + WIN + 1)) | (
        (ends[:, None] >= HID) & (start + WIN + 1 >= HID))
    fits = fits.all(2)
    group = [[] for _ in range(GROUPS)]
    for i in sorted(range(INTER), key=lambda i: (fits[i].sum(), int(np.argmax(fits[i])))):
        options = np.flatnonzero(fits[i])
        group[next(g for g in options if len(group[g]) < INTER // GROUPS)].append(i)
    assert all(len(g) == INTER // GROUPS for g in group)
    order = np.concatenate([np.array(sorted(g)) for g in group])
    tile = order.reshape(MT, P)

    def center(g, s):
        return PITCH * s + WIN * g - 48

    where = np.array([[PITCH * c + WIN * g + j for c in range(WINDOWS) for j in range(WIN)] for g in range(GROUPS)])
    spare = where >= HID
    where = np.where(spare, (where - HID + 1) * PITCH - 1, where)

    psi = np.zeros((4, INTER, SEGS, DEG))
    phi = np.zeros((5, INTER, WINDOWS))
    for n, i in enumerate(order):
        g = n // (INTER // GROUPS)
        s = np.arange(SEGS)
        f0 = (i * HID + center(g, s)) * step - (first[i] + s)
        psi[:, n] = _psi(f0, U_SCALE * step)
        for c in range(WINDOWS):
            h = start[g, c] + WIN
            if h < HID and rows[i, h] == first[i] + c:
                f = (i * HID + h) * step - (first[i] + c)
                phi[0:4, n, c] += _CR.T @ (f ** np.arange(4))
                phi[1:5, n, c] -= _CR.T @ ((f - 1) ** np.arange(4))

    moments = np.zeros((P, GROUPS, KT, FEAT))
    for g in range(GROUPS):
        for t in range(KT):
            for r in range(P):
                h = where[t, r]
                if t == g and not spare[t, r]:
                    continue
                s = int((h >= start[g] + WIN).sum())
                moments[r, g, t, DEG * s:DEG * s + DEG] = ((h - center(g, s)) / U_SCALE) ** np.arange(DEG)
                for c in range(WINDOWS):
                    if h == start[g, c] + WIN:
                        moments[r, g, t, MOM + c] = 1.0
    moments = np.concatenate([moments] * 3, axis=3)

    evaluate = np.zeros((MOM, GROUPS, 2, P))
    side = np.zeros((P, INTER), np.uint8)
    for g in range(GROUPS):
        for r in range(P):
            if spare[g, r]:
                continue
            c, h = r // WIN, where[g, r]
            for x in range(2):
                u = (h - center(g, c + x)) / U_SCALE
                evaluate[DEG * (c + x):DEG * (c + x + 1), g, x, r] = u ** np.arange(DEG)
            n = slice(g * INTER // GROUPS, (g + 1) * INTER // GROUPS)
            side[r, n] = rows[order[n], h] - first[order[n]] - c
    assert side.max() == 1

    d_first = interval.reshape(HID, INTER)[:, 0]
    s = np.arange(D_SEGS)
    f0 = (np.arange(HID)[:, None] * INTER + PITCH * s) * step - (d_first[:, None] + s)
    d_psi = _psi(f0, D_SCALE * step)
    d_eval = np.zeros((D_K, MT, 2, P))
    d_side = np.zeros((P, MT, HID), np.uint8)
    low = np.floor(np.arange(INTER) * step).astype(np.int64)
    for m in range(MT):
        for r in range(P):
            i = tile[m, r]
            for x in range(2):
                k = low[i] + x
                d_eval[DEG * k:DEG * k + DEG, m, x, r] = ((i - PITCH * k) / D_SCALE) ** np.arange(DEG)
            d_side[r, m] = interval.reshape(HID, INTER)[:, i] - d_first - low[i]
    assert d_side.max() == 1

    def by_partition(a, lead):
        a = a.reshape(a.shape[:lead] + (-1, P) + a.shape[lead + 1:])
        return np.moveaxis(a, lead + 1, 0).reshape(P, -1)

    causal = np.where(np.arange(P)[None] > np.arange(P)[:, None], MASKED, 0.0)
    f32 = {
        "c_psi": by_partition(psi, 1), "c_phi": by_partition(phi, 1), "c_moments": moments.reshape(P, -1),
        "c_evaluate": evaluate.reshape(MOM, -1), "c_dpsi": by_partition(d_psi, 1), "c_deval": d_eval.reshape(D_K, -1),
        "c_mask": np.concatenate([causal, np.zeros((P, P)), causal], 1), "c_ident": np.eye(P),
    }
    tables = {k: np.ascontiguousarray(v, np.float32) for k, v in f32.items()}
    tables["c_side"] = side.view(np.uint32)
    tables["c_dside"] = d_side.reshape(P, -1).view(np.uint32)
    return tables, first[order], d_first


def _windows(points, starts, width, tiles):
    padded = np.concatenate([points[:1], points, np.repeat(points[-1:], D_WIN)])
    rows = np.stack([padded[s:s + width] for s in starts])
    return np.ascontiguousarray(rows.reshape(tiles, P, width).transpose(1, 0, 2).reshape(P, -1))



def build(nc, a, out):
    with ExitStack() as top:
        def psum(name):
            return top.enter_context(nc.psum_tensor(name, [P, 512], F32))

        bank = [psum(f"bank{n}") for n in range(8)]

        def sems(*names):
            return [top.enter_context(nc.semaphore(n)) for n in names]

        h_all = top.enter_context(nc.sbuf_tensor("h_all", [P, TILES, HID], F32))
        ident = top.enter_context(nc.sbuf_tensor("ident", [P, P], F32))
        with ExitStack() as ctx:
            attention(nc, a, ctx, sems, bank, h_all, ident)
        with ExitStack() as ctx:
            ffn(nc, a, out, ctx, sems, bank, h_all, ident)


def chained(engine, sem):
    count = [0]

    def link(instruction):
        count[0] += 1
        instruction.then_inc(sem, 1)
        engine.wait_ge(sem, count[0])
    return link


def apart(engine, tick):
    engine.sem_inc(tick, 1)


def attention(nc, a, ctx, sems, bank, h_all, ident):
    def sb(name, shape, dt=F32, where=ctx):
        return where.enter_context(nc.sbuf_tensor(name, shape, dt))

    win_hi = sb("win_hi", [P, KT, 3 * HID], F32R)
    win_lo = sb("win_lo", [P, KT, 3 * HID], F32R)
    wout_hi = sb("wout_hi", [P, KT, HID], F32R)
    wout_lo = sb("wout_lo", [P, KT, HID], F32R)
    up_hi = sb("up_hi", [P, HID], F32R)
    up_lo = sb("up_lo", [RANK, HID], F32R)
    low_all = sb("low_all", [P, TILES, RANK])
    tok = sb("tok", [P, TILES], U32)
    bias_qk = sb("bias_qk", [P, 2 * KT])
    bias_v = sb("bias_v", [P, HID])
    bias_out = sb("bias_out", [P, HID])
    mask = sb("mask", [P, 3 * P])

    loaded, split_hi, split_lo, gathered, const_in, tok_in = sems(
        "loaded", "split_hi", "split_lo", "gathered", "const_in", "tok_in")

    with ExitStack() as prep:
        win_f = sb("win_f", [P, KT, 3 * HID], where=prep)
        wout_f = sb("wout_f", [P, KT, HID], where=prep)
        up_f = sb("up_f", [P, HID], where=prep)
        parts = [(up_f[:, :], up_hi[:, :])] + [(win_f[:, k, :], win_hi[:, k, :]) for k in range(KT)] \
            + [(wout_f[:, k, :], wout_hi[:, k, :]) for k in range(KT)]
        rests = [(up_f[0:RANK, :], up_hi[0:RANK, :], up_lo[:, :])] \
            + [(win_f[:, k, :], win_hi[:, k, :], win_lo[:, k, :]) for k in range(KT)] \
            + [(wout_f[:, k, :], wout_hi[:, k, :], wout_lo[:, k, :]) for k in range(KT)]

        block = prep.enter_context(nc.Block())

        @block.sync
        def _(sp):
            sp.dma_start(tok[:, :], a["tokens"]).then_inc(tok_in, 16)
            for half in range(2):
                sp.dma_start(up_f[half * RANK:(half + 1) * RANK, :], a["up_t"]).then_inc(loaded, 16)
            w = a["w_in_t"].rearrange("(k p) n -> p k n", p=P)
            for k in range(KT):
                sp.dma_start(win_f[:, k, :], w[:, k, :]).then_inc(loaded, 16)
            w = a["w_out_t"].rearrange("(k p) n -> p k n", p=P)
            for k in range(KT):
                sp.dma_start(wout_f[:, k, :], w[:, k, :]).then_inc(loaded, 16)
            sp.dma_start(ident[:, :], a["c_ident"]).then_inc(const_in, 16)
            sp.dma_start(bias_qk[:, :], a["b_qk"]).then_inc(const_in, 16)
            sp.dma_start(bias_v[:, :], a["b_v"].broadcast_to([P, HID])).then_inc(const_in, 16)
            sp.dma_start(bias_out[:, :], a["b_out"].broadcast_to([P, HID])).then_inc(const_in, 16)
            sp.dma_start(mask[:, :], a["c_mask"]).then_inc(const_in, 16)
            sp.wait_ge(const_in, 5 * 16)

        @block.gpsimd
        def _(pool):
            pool.wait_ge(tok_in, 16)
            for n in range(TILES):
                pool.indirect_dma_start(
                    out=low_all[:, n, :], out_offset=None, in_=a["embed"],
                    in_offset=bass.IndirectOffsetOnAxis(ap=tok[:, n:n + 1], axis=0)).then_inc(gathered, 16)
            pool.wait_ge(gathered, 16 * TILES)

        @block.scalar
        def _(act):
            for n, (src, hi) in enumerate(parts):
                act.wait_ge(loaded, 16 * (2 + 2 * KT))
                act.activation(hi, src, ACT.Copy).then_inc(split_hi, 1)

        @block.vector
        def _(dve):
            for n, (src, hi, lo) in enumerate(rests):
                dve.wait_ge(split_hi, n + 1)
                dve.tensor_tensor(lo, src, hi.bitcast(F32), ALU.subtract).then_inc(split_lo, 1)

    low2 = sb("low2", [P, BLOCK_TILES, 2, RANK])
    low_t = sb("low_t", [P, BLOCK], F32R)
    x = sb("x", [P, BLOCK_TILES, HID])
    xt_hi = sb("xt_hi", [P, KT, BLOCK], F32R)
    xt_lo = sb("xt_lo", [P, KT, BLOCK], F32R)
    qk_hi = sb("qk_hi", [P, 2 * KT, BLOCK], F32R)
    qk_lo = sb("qk_lo", [P, 2 * KT, BLOCK], F32R)
    v = sb("v", [P, BLOCK_TILES, HID])
    S_BUFS, PT_BUFS = 4, 3
    s = sb("s", [P, S_BUFS, 3 * P])
    pt = sb("pt", [P, PT_BUFS, 3 * P])
    row_max = sb("row_max", [P, S_BUFS, 2])
    neg_max = sb("neg_max", [P, S_BUFS, 2])
    sums = sb("sums", [P, BLOCK_SEQS, 2, HEADS])
    recips = sb("recips", [P, BLOCK_SEQS, 2, HEADS])
    stats = sb("stats", [P, BLOCK_TILES, 6])
    mean_var = sb("mean_var", [P, BLOCK_TILES, 2])
    var_eps = sb("var_eps", [P, BLOCK_TILES])
    minus_half = sb("minus_half", [P, BLOCK_TILES])
    rstd = sb("rstd", [P, BLOCK_TILES])

    (low2_ready, low_mm, low_hi, low_ready, h_mm, h_copied, h_kept, stat_ready, rstd_ready, x_ready, xt_mm, xt_hi_done,
     xt_done, proj_mm, proj_hi, proj_done, sc_mm, sc_read, max_ready, p_ready, pt_mm, pt_done, pv_mm, o_done, at_mm,
     at_hi, at_done, out_mm, out_done, dve_a, dve_b, pool_a, dve_tick, pool_tick) = sems(
        "low2_ready", "low_mm", "low_hi", "low_ready", "h_mm", "h_copied", "h_kept", "stat_ready", "rstd_ready",
        "x_ready", "xt_mm", "xt_hi_done", "xt_done", "proj_mm", "proj_hi", "proj_done", "sc_mm", "sc_read",
        "max_ready", "p_ready", "pt_mm", "pt_done", "pv_mm", "o_done", "at_mm", "at_hi", "at_done", "out_mm",
        "out_done", "dve_a", "dve_b", "pool_a", "dve_tick", "pool_tick")

    proj_bank = [bank[0], bank[1]]
    turn_bank = [bank[2], bank[3]]
    score_bank = [bank[4], bank[5]]
    o_bank = [bank[6], bank[7]]
    h_bank = [bank[0], bank[1], bank[6], bank[7]]
    PROJ = BLOCK_TILES + 2 * KT
    qk_tile = [m // 2 + KT * (m % 2) for m in range(2 * KT)]
    seq_tiles = SEQ // P

    def split3(pe, psum_out, hi_t, lo_t, hi, lo, first, last):
        pe.matmul(psum_out, hi_t, hi, start=first, stop=False)
        pe.matmul(psum_out, lo_t, hi, start=False, stop=False)
        return pe.matmul(psum_out, hi_t, lo, start=False, stop=last)

    block = ctx.enter_context(nc.Block())


    @block.tensor
    def _(pe):
        with pe.Fori(0, STEPS) as i:
            pe.wait_ge(low2_ready, i + 1)
            for t in range(BLOCK_TILES):
                mm = pe.transpose(turn_bank[0][:, t * P:(t + 1) * P], low2[:, t, :, :].rearrange("p a r -> p (a r)"),
                                  ident[:, :])
            mm.then_inc(low_mm, 1)
            pe.wait_ge(low_ready, i + 1)
            for t in range(BLOCK_TILES):
                tk = slice(t * P, (t + 1) * P)
                pe.matmul(h_bank[t][:, :], low_t[:, tk], up_hi[:, :], start=True, stop=False)
                pe.matmul(h_bank[t][:, :], low_t[0:RANK, tk], up_lo[:, :], start=False, stop=True).then_inc(h_mm, 1)
            pe.wait_ge(x_ready, i * BLOCK_TILES + BLOCK_TILES)
            for k in range(KT):
                if k >= 2:
                    pe.wait_ge(xt_done, i * KT + k - 1)
                for t in range(BLOCK_TILES):
                    mm = pe.transpose(turn_bank[k % 2][:, t * P:(t + 1) * P], x[:, t, k * P:(k + 1) * P], ident[:, :])
                mm.then_inc(xt_mm, 1)
            pe.wait_ge(xt_done, i * KT + KT)
            for j in range(PROJ):
                if j >= 2:
                    pe.wait_ge(proj_done, i * PROJ + j - 1)
                for k in range(KT):
                    if j < BLOCK_TILES:
                        tk = slice(j * P, (j + 1) * P)
                        cols = slice(2 * HID, 3 * HID)
                        mm = split3(pe, proj_bank[j % 2][:, :], xt_hi[:, k, tk], xt_lo[:, k, tk],
                                    win_hi[:, k, cols], win_lo[:, k, cols], k == 0, k == KT - 1)
                    else:
                        m = qk_tile[j - BLOCK_TILES]
                        cols = slice(m * P, (m + 1) * P)
                        mm = split3(pe, proj_bank[j % 2][:, :], win_hi[:, k, cols], win_lo[:, k, cols],
                                    xt_hi[:, k, :], xt_lo[:, k, :], k == 0, k == KT - 1)
                mm.then_inc(proj_mm, 1)

            def scores(n):
                sq, hd = divmod(n, HEADS)
                m, r = divmod(hd * HEAD_DIM, P)
                rows = slice(r, r + HEAD_DIM)
                if sq == 0 and r == 0:
                    pe.wait_ge(proj_done, i * PROJ + BLOCK_TILES + 2 * m + 2)
                if n >= 2:
                    pe.wait_ge(sc_read, i * PAIRS + n - 1)
                b = score_bank[n % 2]
                for q in range(seq_tiles):
                    tq = slice(sq * SEQ + q * P, sq * SEQ + (q + 1) * P)
                    tk = slice(sq * SEQ, sq * SEQ + (q + 1) * P)
                    o = b[:, q * P:q * P + (q + 1) * P]
                    mm = split3(pe, o, qk_hi[rows, m, tq], qk_lo[rows, m, tq],
                                qk_hi[rows, KT + m, tk], qk_lo[rows, KT + m, tk], True, True)
                mm.then_inc(sc_mm, 1)

            def turn(n):
                pe.wait_ge(p_ready, i * PAIRS + n + 1)
                if n >= 2:
                    pe.wait_ge(pt_done, i * PAIRS + n - 1)
                for c in range(3):
                    cols = slice(c * P, (c + 1) * P)
                    mm = pe.transpose(turn_bank[n % 2][:, cols], s[:, n % S_BUFS, cols], ident[:, :])
                mm.then_inc(pt_mm, 1)

            def values(n):
                sq, hd = divmod(n, HEADS)
                pe.wait_ge(pt_done, i * PAIRS + n + 1)
                if sq > 0 and hd == 0:
                    pe.wait_ge(o_done, i * BLOCK_SEQS + sq)
                cols = slice(hd * HEAD_DIM, (hd + 1) * HEAD_DIM)
                p = pt[:, n % PT_BUFS, :]
                pe.matmul(o_bank[0][:, cols], p[:, 0:P], v[:, sq * seq_tiles, cols], start=True, stop=True)
                pe.matmul(o_bank[1][:, cols], p[:, P:2 * P], v[:, sq * seq_tiles, cols], start=True, stop=False)
                pe.matmul(o_bank[1][:, cols], p[:, 2 * P:3 * P], v[:, sq * seq_tiles + 1, cols],
                          start=False, stop=True).then_inc(pv_mm, 1)

            for n in range(PAIRS + 3):
                if n < PAIRS:
                    scores(n)
                if 2 <= n < PAIRS + 2:
                    turn(n - 2)
                if n >= 3:
                    values(n - 3)
            pe.wait_ge(o_done, i * BLOCK_SEQS + BLOCK_SEQS)
            for k in range(KT):
                if k >= 2:
                    pe.wait_ge(at_done, i * KT + k - 1)
                for t in range(BLOCK_TILES):
                    mm = pe.transpose(turn_bank[k % 2][:, t * P:(t + 1) * P], x[:, t, k * P:(k + 1) * P], ident[:, :])
                mm.then_inc(at_mm, 1)
            pe.wait_ge(at_done, i * KT + KT)
            for t in range(BLOCK_TILES):
                if t >= 2:
                    pe.wait_ge(out_done, i * BLOCK_TILES + t - 1)
                tk = slice(t * P, (t + 1) * P)
                for k in range(KT):
                    mm = split3(pe, proj_bank[t % 2][:, :], xt_hi[:, k, tk], xt_lo[:, k, tk],
                                wout_hi[:, k, :], wout_lo[:, k, :], k == 0, k == KT - 1)
                mm.then_inc(out_mm, 1)

    @block.scalar
    def _(act):
        with act.Fori(0, STEPS) as i:
            act.wait_ge(low_mm, i + 1)
            act.activation(low_t[:, :], turn_bank[0][:, :], ACT.Copy).then_inc(low_hi, 1)
            for t in range(BLOCK_TILES):
                act.wait_ge(h_mm, i * BLOCK_TILES + t + 1)
                act.activation(x[:, t, :], h_bank[t][:, :], ACT.Copy).then_inc(h_copied, 1)
            for k in range(KT):
                act.wait_ge(xt_mm, i * KT + k + 1)
                act.activation(xt_hi[:, k, :], turn_bank[k % 2][:, :], ACT.Copy).then_inc(xt_hi_done, 1)
            for j in range(BLOCK_TILES, PROJ):
                m = qk_tile[j - BLOCK_TILES]
                act.wait_ge(proj_mm, i * PROJ + j + 1)
                act.activation(qk_hi[:, m, :], proj_bank[j % 2][:, :], ACT.Identity,
                               bias=bias_qk[:, m:m + 1]).then_inc(proj_hi, 1)
            for n in range(PAIRS):
                sq, hd = divmod(n, HEADS)
                act.wait_ge(max_ready, i * PAIRS + n + 1)
                for q in range(seq_tiles):
                    cols = s[:, n % S_BUFS, q * P:q * P + (q + 1) * P]
                    e = act.activation(cols, cols, ACT.Exp, bias=neg_max[:, n % S_BUFS, q:q + 1], scale=SCALE,
                                       accum_out=sums[:, sq, q, hd:hd + 1])
                e.then_inc(p_ready, 1)
            for k in range(KT):
                act.wait_ge(at_mm, i * KT + k + 1)
                act.activation(xt_hi[:, k, :], turn_bank[k % 2][:, :], ACT.Copy).then_inc(at_hi, 1)

    @block.gpsimd
    def _(pool):
        pool.memset(minus_half[:, :], -0.5)
        with pool.Fori(0, STEPS) as i:
            for t in range(BLOCK_TILES):
                pool.wait_ge(h_copied, i * BLOCK_TILES + t + 1)
                pool.tensor_tensor(h_all[:, bass.ds(i * BLOCK_TILES + t, 1), :].rearrange("p a n -> p (a n)"),
                                   x[:, t, :], bias_out[:, :], ALU.add).then_inc(h_kept, 1)
            pool.wait_ge(stat_ready, i + 1)
            apart(pool, pool_tick)
            pool.tensor_scalar(var_eps[:, :], mean_var[:, :, 1], EPS, None, ALU.add).then_inc(pool_a, 1)
            pool.wait_ge(pool_a, i + 1)
            pool.tensor_tensor(rstd[:, :], var_eps[:, :], minus_half[:, :], ALU.pow).then_inc(rstd_ready, 1)

    @block.vector
    def _(dve):
        with dve.Fori(0, STEPS) as i:
            dve.tensor_copy(low2[:, :, :, :], low_all[:, bass.ds(i * BLOCK_TILES, BLOCK_TILES), :].unsqueeze(2)
                            .broadcast_to([P, BLOCK_TILES, 2, RANK])).then_inc(low2_ready, 1)
            dve.wait_ge(low_hi, i + 1)
            dve.tensor_tensor(low_t[RANK:, :], turn_bank[0][RANK:, :], low_t[RANK:, :].bitcast(F32),
                              ALU.subtract).then_inc(low_ready, 1)
            for t in range(BLOCK_TILES):
                dve.wait_ge(h_copied, i * BLOCK_TILES + t + 1)
                dve.bn_stats(stats[:, t, :], x[:, t, :]).then_inc(dve_a, 1)
                dve.wait_ge(dve_a, i * BLOCK_TILES + t + 1)
                apart(dve, dve_tick)
                st = dve.bn_aggr(mean_var[:, t, :], stats[:, t, :])
            st.then_inc(stat_ready, 1)
            dve.wait_ge(rstd_ready, i + 1)
            for t in range(BLOCK_TILES):
                dve.wait_ge(h_kept, i * BLOCK_TILES + t + 1)
                dve.tensor_scalar(x[:, t, :], x[:, t, :], mean_var[:, t, 0:1], rstd[:, t:t + 1], ALU.subtract,
                                  ALU.mult).then_inc(x_ready, 1)
            for k in range(KT):
                dve.wait_ge(xt_hi_done, i * KT + k + 1)
                dve.tensor_tensor(xt_lo[:, k, :], turn_bank[k % 2][:, :], xt_hi[:, k, :].bitcast(F32),
                                  ALU.subtract).then_inc(xt_done, 1)
            for j in range(PROJ):
                if j < BLOCK_TILES:
                    dve.wait_ge(proj_mm, i * PROJ + j + 1)
                    dve.tensor_tensor(v[:, j, :], proj_bank[j % 2][:, :], bias_v[:, :], ALU.add).then_inc(proj_done, 1)
                else:
                    m = qk_tile[j - BLOCK_TILES]
                    dve.wait_ge(proj_hi, i * 2 * KT + j - BLOCK_TILES + 1)
                    dve.scalar_tensor_tensor(out=qk_lo[:, m, :], in0=proj_bank[j % 2][:, :], scalar=bias_qk[:, m:m + 1],
                                             in1=qk_hi[:, m, :].bitcast(F32), op0=ALU.add,
                                             op1=ALU.subtract).then_inc(proj_done, 1)

            def maxima(n):
                dve.wait_ge(sc_mm, i * PAIRS + n + 1)
                if n >= S_BUFS:
                    dve.wait_ge(pt_mm, i * PAIRS + n - S_BUFS + 1)
                apart(dve, dve_tick)
                for q in range(seq_tiles):
                    cols = slice(q * P, q * P + (q + 1) * P)
                    ins = dve.tensor_tensor_reduce(s[:, n % S_BUFS, cols], score_bank[n % 2][:, cols], mask[:, cols],
                                                   1.0, LOWEST, ALU.add, ALU.max, row_max[:, n % S_BUFS, q:q + 1])
                ins.then_inc(sc_read, 1)
                dve.wait_ge(sc_read, i * PAIRS + n + 1)
                dve.tensor_scalar(neg_max[:, n % S_BUFS, :], row_max[:, n % S_BUFS, :], -SCALE, None,
                                  ALU.mult).then_inc(max_ready, 1)

            def keep_turned(n):
                dve.wait_ge(pt_mm, i * PAIRS + n + 1)
                if n >= PT_BUFS:
                    dve.wait_ge(pv_mm, i * PAIRS + n - PT_BUFS + 1)
                dve.tensor_copy(pt[:, n % PT_BUFS, :], turn_bank[n % 2][:, 0:3 * P]).then_inc(pt_done, 1)

            def normalise(sq):
                dve.wait_ge(pv_mm, i * PAIRS + (sq + 1) * HEADS)
                dve.reciprocal(recips[:, sq, :, :], sums[:, sq, :, :]).then_inc(dve_b, 1)
                dve.wait_ge(dve_b, i * BLOCK_SEQS + sq + 1)
                for q in range(seq_tiles):
                    ins = dve.tensor_tensor(
                        x[:, sq * seq_tiles + q, :].rearrange("p (h d) -> p h d", d=HEAD_DIM),
                        o_bank[q][:, :].rearrange("p (h d) -> p h d", d=HEAD_DIM),
                        recips[:, sq, q, :].unsqueeze(2).broadcast_to([P, HEADS, HEAD_DIM]), ALU.mult)
                ins.then_inc(o_done, 1)

            for n in range(PAIRS + 3):
                if n < PAIRS:
                    maxima(n)
                if 2 <= n < PAIRS + 2:
                    keep_turned(n - 2)
                if n == HEADS + 2:
                    normalise(0)
            normalise(1)
            for k in range(KT):
                dve.wait_ge(at_hi, i * KT + k + 1)
                dve.tensor_tensor(xt_lo[:, k, :], turn_bank[k % 2][:, :], xt_hi[:, k, :].bitcast(F32),
                                  ALU.subtract).then_inc(at_done, 1)
            for t in range(BLOCK_TILES):
                dve.wait_ge(out_mm, i * BLOCK_TILES + t + 1)
                row = h_all[:, bass.ds(i * BLOCK_TILES + t, 1), :].rearrange("p a n -> p (a n)")
                dve.tensor_tensor(row, proj_bank[t % 2][:, :], row, ALU.add).then_inc(out_done, 1)


def evaluation(jobs, w_f, bank, sem, matrices_ready):
    evaluated, copied, picked, hi_done, lo_done = sem
    bufs = w_f.shape[1]

    def pe_part(pe):
        for j, (coefs, matrices, _, _, _) in enumerate(jobs):
            if j >= 2:
                pe.wait_ge(picked, j - 1)
            for x in range(2):
                mm = pe.matmul(bank[2 * (j % 2) + x][:, :], matrices[:, x, :], coefs, start=True, stop=True)
            mm.then_inc(evaluated, 1)

    def act_part(act):
        def copy_hi(j):
            act.wait_ge(picked, j + 1)
            act.activation(jobs[j][3], w_f[:, j % bufs, :], ACT.Copy).then_inc(hi_done, 1)

        for j in range(len(jobs)):
            act.wait_ge(evaluated, j + 1)
            if j >= bufs:
                act.wait_ge(lo_done, j - bufs + 1)
            act.activation(w_f[:, j % bufs, :], bank[2 * (j % 2)][:, :], ACT.Copy).then_inc(copied, 1)
            if j > 0:
                copy_hi(j - 1)
        copy_hi(len(jobs) - 1)

    def dve_part(dve):
        def rest(j):
            dve.wait_ge(hi_done, j + 1)
            dve.tensor_tensor(jobs[j][4], w_f[:, j % bufs, :], jobs[j][3].bitcast(F32),
                              ALU.subtract).then_inc(lo_done, 1)

        dve.wait_ge(*matrices_ready)
        for j, (_, _, mask, _, _) in enumerate(jobs):
            dve.wait_ge(copied, j + 1)
            dve.copy_predicated(w_f[:, j % bufs, :], mask, bank[2 * (j % 2) + 1][:, :]).then_inc(picked, 1)
            if j > 0:
                rest(j - 1)
        rest(len(jobs) - 1)

    return pe_part, act_part, dve_part


def weighted(dve, link, term, dst, points_of, table_of, taps, shape):
    t = term[:, 0:int(np.prod(shape))].rearrange("p (a b c) -> p a b c", a=shape[0], b=shape[1])
    link(dve.tensor_tensor(dst, points_of(0), table_of(0), ALU.mult))
    for m in range(1, taps):
        link(dve.tensor_tensor(t, points_of(m), table_of(m), ALU.mult))
        link(dve.tensor_tensor(dst, dst, t, ALU.add))


def ffn(nc, a, out, ctx, sems, bank, h_all, ident):
    def sb(name, shape, dt=F32, where=ctx):
        return where.enter_context(nc.sbuf_tensor(name, shape, dt))

    NAMES = ("gate", "up")
    near_hi = {w: sb(f"{w}_near_hi", [P, INTER], F32R) for w in NAMES}
    near_lo = {w: sb(f"{w}_near_lo", [P, INTER], F32R) for w in NAMES}
    far = {w: sb(f"{w}_far", [STACK, INTER], F32R) for w in NAMES}
    basis_hi = sb("basis_hi", [P, GROUPS, KT, STACK], F32R)
    basis_lo = sb("basis_lo", [P, GROUPS, KT, STACK], F32R)
    GM = MT // GROUPS
    W_BUFS = 3

    with ExitStack() as gen:
        psi = sb("psi", [P, 4, MT, SEGS, DEG], where=gen)
        phi = sb("phi", [P, 5, MT, WINDOWS], where=gen)
        points = {w: sb(f"{w}_points", [P, MT, G_WIN], where=gen) for w in NAMES}
        coef = {w: sb(f"{w}_coef", [P, MT, 3, FEAT], where=gen) for w in NAMES}
        term = sb("term", [P, MT * MOM], where=gen)
        coef_t = {w: sb(f"{w}_coef_t", [FEAT, INTER], where=gen) for w in NAMES}
        evaluate = sb("evaluate", [MOM, GROUPS, 2, P], where=gen)
        side = sb("side", [P, INTER // 4], U32, where=gen)
        w_f = sb("w_f", [P, W_BUFS, 512], where=gen)
        moments_f = sb("moments_f", [P, GROUPS * KT * STACK], where=gen)

        table_in, basis_in, eval_in, coef_done, turn_mm, far_hi, far_lo, turned, basis_done, gen_a, *job_sems = sems(
            "table_in", "basis_in", "eval_in", "coef_done", "turn_mm", "far_hi", "far_lo", "turned", "basis_done",
            "gen_a", "g_evaluated", "g_copied", "g_picked", "g_hi", "g_lo")

        jobs = []
        for w in NAMES:
            for g in range(GROUPS):
                n = slice(g * INTER // GROUPS, (g + 1) * INTER // GROUPS)
                jobs.append((coef_t[w][0:MOM, n], evaluate[:, g, :, :], side[:, n.start // 4:n.stop // 4].bitcast(U8), near_hi[w][:, n], near_lo[w][:, n]))
        pe_jobs, act_jobs, dve_jobs = evaluation(jobs, w_f, bank[4:8], job_sems, (eval_in, 32))

        block = gen.enter_context(nc.Block())

        @block.sync
        def _(sp):
            sp.dma_start(psi[:, :, :, :, :].rearrange("p a b c d -> p (a b c d)"), a["c_psi"]).then_inc(table_in, 16)
            sp.dma_start(phi[:, :, :, :].rearrange("p a b c -> p (a b c)"), a["c_phi"]).then_inc(table_in, 16)
            for w in NAMES:
                sp.dma_start(points[w][:, :, :].rearrange("p a b -> p (a b)"), a[f"{w}_points"]).then_inc(table_in, 16)
            sp.dma_start(evaluate[:, :, :, :].rearrange("p a b c -> p (a b c)"), a["c_evaluate"]).then_inc(eval_in, 16)
            sp.dma_start(side[:, :], a["c_side"]).then_inc(eval_in, 16)
            sp.dma_start(moments_f[:, :], a["c_moments"]).then_inc(basis_in, 16)

        @block.vector
        def _(dve):
            link = chained(dve, gen_a)
            for w in NAMES:
                link(dve.memset(coef[w][:, :, :, :], 0.0))
            dve.wait_ge(table_in, 4 * 16)
            for w in NAMES:
                weighted(dve, link, term, coef[w][:, :, 0, 0:MOM].rearrange("p m (s d) -> p m s d", d=DEG),
                         lambda m: points[w][:, :, m:m + SEGS].unsqueeze(3).broadcast_to([P, MT, SEGS, DEG]),
                         lambda m: psi[:, m, :, :, :], 4, (MT, SEGS, DEG))
                weighted(dve, link, term, coef[w][:, :, 0, MOM:MOM + WINDOWS].unsqueeze(3),
                         lambda m: points[w][:, :, m:m + WINDOWS].unsqueeze(3),
                         lambda m: phi[:, m, :, :].unsqueeze(3), 5, (MT, WINDOWS, 1))
                for c in (1, 2):
                    ins = dve.tensor_copy(coef[w][:, :, c, :], coef[w][:, :, 0, :])
                ins.then_inc(coef_done, 1)
            for t in range(2 * GROUPS):
                w, g = NAMES[t // GROUPS], t % GROUPS
                n = slice(g * INTER // GROUPS, (g + 1) * INTER // GROUPS)
                dve.wait_ge(far_hi, t + 1)
                dve.tensor_tensor(far[w][2 * FEAT:, n], bank[t % 2][2 * FEAT:STACK, :],
                                  far[w][2 * FEAT:, n].bitcast(F32), ALU.subtract).then_inc(far_lo, 1)
            dve_jobs(dve)
            dve.wait_ge(basis_done, 1)
            dve.tensor_tensor(basis_lo[:, :, :, :].rearrange("p a b c -> p (a b c)"), moments_f[:, :],
                              basis_hi[:, :, :, :].rearrange("p a b c -> p (a b c)").bitcast(F32), ALU.subtract)

        @block.scalar
        def _(act):
            act.wait_ge(basis_in, 16)
            act.activation(basis_hi[:, :, :, :].rearrange("p a b c -> p (a b c)"), moments_f[:, :],
                           ACT.Copy).then_inc(basis_done, 1)
            for t in range(2 * GROUPS):
                w, g = NAMES[t // GROUPS], t % GROUPS
                n = slice(g * INTER // GROUPS, (g + 1) * INTER // GROUPS)
                act.wait_ge(turn_mm, t + 1)
                act.activation(coef_t[w][:, n], bank[t % 2][0:FEAT, :], ACT.Copy).then_inc(turned, 1)
                act.activation(far[w][:, n], bank[t % 2][0:STACK, :], ACT.Copy).then_inc(far_hi, 1)
            act_jobs(act)

        @block.tensor
        def _(pe):
            for t in range(2 * GROUPS):
                w, g = NAMES[t // GROUPS], t % GROUPS
                pe.wait_ge(coef_done, t // GROUPS + 1)
                if t >= 2:
                    pe.wait_ge(far_lo, t - 1)
                for m in range(GM):
                    mm = pe.transpose(bank[t % 2][0:STACK, m * P:(m + 1) * P],
                                      coef[w][:, g * GM + m, :, :].rearrange("p a f -> p (a f)"), ident[:, :])
                mm.then_inc(turn_mm, 1)
            pe.wait_ge(eval_in, 32)
            pe.wait_ge(turned, 2 * GROUPS)
            pe_jobs(pe)

    down_hi = sb("down_hi", [P, MT, HID], F32R)
    down_lo = sb("down_lo", [P, MT, HID], F32R)
    with ExitStack() as gen:
        d_psi = sb("d_psi", [P, 4, KT, D_SEGS, DEG], where=gen)
        d_points = sb("d_points", [P, KT, D_WIN], where=gen)
        d_coef = sb("d_coef", [P, KT, D_SEGS, DEG], where=gen)
        d_term = sb("d_term", [P, KT * D_K], where=gen)
        d_coef_t = sb("d_coef_t", [D_K, HID], where=gen)
        d_eval = sb("d_eval", [D_K, MT, 2, P], where=gen)
        d_side = sb("d_side", [P, MT, HID // 4], U32, where=gen)
        d_f = sb("d_f", [P, W_BUFS, 512], where=gen)
        d_table_in, d_eval_in, d_coef_done, d_turn_mm, d_turned, gen_b, *job_sems = sems(
            "d_table_in", "d_eval_in", "d_coef_done", "d_turn_mm", "d_turned", "gen_b",
            "d_evaluated", "d_copied", "d_picked", "d_hi", "d_lo")
        jobs = [(d_coef_t[:, :], d_eval[:, m, :, :], d_side[:, m, :].bitcast(U8), down_hi[:, m, :], down_lo[:, m, :])
                for m in range(MT)]
        pe_jobs_d, act_jobs_d, dve_jobs_d = evaluation(jobs, d_f, bank[4:8], job_sems, (d_eval_in, 32))

        block = gen.enter_context(nc.Block())

        @block.sync
        def _(sp):
            sp.dma_start(d_psi[:, :, :, :, :].rearrange("p a b c d -> p (a b c d)"), a["c_dpsi"]).then_inc(d_table_in, 16)
            sp.dma_start(d_points[:, :, :].rearrange("p a b -> p (a b)"), a["down_points"]).then_inc(d_table_in, 16)
            sp.dma_start(d_eval[:, :, :, :].rearrange("p a b c -> p (a b c)"), a["c_deval"]).then_inc(d_eval_in, 16)
            sp.dma_start(d_side[:, :, :].rearrange("p a b -> p (a b)"), a["c_dside"]).then_inc(d_eval_in, 16)

        @block.vector
        def _(dve):
            dve.wait_ge(d_table_in, 32)
            weighted(dve, chained(dve, gen_b), d_term, d_coef[:, :, :, :],
                     lambda m: d_points[:, :, m:m + D_SEGS].unsqueeze(3).broadcast_to([P, KT, D_SEGS, DEG]),
                     lambda m: d_psi[:, m, :, :, :], 4, (KT, D_SEGS, DEG))
            dve.sem_inc(d_coef_done, 1)
            dve_jobs_d(dve)

        @block.scalar
        def _(act):
            act.wait_ge(d_turn_mm, 1)
            act.activation(d_coef_t[:, :], bank[2][0:D_K, :], ACT.Copy).then_inc(d_turned, 1)
            act_jobs_d(act)

        @block.tensor
        def _(pe):
            pe.wait_ge(d_coef_done, 1)
            for k in range(KT):
                mm = pe.transpose(bank[2][0:D_K, k * P:(k + 1) * P],
                                  d_coef[:, k, :, :].rearrange("p s d -> p (s d)"), ident[:, :])
            mm.then_inc(d_turn_mm, 1)
            pe.wait_ge(d_eval_in, 32)
            pe.wait_ge(d_turned, 1)
            pe_jobs_d(pe)

    x = sb("x2", [P, BLOCK_TILES, HID])
    xt_hi = sb("x2t_hi", [P, KT, BLOCK], F32R)
    xt_lo = sb("x2t_lo", [P, KT, BLOCK], F32R)
    feat = sb("feat", [STACK, GROUPS, BLOCK], F32R)
    act_f = sb("act_f", [P, 2, BLOCK])
    act_hi = sb("act_hi", [P, 2, BLOCK], F32R)
    act_lo = sb("act_lo", [P, 2, BLOCK], F32R)
    stats = sb("stats2", [P, BLOCK_TILES, 6])
    mean_var = sb("mean_var2", [P, BLOCK_TILES, 2])
    var_eps = sb("var_eps2", [P, BLOCK_TILES])
    minus_half = sb("minus_half2", [P, BLOCK_TILES])
    rstd = sb("rstd2", [P, BLOCK_TILES])

    (stat_ready, rstd_ready, x_ready, xt_mm, xt_hi_done, xt_done, feat_mm, feat_hi, feat_done, gu_mm, silu_done,
     prod_done, act_hi_done, act_done, down_mm, out_ready, stored, dve_a, pool_a, dve_tick, pool_tick) = sems(
        "stat_ready2", "rstd_ready2", "x_ready2", "xt_mm2", "xt_hi_done2", "xt_done2", "feat_mm", "feat_hi",
        "feat_done", "gu_mm", "silu_done", "prod_done", "act_hi_done", "act_done", "down_mm", "out_ready", "stored",
        "dve_a2", "pool_a2", "dve_tick2", "pool_tick2")
    acc = bank[0:4]
    front = bank[4:8]

    block = ctx.enter_context(nc.Block())


    @block.tensor
    def _(pe):
        with pe.Fori(0, STEPS) as i:
            pe.wait_ge(x_ready, i * BLOCK_TILES + BLOCK_TILES)
            for g in range(KT):
                for t in range(BLOCK_TILES):
                    mm = pe.transpose(front[g][:, t * P:(t + 1) * P], x[:, t, g * P:(g + 1) * P], ident[:, :])
                mm.then_inc(xt_mm, 1)
            for g in range(GROUPS):
                pe.wait_ge(xt_done, i * KT + KT)
                for k in range(KT):
                    for n, (w, y) in enumerate(((basis_hi, xt_hi), (basis_hi, xt_lo), (basis_lo, xt_hi))):
                        mm = pe.matmul(front[g][0:STACK, :], w[:, g, k, :], y[:, k, :], start=(k == 0 and n == 0),
                                       stop=(k == KT - 1 and n == 2))
                mm.then_inc(feat_mm, 1)

            def gate_up(m):
                g = m // GM
                if m < 2:
                    pe.wait_ge(feat_done, i * GROUPS + 2 * m + 2)
                elif m % GM == 0:
                    pe.wait_ge(feat_done, i * GROUPS + g + 1)
                if m >= 2:
                    pe.wait_ge(prod_done, i * MT + m - 1)
                cols = slice(m * P, (m + 1) * P)
                for n, w in enumerate(NAMES):
                    o = front[2 * (m % 2) + n][:, :]
                    pe.matmul(o, near_hi[w][:, cols], xt_hi[:, g, :], start=True, stop=False)
                    pe.matmul(o, near_lo[w][:, cols], xt_hi[:, g, :], start=False, stop=False)
                    pe.matmul(o, near_hi[w][:, cols], xt_lo[:, g, :], start=False, stop=False)
                    mm = pe.matmul(o, far[w][:, cols], feat[:, g, :], start=False, stop=True)
                mm.then_inc(gu_mm, 1)

            def down(m):
                pe.wait_ge(act_done, i * MT + m + 1)
                for t in range(BLOCK_TILES):
                    tk = slice(t * P, (t + 1) * P)
                    first, last = m == 0, m == MT - 1
                    pe.matmul(acc[t][:, :], act_hi[:, m % 2, tk], down_hi[:, m, :], start=first, stop=False)
                    pe.matmul(acc[t][:, :], act_lo[:, m % 2, tk], down_hi[:, m, :], start=False, stop=False)
                    mm = pe.matmul(acc[t][:, :], act_hi[:, m % 2, tk], down_lo[:, m, :], start=False, stop=last)
                mm.then_inc(down_mm, 1)

            for m in range(MT + 2):
                if m < MT:
                    gate_up(m)
                if m >= 2:
                    down(m - 2)

    @block.scalar
    def _(act):
        with act.Fori(0, STEPS) as i:
            for g in range(KT):
                act.wait_ge(xt_mm, i * KT + g + 1)
                act.activation(xt_hi[:, g, :], front[g][:, :], ACT.Copy).then_inc(xt_hi_done, 1)
            for g in range(GROUPS):
                act.wait_ge(feat_mm, i * GROUPS + g + 1)
                act.activation(feat[:, g, :], front[g][0:STACK, :], ACT.Copy).then_inc(feat_hi, 1)

            def copy_hi(m):
                act.wait_ge(prod_done, i * MT + m + 1)
                if m >= 2:
                    act.wait_ge(down_mm, i * MT + m - 1)
                act.activation(act_hi[:, m % 2, :], act_f[:, m % 2, :], ACT.Copy).then_inc(act_hi_done, 1)

            for m in range(MT):
                act.wait_ge(gu_mm, i * MT + m + 1)
                if m >= 2:
                    act.wait_ge(act_done, i * MT + m - 1)
                act.activation(act_f[:, m % 2, :], front[2 * (m % 2)][:, :], ACT.Silu).then_inc(silu_done, 1)
                if m > 0:
                    copy_hi(m - 1)
            copy_hi(MT - 1)

    @block.gpsimd
    def _(pool):
        pool.memset(minus_half[:, :], -0.5)
        with pool.Fori(0, STEPS) as i:
            pool.wait_ge(stat_ready, i + 1)
            apart(pool, pool_tick)
            pool.tensor_scalar(var_eps[:, :], mean_var[:, :, 1], EPS, None, ALU.add).then_inc(pool_a, 1)
            pool.wait_ge(pool_a, i + 1)
            pool.tensor_tensor(rstd[:, :], var_eps[:, :], minus_half[:, :], ALU.pow).then_inc(rstd_ready, 1)

    def h_row(i, t):
        return h_all[:, bass.ds(i * BLOCK_TILES + t, 1), :].rearrange("p a n -> p (a n)")

    @block.vector
    def _(dve):
        with dve.Fori(0, STEPS) as i:
            for t in range(BLOCK_TILES):
                dve.bn_stats(stats[:, t, :], h_row(i, t)).then_inc(dve_a, 1)
                dve.wait_ge(dve_a, i * BLOCK_TILES + t + 1)
                apart(dve, dve_tick)
                ins = dve.bn_aggr(mean_var[:, t, :], stats[:, t, :])
            ins.then_inc(stat_ready, 1)
            dve.wait_ge(rstd_ready, i + 1)
            for t in range(BLOCK_TILES):
                row = h_row(i, t)
                whole = (WINDOWS - 1) * PITCH
                late = HID - whole - (GROUPS - 1) * WIN
                by_window = x[:, t, :].rearrange("p (g c j) -> p c g j", g=GROUPS, c=WINDOWS)
                pieces = (
                    (by_window[:, 0:WINDOWS - 1, :, :],
                     row[:, 0:whole].rearrange("p (c w) -> p c w", w=PITCH)[:, :, 0:P]
                     .rearrange("p c (g j) -> p c g j", j=WIN)),
                    (by_window[:, WINDOWS - 1, 0:GROUPS - 1, :],
                     row[:, whole:whole + (GROUPS - 1) * WIN].rearrange("p (g j) -> p g j", j=WIN)),
                    (x[:, t, HID - WIN:HID - WIN + late], row[:, HID - late:HID]),
                    (x[:, t, HID - WIN + late:HID], row[:, 0:whole].rearrange("p (c w) -> p c w", w=PITCH)[:, :, PITCH - 1]),
                )
                for dst, src in pieces:
                    ins = dve.tensor_scalar(dst, src, mean_var[:, t, 0:1], rstd[:, t:t + 1], ALU.subtract, ALU.mult)
                ins.then_inc(x_ready, 1)
            for g in range(KT):
                dve.wait_ge(xt_hi_done, i * KT + g + 1)
                dve.tensor_tensor(xt_lo[:, g, :], front[g][:, :], xt_hi[:, g, :].bitcast(F32),
                                  ALU.subtract).then_inc(xt_done, 1)
            for g in range(GROUPS):
                mid = slice(FEAT, 2 * FEAT)
                dve.wait_ge(feat_hi, i * GROUPS + g + 1)
                dve.tensor_tensor(feat[mid, g, :], front[g][mid, :], feat[mid, g, :].bitcast(F32),
                                  ALU.subtract).then_inc(feat_done, 1)

            def split_lo(m):
                dve.wait_ge(act_hi_done, i * MT + m + 1)
                dve.tensor_tensor(act_lo[:, m % 2, :], act_f[:, m % 2, :], act_hi[:, m % 2, :].bitcast(F32),
                                  ALU.subtract).then_inc(act_done, 1)

            for m in range(MT):
                dve.wait_ge(silu_done, i * MT + m + 1)
                dve.tensor_tensor(act_f[:, m % 2, :], act_f[:, m % 2, :], front[2 * (m % 2) + 1][:, :],
                                  ALU.mult).then_inc(prod_done, 1)
                if m > 0:
                    split_lo(m - 1)
            split_lo(MT - 1)
            for t in range(BLOCK_TILES):
                dve.wait_ge(down_mm, i * MT + MT)
                dve.tensor_tensor(h_row(i, t), acc[t][:, :], h_row(i, t), ALU.add).then_inc(out_ready, 1)

    @block.sync
    def _(sp):
        rows = out.rearrange("b s d -> (b s) d")
        with sp.Fori(0, STEPS) as i:
            for t in range(BLOCK_TILES):
                sp.wait_ge(out_ready, i * BLOCK_TILES + t + 1)
                sp.dma_start(rows[bass.ds(i * BLOCK + t * P, P), :], h_row(i, t)).then_inc(stored, 16)
        sp.wait_ge(stored, 16 * TILES)



def kernel(x, L0_tok_embed_low, L0_tok_project_up, L0_attn_W_in, L0_attn_b_in, L0_attn_W_out, L0_attn_b_out,
           L0_ffn_gate_cp, L0_ffn_up_cp, L0_ffn_down_cp):
    import concourse.bacc as bacc
    from concourse.bass_utils import run_bass_kernel_spmd

    tables, gate_starts, down_starts = _tables()
    b_in = np.asarray(L0_attn_b_in)
    arrays = {
        "tokens": np.ascontiguousarray(np.asarray(x).reshape(TILES, P).T).view(np.uint32),
        "embed": np.asarray(L0_tok_embed_low),
        "up_t": np.ascontiguousarray(np.asarray(L0_tok_project_up).T),
        "w_in_t": np.ascontiguousarray(np.asarray(L0_attn_W_in).T),
        "w_out_t": np.ascontiguousarray(np.asarray(L0_attn_W_out).T),
        "b_qk": np.ascontiguousarray(b_in[:2 * HID].reshape(2 * KT, P).T),
        "b_v": np.ascontiguousarray(b_in[2 * HID:].reshape(1, HID)),
        "b_out": np.asarray(L0_attn_b_out).reshape(1, HID),
        "gate_points": _windows(np.asarray(L0_ffn_gate_cp), gate_starts, G_WIN, MT),
        "up_points": _windows(np.asarray(L0_ffn_up_cp), gate_starts, G_WIN, MT),
        "down_points": _windows(np.asarray(L0_ffn_down_cp), down_starts, D_WIN, KT),
        **tables,
    }
    nc = bacc.Bacc("TRN2", target_bir_lowering=False, num_devices=1)
    aps = {n: nc.dram_tensor(f"in_{n}", v.shape, mybir.dt.from_np(v.dtype), kind="ExternalInput").ap() for n, v in arrays.items()}
    out = nc.dram_tensor("out", (BATCH, SEQ, HID), F32, kind="ExternalOutput").ap()
    build(nc, aps, out)
    return run_bass_kernel_spmd(nc, [{f"in_{n}": v for n, v in arrays.items()}], core_ids=[0]).results[0]["out"]
```

```python
from contextlib import ExitStack
from math import comb

import numpy as np

import concourse.bass as bass
from concourse import mybir

F32 = mybir.dt.float32
F32R = mybir.dt.float32r
U32 = mybir.dt.uint32
U8 = mybir.dt.uint8
ALU = mybir.AluOpType
ACT = mybir.ActivationFunctionType
AX = mybir.AxisListType

P = 128
HID = 512
INTER = 2048
BATCH, SEQ = 8, 256
TOKENS = BATCH * SEQ
RANK = 64
HEADS, HEAD_DIM = 16, 32
EPS = 1e-5
SCALE = float(HEAD_DIM) ** -0.5
MASKED = -1e30

BLOCK_TILES = 4
BLOCK = BLOCK_TILES * P
STEPS = TOKENS // BLOCK
TILES = TOKENS // P
KT = HID // P
MT = INTER // P
BLOCK_SEQS = BLOCK // SEQ
SEQ_TILES = SEQ // P
QUAD = P // HEAD_DIM
GROUPS_A = KT * BLOCK_SEQS

N_WEIGHTS = HID * INTER
N_CTRL = max(16, int(N_WEIGHTS / 128.9))
DEG = 4
WINDOWS = 4
GROUPS = 4
WIN = 32
PITCH = 129
SEGS = WINDOWS + 1
MOM = SEGS * DEG
FEAT = 32
STACK = 3 * FEAT
U_SCALE = 64.0
GM = MT // GROUPS
D_SEGS = 17
D_WIDE = FEAT // DEG
D_SCALE = 128.0
G_WIN = SEGS + 3
D_WIN = D_SEGS + 3



def _grid():
    t = np.linspace(0.0, N_CTRL - 1.0, N_WEIGHTS, dtype=np.float64)
    return np.clip(np.floor(t).astype(np.int64), 0, N_CTRL - 2), (N_CTRL - 1.0) / (N_WEIGHTS - 1)


_CR = 0.5 * np.array([[0, 2, 0, 0], [-1, 0, 1, 0], [2, -5, 4, -1], [-1, 3, -3, 1]], np.float64)


def _psi(center, scale):
    out = np.zeros((4,) + center.shape + (DEG,))
    for d in range(DEG):
        for e in range(d, DEG):
            out[..., d] += np.multiply.outer(_CR[e], comb(e, d) * center ** (e - d) * scale ** d)
    return out


def _split(a):
    a = np.ascontiguousarray(a, np.float32)
    bits = a.view(np.uint32)
    hi = ((bits + 0x7FF + ((bits >> 12) & 1)) & np.uint32(0xFFFFF000)).view(np.float32)
    return hi, a - hi


def _stack(a):
    hi, lo = _split(np.concatenate([a, np.zeros((FEAT - len(a),) + a.shape[1:])]).reshape(FEAT, -1))
    return np.concatenate([hi, lo, hi])


def _tables():
    interval, step = _grid()
    rows = interval.reshape(INTER, HID)
    first = rows[:, 0]
    ends = np.array([[np.searchsorted(r, r[0] + 1 + c) for c in range(WINDOWS)] for r in rows])
    start = PITCH * np.arange(WINDOWS)[None] + WIN * np.arange(GROUPS)[:, None]
    fits = ((ends[:, None] >= start) & (ends[:, None] <= start + WIN + 1)) | (
        (ends[:, None] >= HID) & (start + WIN + 1 >= HID))
    fits = fits.all(2)
    group = [[] for _ in range(GROUPS)]
    for i in sorted(range(INTER), key=lambda i: (fits[i].sum(), int(np.argmax(fits[i])))):
        options = np.flatnonzero(fits[i])
        group[next(g for g in options if len(group[g]) < INTER // GROUPS)].append(i)
    assert all(len(g) == INTER // GROUPS for g in group)
    order = np.concatenate([np.array(sorted(g)) for g in group])
    tile = order.reshape(MT, P)

    def center(g, s):
        return PITCH * s + WIN * g - 48

    where = np.array([[PITCH * c + WIN * g + j for c in range(WINDOWS) for j in range(WIN)] for g in range(GROUPS)])
    spare = where >= HID
    where = np.where(spare, (where - HID + 1) * PITCH - 1, where)

    psi = np.zeros((4, INTER, SEGS, DEG))
    phi = np.zeros((5, INTER, WINDOWS))
    for n, i in enumerate(order):
        g = n // (INTER // GROUPS)
        s = np.arange(SEGS)
        f0 = (i * HID + center(g, s)) * step - (first[i] + s)
        psi[:, n] = _psi(f0, U_SCALE * step)
        for c in range(WINDOWS):
            h = start[g, c] + WIN
            if h < HID and rows[i, h] == first[i] + c:
                f = (i * HID + h) * step - (first[i] + c)
                phi[0:4, n, c] += _CR.T @ (f ** np.arange(4))
                phi[1:5, n, c] -= _CR.T @ ((f - 1) ** np.arange(4))

    moments = np.zeros((P, GROUPS, KT, FEAT))
    for g in range(GROUPS):
        for t in range(KT):
            for r in range(P):
                h = where[t, r]
                if t == g and not spare[t, r]:
                    continue
                s = int((h >= start[g] + WIN).sum())
                moments[r, g, t, DEG * s:DEG * s + DEG] = ((h - center(g, s)) / U_SCALE) ** np.arange(DEG)
                for c in range(WINDOWS):
                    if h == start[g, c] + WIN:
                        moments[r, g, t, MOM + c] = 1.0
    moments = np.concatenate([moments] * 3, axis=3)

    evaluate = np.zeros((MOM, GROUPS, 2, P))
    side = np.zeros((P, INTER), np.uint8)
    for g in range(GROUPS):
        for r in range(P):
            if spare[g, r]:
                continue
            c, h = r // WIN, where[g, r]
            for x in range(2):
                u = (h - center(g, c + x)) / U_SCALE
                evaluate[DEG * (c + x):DEG * (c + x + 1), g, x, r] = u ** np.arange(DEG)
            n = slice(g * INTER // GROUPS, (g + 1) * INTER // GROUPS)
            side[r, n] = rows[order[n], h] - first[order[n]] - c
    assert side.max() == 1

    d_first = interval.reshape(HID, INTER)[:, 0]
    s = np.arange(D_SEGS)
    f0 = (np.arange(HID)[:, None] * INTER + PITCH * s) * step - (d_first[:, None] + s)
    d_psi = _psi(f0, D_SCALE * step)
    d_eval = np.zeros((FEAT, MT, 2, P))
    d_side = np.zeros((P, MT, HID), np.uint8)
    low = np.floor(np.arange(INTER) * step).astype(np.int64)
    kind = low[tile].reshape(GROUPS, GM, P)
    d_starts = [min(int(kind[:, r].min()), D_SEGS - D_WIDE) for r in range(GM)]
    assert all(kind[:, r].max() + 1 < d_starts[r] + D_WIDE for r in range(GM))
    for m in range(MT):
        for r in range(P):
            i = tile[m, r]
            for x in range(2):
                k = low[i] + x
                at = DEG * (k - d_starts[m % GM])
                d_eval[at:at + DEG, m, x, r] = ((i - PITCH * k) / D_SCALE) ** np.arange(DEG)
            d_side[r, m] = interval.reshape(HID, INTER)[:, i] - d_first - low[i]
    assert d_side.max() == 1

    def by_partition(a, lead):
        a = a.reshape(a.shape[:lead] + (-1, P) + a.shape[lead + 1:])
        return np.moveaxis(a, lead + 1, 0).reshape(P, -1)

    causal = np.where(np.arange(P)[None] > np.arange(P)[:, None], MASKED, 0.0)
    f32 = {
        "c_psi": by_partition(psi, 1), "c_phi": by_partition(phi, 1), "c_dpsi": by_partition(d_psi, 1),
        "c_mask": np.tile(causal, (1, QUAD)), "c_ident": np.eye(P),
    }
    tables = {k: np.ascontiguousarray(v, np.float32) for k, v in f32.items()}
    tables["c_basis_hi"], tables["c_basis_lo"] = _split(moments.reshape(P, -1))
    tables["c_evaluate"], tables["c_deval"] = _stack(evaluate), _stack(d_eval)
    tables["c_side"] = side.view(np.uint32)
    tables["c_dside"] = d_side.reshape(P, -1).view(np.uint32)
    return tables, first[order], d_first, d_starts


def _windows(points, starts, width, tiles):
    padded = np.concatenate([points[:1], points, np.repeat(points[-1:], D_WIN)])
    rows = np.stack([padded[s:s + width] for s in starts])
    return np.ascontiguousarray(rows.reshape(tiles, P, width).transpose(1, 0, 2).reshape(P, -1))



def build(nc, a, out, d_starts):
    with ExitStack() as top:
        banks = top.enter_context(nc.psum_tensor("banks", [P, 8, 512], F32))
        bank = [banks[:, n, :] for n in range(8)]

        def sems(*names):
            return [top.enter_context(nc.semaphore(n)) for n in names]

        h_all = top.enter_context(nc.sbuf_tensor("h_all", [P, TILES, HID], F32))
        ident = top.enter_context(nc.sbuf_tensor("ident", [P, P], F32))
        norm2 = SecondNorm(nc, top, sems, h_all)
        splines = Splines(nc, a, sems, d_starts)
        with ExitStack() as ctx:
            attention(nc, a, ctx, sems, banks, bank, h_all, ident, splines, norm2)
        with ExitStack() as ctx:
            ffn(nc, a, out, ctx, sems, bank, h_all, ident, splines, norm2)


def chained(engine, sem):
    count = [0]

    def link(instruction):
        count[0] += 1
        instruction.then_inc(sem, 1)
        engine.wait_ge(sem, count[0])
    return link


def apart(engine, tick):
    engine.sem_inc(tick, 1)


def attention(nc, a, ctx, sems, banks, bank, h_all, ident, splines, norm2):
    def sb(name, shape, dt=F32, where=ctx):
        return where.enter_context(nc.sbuf_tensor(name, shape, dt))

    win_hi = sb("win_hi", [P, KT, 3 * HID], F32R)
    win_lo = sb("win_lo", [P, KT, 3 * HID], F32R)
    xt_hi = sb("xt_hi", [P, KT, BLOCK], F32R)
    xt_lo = sb("xt_lo", [P, KT, BLOCK], F32R)
    assert 4 * 2 * KT * (3 * HID + BLOCK) >= splines.size
    wout_hi = sb("wout_hi", [P, KT, HID], F32R)
    wout_lo = sb("wout_lo", [P, KT, HID], F32R)
    up_hi = sb("up_hi", [P, HID], F32R)
    up_lo = sb("up_lo", [RANK, HID], F32R)
    late = TILES * RANK // HID
    low_all = h_all[:, TILES - late:, :].rearrange("p a (b r) -> p (a b) r", r=RANK)
    tok = sb("tok", [P, TILES], U32)
    bias_qk = sb("bias_qk", [P, 2 * KT])
    bias_v = sb("bias_v", [P, KT])
    bias_out = sb("bias_out", [P, HID])
    mask = sb("mask", [P, QUAD * P], F32R)
    ident_r = sb("ident_r", [P, P], F32R)

    loaded, split_hi, split_lo, gathered, const_in, tok_in = sems(
        "loaded", "split_hi", "split_lo", "gathered", "const_in", "tok_in")

    with ExitStack() as prep:
        win_f = sb("win_f", [P, KT, 3 * HID], where=prep)
        wout_f = sb("wout_f", [P, KT, HID], where=prep)
        up_f = sb("up_f", [P, HID], where=prep)
        mask_f = sb("mask_f", [P, QUAD * P], where=prep)
        parts = [(up_f[:, :], up_hi[:, :])] + [(win_f[:, k, :], win_hi[:, k, :]) for k in range(KT)] \
            + [(wout_f[:, k, :], wout_hi[:, k, :]) for k in range(KT)]
        rests = [(up_f[0:RANK, :], up_hi[0:RANK, :], up_lo[:, :])] \
            + [(win_f[:, k, :], win_hi[:, k, :], win_lo[:, k, :]) for k in range(KT)] \
            + [(wout_f[:, k, :], wout_hi[:, k, :], wout_lo[:, k, :]) for k in range(KT)]

        block = prep.enter_context(nc.Block())

        @block.sync
        def _(sp):
            sp.dma_start(tok[:, :], a["tokens"]).then_inc(tok_in, 16)
            for half in range(2):
                sp.dma_start(up_f[half * RANK:(half + 1) * RANK, :], a["up_t"]).then_inc(loaded, 16)
            w = a["w_in_t"].rearrange("(k p) n -> p k n", p=P)
            for k in range(KT):
                sp.dma_start(win_f[:, k, :], w[:, k, :]).then_inc(loaded, 16)
            w = a["w_out_t"].rearrange("(k p) n -> p k n", p=P)
            for k in range(KT):
                sp.dma_start(wout_f[:, k, :], w[:, k, :]).then_inc(loaded, 16)
            sp.dma_start(ident[:, :], a["c_ident"]).then_inc(const_in, 16)
            sp.dma_start(bias_qk[:, :], a["b_qk"]).then_inc(const_in, 16)
            sp.dma_start(bias_v[:, :], a["b_v"]).then_inc(const_in, 16)
            sp.dma_start(bias_out[:, :], a["b_out"].broadcast_to([P, HID])).then_inc(const_in, 16)
            sp.dma_start(mask_f[:, :], a["c_mask"]).then_inc(const_in, 16)

        @block.gpsimd
        def _(pool):
            pool.wait_ge(tok_in, 16)
            for n in range(TILES):
                pool.indirect_dma_start(
                    out=low_all[:, n, :], out_offset=None, in_=a["embed"],
                    in_offset=bass.IndirectOffsetOnAxis(ap=tok[:, n:n + 1], axis=0)).then_inc(gathered, 16)
            pool.wait_ge(gathered, 16 * TILES)

        @block.scalar
        def _(act):
            for n, (src, hi) in enumerate(parts):
                act.wait_ge(loaded, 16 * (2 + 2 * KT))
                act.activation(hi, src, ACT.Copy).then_inc(split_hi, 1)
            act.wait_ge(const_in, 5 * 16)
            act.activation(mask[:, :], mask_f[:, :], ACT.Copy)
            act.activation(ident_r[:, :], ident[:, :], ACT.Copy)

        @block.vector
        def _(dve):
            for n, (src, hi, lo) in enumerate(rests):
                dve.wait_ge(split_hi, n + 1)
                dve.tensor_tensor(lo, src, hi.bitcast(F32), ALU.subtract).then_inc(split_lo, 1)

    low2 = sb("low2", [P, BLOCK_TILES, 2, RANK])
    low_t = sb("low_t", [P, BLOCK], F32R)
    x = sb("x", [P, BLOCK_TILES, HID])
    q_hi = sb("q_hi", [P, 2, BLOCK], F32R)
    q_lo = sb("q_lo", [P, 2, BLOCK], F32R)
    k_hi = sb("k_hi", [P, BLOCK_TILES, QUAD, P], F32R)
    k_lo = sb("k_lo", [P, BLOCK_TILES, QUAD, P], F32R)
    v = sb("v", [P, BLOCK_TILES, HID])
    p = sb("p", [P, 2, 3, QUAD, P])
    pt = sb("pt", [P, 2, 3, BLOCK])
    at_hi = sb("at_hi", [P, KT, BLOCK], F32R)
    at_lo = sb("at_lo", [P, KT, BLOCK], F32R)
    row_max = sb("row_max", [P, 2, 2, QUAD])
    neg_max = sb("neg_max", [P, 2, 2, QUAD])
    sums = sb("sums", [P, 2, 2, QUAD])
    recips = sb("recips", [P, 2, 2, QUAD])
    stats = sb("stats", [P, BLOCK_TILES, 6])
    mean_var = sb("mean_var", [P, BLOCK_TILES, 2])
    var_eps = sb("var_eps", [P, BLOCK_TILES])
    minus_half = sb("minus_half", [P, BLOCK_TILES])
    rstd = sb("rstd", [P, BLOCK_TILES])

    (low2_ready, low_mm, low_hi, low_ready, h_mm, h_copied, h_kept, stat_ready, rstd_ready, x_ready, xt_mm, xt_hi_done,
     xt_done, proj_mm, proj_hi, proj_done, k_ready, sc_mm, max_read, max_ready, p_ready, recip_ready, p_normal, pt_mm,
     pt_done, pv_mm, at_hi_done, at_done, out_mm, out_done, keys_clear, dve_a, pool_a, dve_tick, pool_tick) = sems(
        "low2_ready", "low_mm", "low_hi", "low_ready", "h_mm", "h_copied", "h_kept", "stat_ready", "rstd_ready",
        "x_ready", "xt_mm", "xt_hi_done", "xt_done", "proj_mm", "proj_hi", "proj_done", "k_ready", "sc_mm", "max_read",
        "max_ready", "p_ready", "recip_ready", "p_normal", "pt_mm", "pt_done", "pv_mm", "at_hi_done",
        "at_done", "out_mm", "out_done", "keys_clear", "dve_a", "pool_a", "dve_tick", "pool_tick")

    score_banks = banks[:, 0:3, :]
    turn_bank = [bank[3], bank[4]]
    o_banks = banks[:, 5:7, :]
    spare = bank[7]
    out_bank = [bank[0], bank[1], bank[3], bank[4]]
    ORDER = (("q", 0, bank[7]), ("k", 0, bank[7]), ("v", 0, bank[5]), ("v", 1, bank[6]), ("v", 2, bank[5]),
             ("q", 1, bank[7]), ("k", 1, bank[7]), ("v", 3, bank[6]), ("q", 2, bank[7]), ("k", 2, bank[7]),
             ("q", 3, bank[7]), ("k", 3, bank[7]))
    JOBS = len(ORDER)
    PLACE = {(what, n): j for j, (what, n, _) in enumerate(ORDER)}
    WITH_GROUP = [PLACE[("q", 1)], PLACE[("k", 1)], PLACE[("q", 2)], PLACE[("k", 2)], PLACE[("q", 3)], PLACE[("k", 3)]]
    BLOCKS = ((0, 0), (1, 0), (1, 1))

    def xt_bank(i, k):
        return bank[k] if first_step(i) else spare

    def split3(pe, psum_out, hi_t, lo_t, hi, lo, first, last):
        pe.matmul(psum_out, hi_t, hi, start=first, stop=False)
        pe.matmul(psum_out, lo_t, hi, start=False, stop=False)
        return pe.matmul(psum_out, hi_t, lo, start=False, stop=last)

    block = ctx.enter_context(nc.Block())

    HIS = KT * (1 + 2 * QUAD)
    LN_AT = 3
    XT_AT = 6

    @block.tensor
    def _(pe):
        def low_turn(i):
            pe.wait_ge(low2_ready, i + 1)
            for t in range(BLOCK_TILES):
                mm = pe.transpose(spare[:, t * P:(t + 1) * P], low2[:, t, :, :].rearrange("p a r -> p (a r)"),
                                  ident[:, :])
            mm.then_inc(low_mm, 1)

        def embed(i, t):
            if t == 0:
                pe.wait_ge(low_ready, i + 1)
            else:
                pe.wait_ge(h_copied, i * BLOCK_TILES + t)
            tk = slice(t * P, (t + 1) * P)
            pe.matmul(spare[:, :], low_t[:, tk], up_hi[:, :], start=True, stop=False)
            pe.matmul(spare[:, :], low_t[0:RANK, tk], up_lo[:, :], start=False, stop=True).then_inc(h_mm, 1)

        def turn_tokens(i, k):
            if k == 0:
                pe.wait_ge(x_ready, i * BLOCK_TILES + BLOCK_TILES)
            elif not first_step(i):
                pe.wait_ge(xt_done, i * KT + k)
            for t in range(BLOCK_TILES):
                mm = pe.transpose(xt_bank(i, k)[:, t * P:(t + 1) * P], x[:, t, k * P:(k + 1) * P], ident[:, :])
            mm.then_inc(xt_mm, 1)

        def project(i, j):
            what, m, o = ORDER[j]
            if j == 0:
                pe.wait_ge(xt_done, i * KT + KT)
            for k in range(KT):
                if what == "v":
                    tk, cols = slice(m * P, (m + 1) * P), slice(2 * HID, 3 * HID)
                    mm = split3(pe, o[:, :], xt_hi[:, k, tk], xt_lo[:, k, tk],
                                win_hi[:, k, cols], win_lo[:, k, cols], k == 0, k == KT - 1)
                else:
                    at = (what == "k") * HID + m * P
                    cols = slice(at, at + P)
                    mm = split3(pe, o[:, :], win_hi[:, k, cols], win_lo[:, k, cols],
                                xt_hi[:, k, :], xt_lo[:, k, :], k == 0, k == KT - 1)
            mm.then_inc(proj_mm, 1)

        def tile_read(i, what, n):
            pe.wait_ge(proj_done, i * JOBS + PLACE[(what, n)] + 1)

        def scores(i, g):
            m, sq = divmod(g, BLOCK_SEQS)
            if sq == 0:
                tile_read(i, "q", m)
                pe.wait_ge(k_ready, i * KT + m + 1)
            else:
                tile_read(i, "k", m)
            if g > 0:
                pe.wait_ge(p_ready, i * GROUPS_A + g)
            for n, (q, k) in enumerate(BLOCKS):
                o = score_banks[:, n, :]
                tq = slice(sq * SEQ + q * P, sq * SEQ + (q + 1) * P)
                if q == k:
                    pe.matmul(o, ident_r[:, :], mask[:, :], start=True, stop=False)
                tk = sq * SEQ_TILES + k
                mm = split3(pe, o, q_hi[:, m % 2, tq], q_lo[:, m % 2, tq],
                            k_hi[:, tk, :, :].rearrange("p h k -> p (h k)"),
                            k_lo[:, tk, :, :].rearrange("p h k -> p (h k)"), q != k, True)
                if n != 1:
                    mm.then_inc(sc_mm, 1)

        def turn(i, g):
            pe.wait_ge(p_normal, i * GROUPS_A + g + 1)
            for n in range(3):
                c = 3 * g + n
                if c >= 2:
                    pe.wait_ge(pt_done, i * 3 * GROUPS_A + c - 1)
                for hd in range(QUAD):
                    mm = pe.transpose(turn_bank[c % 2][:, hd * P:(hd + 1) * P], p[:, g % 2, n, hd, :], ident[:, :])
                mm.then_inc(pt_mm, 1)

        def values(i, g):
            m, sq = divmod(g, BLOCK_SEQS)
            cols = slice(m * P, (m + 1) * P)
            pe.wait_ge(pt_done, i * 3 * GROUPS_A + 3 * g + 3)
            if g > 0:
                pe.wait_ge(at_done, i * GROUPS_A + g)
            else:
                tile_read(i, "v", BLOCK_TILES - 1)
            for n, (q, k) in enumerate(BLOCKS):
                mm = pe.matmul(o_banks[:, q, :], v[:, sq * SEQ_TILES + k, cols], pt[:, g % 2, n, :],
                               start=k == 0, stop=q == k)
            mm.then_inc(pv_mm, 1)

        def project_out(i, t):
            if t == 0:
                pe.wait_ge(p_ready, i * GROUPS_A + GROUPS_A)
            if t % SEQ_TILES == 0:
                pe.wait_ge(at_done, i * GROUPS_A + GROUPS_A - BLOCK_SEQS + t // SEQ_TILES + 1)
            tk = slice(t * P, (t + 1) * P)
            for k in range(KT):
                mm = split3(pe, out_bank[t][:, :], at_hi[:, k, tk], at_lo[:, k, tk],
                            wout_hi[:, k, :], wout_lo[:, k, :], k == 0, k == KT - 1)
            mm.then_inc(out_mm, 1)

        def step(i, more):
            nxt = i + 1
            for g in range(GROUPS_A):
                if g == 0:
                    if not first_step(i):
                        project_out(i - 1, 2)
                    if more:
                        tile_read(i, "k", 0)
                        low_turn(nxt)
                    if not first_step(i):
                        project_out(i - 1, 3)
                    if more:
                        embed(nxt, 0)
                    project(i, PLACE[("v", 0)])
                    if more:
                        embed(nxt, 1)
                    project(i, PLACE[("v", 1)])
                    if more:
                        embed(nxt, 2)
                    tile_read(i, "v", 0)
                    project(i, PLACE[("v", 2)])
                    if more:
                        pe.wait_ge(h_copied, nxt * BLOCK_TILES + 3)
                    else:
                        tile_read(i, "k", 0)
                    project(i, PLACE[("q", 1)])
                else:
                    scores(i, g)
                    if g < len(WITH_GROUP):
                        before = ORDER[WITH_GROUP[g] - (2 if g == 2 else 1)]
                        tile_read(i, before[0], before[1])
                        if more and g == 3:
                            pe.wait_ge(h_copied, nxt * BLOCK_TILES + BLOCK_TILES)
                        project(i, WITH_GROUP[g])
                if g == 1 and not first_step(i):
                    pe.wait_ge(out_done, i * BLOCK_TILES)
                if g >= 1:
                    turn(i, g - 1)
                if g == 1:
                    tile_read(i, "v", 1)
                    project(i, PLACE[("v", 3)])
                if more and g >= XT_AT:
                    if g == XT_AT:
                        tile_read(i, "k", KT - 1)
                    turn_tokens(nxt, 2 * (g - XT_AT))
                if g >= 2:
                    values(i, g - 2)
                if more and g == 2:
                    tile_read(i, "q", 2)
                    embed(nxt, 3)
                if more and g >= XT_AT:
                    turn_tokens(nxt, 2 * (g - XT_AT) + 1)
            values(i, GROUPS_A - 2)
            if more:
                project(nxt, PLACE[("q", 0)])
            turn(i, GROUPS_A - 1)
            project_out(i, 0)
            if more:
                tile_read(nxt, "q", 0)
                project(nxt, PLACE[("k", 0)])
            project_out(i, 1)
            values(i, GROUPS_A - 1)
            if more:
                pe.wait_ge(out_done, i * BLOCK_TILES + 2)
                scores(nxt, 0)
            else:
                project_out(i, 2)
                project_out(i, 3)

        low_turn(0)
        for t in range(BLOCK_TILES):
            embed(0, t)
        for k in range(KT):
            turn_tokens(0, k)
        project(0, PLACE[("q", 0)])
        tile_read(0, "q", 0)
        project(0, PLACE[("k", 0)])
        scores(0, 0)
        step(0, True)
        with pe.Fori(1, STEPS - 1) as i:
            step(i, True)
        step(STEPS - 1, False)

    def head_keys(t, r, sq):
        return t[r * HEAD_DIM:(r + 1) * HEAD_DIM, sq * SEQ_TILES:(sq + 1) * SEQ_TILES, r, :]

    def copies(m, sq, r):
        return m * (1 + 2 * QUAD) + 1 + sq * QUAD + r + 1

    def by_tile(ap):
        return ap.rearrange("p (t k) -> p t k", k=P)

    @block.scalar
    def _(act):
        def low(i):
            act.wait_ge(low_mm, i + 1)
            act.activation(low_t[:, :], spare[:, :], ACT.Copy).then_inc(low_hi, 1)

        def embedded(i, t):
            act.wait_ge(h_mm, i * BLOCK_TILES + t + 1)
            act.activation(x[:, t, :], spare[:, :], ACT.Copy).then_inc(h_copied, 1)

        def tokens_hi(i, k):
            act.wait_ge(xt_mm, i * KT + k + 1)
            act.activation(xt_hi[:, k, :], xt_bank(i, k)[:, :], ACT.Copy).then_inc(xt_hi_done, 1)

        def queries(i, m):
            j = PLACE[("q", m)]
            act.wait_ge(proj_mm, i * JOBS + j + 1)
            act.activation(q_hi[:, m % 2, :], ORDER[j][2][:, :], ACT.Identity,
                           bias=bias_qk[:, m:m + 1]).then_inc(proj_hi, 1)

        def keys(i, m, sq):
            j = PLACE[("k", m)]
            act.wait_ge(proj_mm, i * JOBS + j + 1)
            if sq > 0:
                act.wait_ge(k_ready, i * KT + m + 1)
            for r in range(QUAD):
                rows = slice(r * HEAD_DIM, (r + 1) * HEAD_DIM)
                act.activation(head_keys(k_hi, r, sq), by_tile(ORDER[j][2][rows, sq * SEQ:(sq + 1) * SEQ]),
                               ACT.Identity, bias=bias_qk[rows, KT + m:KT + m + 1]).then_inc(proj_hi, 1)

        def exponentials(i, g):
            act.wait_ge(max_ready, i * GROUPS_A + g + 1)
            for hd in range(QUAD):
                for q in range(SEQ_TILES):
                    blocks = slice(q, 2 * q + 1)
                    e = act.activation(p[:, g % 2, blocks, hd, :], score_banks[:, blocks, hd * P:(hd + 1) * P],
                                       ACT.Exp, bias=neg_max[:, g % 2, q, hd:hd + 1], scale=SCALE,
                                       accum_out=sums[:, g % 2, q, hd:hd + 1])
            e.then_inc(p_ready, 1)

        def attended(i, g):
            m, sq = divmod(g, BLOCK_SEQS)
            act.wait_ge(pv_mm, i * GROUPS_A + g + 1)
            for r in range(QUAD):
                rows = slice(r * HEAD_DIM, (r + 1) * HEAD_DIM)
                act.activation(by_tile(at_hi[rows, m, sq * SEQ:(sq + 1) * SEQ]), o_banks[rows, :, r * P:(r + 1) * P],
                               ACT.Identity, bias=bias_v[rows, m:m + 1]).then_inc(at_hi_done, 1)

        def step(i, more):
            nxt = i + 1
            for g in range(GROUPS_A):
                exponentials(i, g)
                if more and g == 0:
                    low(nxt)
                    for t in range(BLOCK_TILES - 1):
                        embedded(nxt, t)
                if g < len(WITH_GROUP):
                    if g % 2 == 0:
                        queries(i, 1 + g // 2)
                    else:
                        keys(i, 1 + g // 2, 0)
                if more and g >= XT_AT:
                    tokens_hi(nxt, 2 * (g - XT_AT))
                if g >= 2:
                    attended(i, g - 2)
                if g < len(WITH_GROUP) and g % 2 == 1:
                    keys(i, 1 + g // 2, 1)
                if more and g == 2:
                    embedded(nxt, 3)
                if more and g >= XT_AT:
                    tokens_hi(nxt, 2 * (g - XT_AT) + 1)
            attended(i, GROUPS_A - 2)
            if more:
                queries(nxt, 0)
                keys(nxt, 0, 0)
                keys(nxt, 0, 1)
            attended(i, GROUPS_A - 1)

        act.wait_ge(keys_clear, 2)
        low(0)
        for t in range(BLOCK_TILES):
            embedded(0, t)
        for k in range(KT):
            tokens_hi(0, k)
        queries(0, 0)
        keys(0, 0, 0)
        keys(0, 0, 1)
        step(0, True)
        with act.Fori(1, STEPS - 1) as i:
            step(i, True)
        step(STEPS - 1, False)
        splines.as_parts(act)

    @block.gpsimd
    def _(pool):
        def keep(i, tiles):
            for t in tiles:
                pool.wait_ge(h_copied, i * BLOCK_TILES + t + 1)
                pool.tensor_tensor(h_all[:, bass.ds(i * BLOCK_TILES + t, 1), :].rearrange("p a n -> p (a n)"),
                                   x[:, t, :], bias_out[:, :], ALU.add).then_inc(h_kept, 1)

        def inverse_deviation(i):
            pool.wait_ge(stat_ready, i + 1)
            apart(pool, pool_tick)
            pool.tensor_scalar(var_eps[:, :], mean_var[:, :, 1], EPS, None, ALU.add).then_inc(pool_a, 1)
            pool.wait_ge(pool_a, i + 1)
            pool.tensor_tensor(rstd[:, :], var_eps[:, :], minus_half[:, :], ALU.pow).then_inc(rstd_ready, 1)

        def step(i, more):
            for g in range(GROUPS_A):
                pool.wait_ge(recip_ready, i * GROUPS_A + g + 1)
                for n in range(3):
                    part = p[:, g % 2, n, :, :]
                    ins = pool.tensor_tensor(part, part, recips[:, g % 2, min(n, 1), :].unsqueeze(2)
                                             .broadcast_to([P, QUAD, P]), ALU.mult)
                ins.then_inc(p_normal, 1)
                if more and g == LN_AT - 1:
                    keep(i + 1, range(BLOCK_TILES - 1))
                if more and g == LN_AT:
                    inverse_deviation(i + 1)
                    keep(i + 1, range(BLOCK_TILES - 1, BLOCK_TILES))

        pool.memset(minus_half[:, :], -0.5)
        pool.memset(k_hi[:, :, :, :].rearrange("p a b c -> p (a b c)").bitcast(F32), 0.0).then_inc(keys_clear, 1)
        pool.memset(k_lo[:, :, :, :].rearrange("p a b c -> p (a b c)").bitcast(F32), 0.0).then_inc(keys_clear, 1)
        keep(0, range(BLOCK_TILES))
        inverse_deviation(0)
        step(0, True)
        with pool.Fori(1, STEPS - 1) as i:
            step(i, True)
        step(STEPS - 1, False)
        splines.coefficients(pool)
        norm2.rstd_of(pool, 0)

    @block.vector
    def _(dve):
        def look_up(i):
            dve.tensor_copy(low2[:, :, :, :], low_all[:, bass.ds(i * BLOCK_TILES, BLOCK_TILES), :].unsqueeze(2)
                            .broadcast_to([P, BLOCK_TILES, 2, RANK])).then_inc(low2_ready, 1)

        def low(i):
            dve.wait_ge(low_hi, i + 1)
            dve.tensor_tensor(low_t[RANK:, :], spare[RANK:, :], low_t[RANK:, :].bitcast(F32),
                              ALU.subtract).then_inc(low_ready, 1)

        def moment_of(i, t):
            dve.wait_ge(h_copied, i * BLOCK_TILES + t + 1)
            dve.bn_stats(stats[:, t, :], x[:, t, :]).then_inc(dve_a, 1)

        def moments_of(i):
            for t in range(BLOCK_TILES):
                dve.wait_ge(dve_a, i * BLOCK_TILES + t + 1)
                apart(dve, dve_tick)
                st = dve.bn_aggr(mean_var[:, t, :], stats[:, t, :])
            st.then_inc(stat_ready, 1)

        def normalise(i):
            dve.wait_ge(rstd_ready, i + 1)
            for t in range(BLOCK_TILES):
                dve.wait_ge(h_kept, i * BLOCK_TILES + t + 1)
                dve.tensor_scalar(x[:, t, :], x[:, t, :], mean_var[:, t, 0:1], rstd[:, t:t + 1], ALU.subtract,
                                  ALU.mult).then_inc(x_ready, 1)

        def tokens_lo(i, k):
            dve.wait_ge(xt_hi_done, i * KT + k + 1)
            dve.tensor_tensor(xt_lo[:, k, :], xt_bank(i, k)[:, :], xt_hi[:, k, :].bitcast(F32),
                              ALU.subtract).then_inc(xt_done, 1)

        def v_tile(i, t):
            j = PLACE[("v", t)]
            dve.wait_ge(proj_mm, i * JOBS + j + 1)
            dve.tensor_copy(v[:, t, :], ORDER[j][2][:, :]).then_inc(proj_done, 1)

        def queries(i, m):
            dve.wait_ge(proj_hi, i * HIS + m * (1 + 2 * QUAD) + 1)
            dve.scalar_tensor_tensor(out=q_lo[:, m % 2, :], in0=ORDER[PLACE[("q", m)]][2][:, :],
                                     scalar=bias_qk[:, m:m + 1], in1=q_hi[:, m % 2, :].bitcast(F32), op0=ALU.add,
                                     op1=ALU.subtract).then_inc(proj_done, 1)

        def keys(i, m, sq):
            for r in range(QUAD):
                rows = slice(r * HEAD_DIM, (r + 1) * HEAD_DIM)
                dve.wait_ge(proj_hi, i * HIS + copies(m, sq, r))
                ins = dve.scalar_tensor_tensor(
                    out=head_keys(k_lo, r, sq), in0=by_tile(ORDER[PLACE[("k", m)]][2][rows, sq * SEQ:(sq + 1) * SEQ]),
                    scalar=bias_qk[rows, KT + m:KT + m + 1], in1=head_keys(k_hi, r, sq).bitcast(F32), op0=ALU.add,
                    op1=ALU.subtract)
            ins.then_inc(k_ready if sq == 0 else proj_done, 1)

        def maxima(i, g):
            for q in range(SEQ_TILES):
                dve.wait_ge(sc_mm, i * 2 * GROUPS_A + 2 * g + q + 1)
                src = score_banks[:, q:2 * q + 1, :].rearrange("p b (h k) -> p h b k", h=QUAD)
                dve.tensor_reduce(row_max[:, g % 2, q, :], src, AX.XY, ALU.max).then_inc(max_read, 1)
            dve.wait_ge(max_read, i * 2 * GROUPS_A + 2 * g + 2)
            dve.tensor_scalar(neg_max[:, g % 2, :, :], row_max[:, g % 2, :, :], -SCALE, None,
                              ALU.mult).then_inc(max_ready, 1)

        def over_sums(i, g):
            dve.wait_ge(p_ready, i * GROUPS_A + g + 1)
            dve.reciprocal(recips[:, g % 2, :, :], sums[:, g % 2, :, :]).then_inc(recip_ready, 1)

        def turned(i, g):
            for n in range(3):
                c = 3 * g + n
                dve.wait_ge(pt_mm, i * 3 * GROUPS_A + c + 1)
                dve.tensor_copy(pt[:, g % 2, n, :], turn_bank[c % 2][:, :]).then_inc(pt_done, 1)

        def attended(i, g):
            m, sq = divmod(g, BLOCK_SEQS)
            for r in range(QUAD):
                rows = slice(r * HEAD_DIM, (r + 1) * HEAD_DIM)
                own = slice(sq * SEQ, (sq + 1) * SEQ)
                dve.wait_ge(at_hi_done, (i * GROUPS_A + g) * QUAD + r + 1)
                ins = dve.scalar_tensor_tensor(
                    out=by_tile(at_lo[rows, m, own]), in0=o_banks[rows, :, r * P:(r + 1) * P],
                    scalar=bias_v[rows, m:m + 1], in1=by_tile(at_hi[rows, m, own]).bitcast(F32),
                    op0=ALU.add, op1=ALU.subtract)
            ins.then_inc(at_done, 1)

        def add_out(i, t):
            dve.wait_ge(out_mm, i * BLOCK_TILES + t + 1)
            row = h_all[:, bass.ds(i * BLOCK_TILES + t, 1), :].rearrange("p a n -> p (a n)")
            dve.tensor_tensor(row, out_bank[t][:, :], row, ALU.add).then_inc(out_done, 1)

        def step(i, more):
            nxt = i + 1
            if more:
                look_up(nxt)
            if not first_step(i):
                add_out(i - 1, 2)
            over_sums(i, 0)
            if more:
                low(nxt)
            if not first_step(i):
                add_out(i - 1, 3)
            for t in range(BLOCK_TILES - 1):
                v_tile(i, t)
                if more:
                    moment_of(nxt, t)
            for g in range(GROUPS_A):
                if g > 0:
                    maxima(i, g)
                    if more and g == LN_AT + 1:
                        normalise(nxt)
                    turned(i, g - 1)
                if g < len(WITH_GROUP):
                    if g % 2 == 0:
                        queries(i, 1 + g // 2)
                    else:
                        keys(i, 1 + g // 2, 0)
                if more and g >= XT_AT:
                    tokens_lo(nxt, 2 * (g - XT_AT))
                if g > 0:
                    over_sums(i, g)
                if g >= 2:
                    attended(i, g - 2)
                if g < len(WITH_GROUP) and g % 2 == 1:
                    keys(i, 1 + g // 2, 1)
                if g == 1:
                    v_tile(i, 3)
                if more and g == LN_AT:
                    moment_of(nxt, BLOCK_TILES - 1)
                    moments_of(nxt)
                if more and g >= XT_AT:
                    tokens_lo(nxt, 2 * (g - XT_AT) + 1)
            attended(i, GROUPS_A - 2)
            if more:
                queries(nxt, 0)
            turned(i, GROUPS_A - 1)
            if not more:
                norm2.moments_of(dve, 0)
            add_out(i, 0)
            if more:
                keys(nxt, 0, 0)
                keys(nxt, 0, 1)
            add_out(i, 1)
            attended(i, GROUPS_A - 1)
            if more:
                maxima(nxt, 0)
            else:
                add_out(i, 2)
                add_out(i, 3)

        dve.wait_ge(keys_clear, 2)
        look_up(0)
        low(0)
        for t in range(BLOCK_TILES):
            moment_of(0, t)
        moments_of(0)
        normalise(0)
        for k in range(KT):
            tokens_lo(0, k)
        queries(0, 0)
        keys(0, 0, 0)
        keys(0, 0, 1)
        maxima(0, 0)
        step(0, True)
        with dve.Fori(1, STEPS - 1) as i:
            step(i, True)
        step(STEPS - 1, False)

    @block.sync
    def _(sp):
        sp.wait_ge(proj_done, STEPS * JOBS)
        splines.load(sp)


def first_step(i):
    return isinstance(i, int) and i == 0


def raw(nc, name, shape):
    with nc.sbuf_tensor(name, shape, F32) as t:
        return t


def flat(t):
    names = " ".join("abcd"[:len(t.shape) - 1])
    return t[(slice(None),) * len(t.shape)].rearrange(f"p {names} -> p ({names})")


def weighted(engine, link, term, dst, points_of, table_of, taps, shape):
    t = term[:, 0:int(np.prod(shape))].rearrange("p (a b c) -> p a b c", a=shape[0], b=shape[1])
    link(engine.tensor_tensor(dst, points_of(0), table_of(0), ALU.mult))
    for m in range(1, taps):
        link(engine.tensor_tensor(t, points_of(m), table_of(m), ALU.mult))
        link(engine.tensor_tensor(dst, dst, t, ALU.add))


class SecondNorm:

    def __init__(self, nc, ctx, sems, h_all):
        def sb(name, shape):
            return ctx.enter_context(nc.sbuf_tensor(name, shape, F32))

        self.h_all = h_all
        self.stats = sb("stats2", [P, BLOCK_TILES, 6])
        self.mean_var = sb("mean_var2", [P, BLOCK_TILES, 2])
        self.var_eps = sb("var_eps2", [P, BLOCK_TILES])
        self.minus_half = sb("minus_half2", [P, BLOCK_TILES])
        self.rstd = sb("rstd2", [P, BLOCK_TILES])
        self.stat_ready, self.rstd_ready, self.x_ready, self.dve_a, self.pool_a, self.dve_tick, self.pool_tick = sems(
            "stat_ready2", "rstd_ready2", "x_ready2", "dve_a2", "pool_a2", "dve_tick2", "pool_tick2")

    def h_row(self, i, t):
        return self.h_all[:, bass.ds(i * BLOCK_TILES + t, 1), :].rearrange("p a n -> p (a n)")

    def moments_of(self, dve, i):
        for t in range(BLOCK_TILES):
            dve.bn_stats(self.stats[:, t, :], self.h_row(i, t)).then_inc(self.dve_a, 1)
        for t in range(BLOCK_TILES):
            dve.wait_ge(self.dve_a, i * BLOCK_TILES + t + 1)
            apart(dve, self.dve_tick)
            ins = dve.bn_aggr(self.mean_var[:, t, :], self.stats[:, t, :])
        ins.then_inc(self.stat_ready, 1)

    def rstd_of(self, pool, i):
        if first_step(i):
            pool.memset(self.minus_half[:, :], -0.5)
        pool.wait_ge(self.stat_ready, i + 1)
        apart(pool, self.pool_tick)
        pool.tensor_scalar(self.var_eps[:, :], self.mean_var[:, :, 1], EPS, None, ALU.add).then_inc(self.pool_a, 1)
        pool.wait_ge(self.pool_a, i + 1)
        pool.tensor_tensor(self.rstd[:, :], self.var_eps[:, :], self.minus_half[:, :],
                           ALU.pow).then_inc(self.rstd_ready, 1)

    def normalise(self, dve, i, x):
        dve.wait_ge(self.rstd_ready, i + 1)
        whole = (WINDOWS - 1) * PITCH
        late = HID - whole - (GROUPS - 1) * WIN
        for t in range(BLOCK_TILES):
            row = self.h_row(i, t)
            by_window = x[:, t, :].rearrange("p (g c j) -> p c g j", g=GROUPS, c=WINDOWS)
            pieces = (
                (by_window[:, 0:WINDOWS - 1, :, :],
                 row[:, 0:whole].rearrange("p (c w) -> p c w", w=PITCH)[:, :, 0:P]
                 .rearrange("p c (g j) -> p c g j", j=WIN)),
                (by_window[:, WINDOWS - 1, 0:GROUPS - 1, :],
                 row[:, whole:whole + (GROUPS - 1) * WIN].rearrange("p (g j) -> p g j", j=WIN)),
                (x[:, t, HID - WIN:HID - WIN + late], row[:, HID - late:HID]),
                (x[:, t, HID - WIN + late:HID], row[:, 0:whole].rearrange("p (c w) -> p c w", w=PITCH)[:, :, PITCH - 1]),
            )
            for dst, src in pieces:
                ins = dve.tensor_scalar(dst, src, self.mean_var[:, t, 0:1], self.rstd[:, t:t + 1], ALU.subtract,
                                        ALU.mult)
            ins.then_inc(self.x_ready, 1)


NAMES = ("gate", "up")


class Splines:

    def __init__(self, nc, a, sems, d_starts):
        self.size = 0
        with ExitStack() as ctx:
            def sb(name, shape, dt=F32):
                self.size += 4 * int(np.prod(shape[1:]))
                return ctx.enter_context(nc.sbuf_tensor(name, shape, dt))

            def twice(name, shape):
                loaded = raw(nc, name + "_in", shape)
                return loaded, sb(name, shape, F32R)

            self.d_side = sb("d_side", [P, MT, HID // 4], U32)
            self.psi = sb("psi", [P, 4, MT, SEGS, DEG])
            self.phi = sb("phi", [P, 5, MT, WINDOWS])
            self.points = {w: sb(f"{w}_points", [P, MT, G_WIN]) for w in NAMES}
            self.d_eval_in, self.d_eval = twice("d_eval", [STACK, MT, 2, P])
            self.d_psi = sb("d_psi", [P, 4, KT, D_SEGS, DEG])
            assert 4 * 4 * INTER <= self.size
            self.d_points = sb("d_points", [P, KT, D_WIN])
            self.d_coef = sb("d_coef", [P, KT, D_SEGS * DEG])
            self.term = sb("term", [P, MT * MOM])
            self.coef = {w: sb(f"{w}_coef", [P, MT, FEAT]) for w in NAMES}
            assert 4 * (4 * INTER + BLOCK_TILES * HID) <= self.size
            self.evaluate_in, self.evaluate = twice("evaluate", [STACK, GROUPS, 2, P])
            self.side = sb("side", [P, INTER // 4], U32)
            self.d_thrice = sb("d_thrice", [P, GM, KT, 3, FEAT])
            self.d_stack = sb("d_stack", [STACK, GM, HID], F32R)
        self.a, self.d_starts = a, d_starts
        self.table_in, self.eval_in, self.matrices_ready, self.d_coef_done, self.d_laid_out, self.coef_done, self.link = sems(
            "table_in", "eval_in", "matrices_ready", "d_coef_done", "d_laid_out", "coef_done", "gen_a")

    def load(self, sp):
        a = self.a
        tables = ((self.d_psi, "c_dpsi"), (self.d_points, "down_points"), (self.psi, "c_psi"), (self.phi, "c_phi"),
                  (self.points["gate"], "gate_points"), (self.points["up"], "up_points"))
        for dst, name in tables:
            sp.dma_start(flat(dst), a[name]).then_inc(self.table_in, 16)
        matrices = ((flat(self.evaluate_in), "c_evaluate"), (self.side[:, :], "c_side"),
                    (flat(self.d_eval_in), "c_deval"), (flat(self.d_side), "c_dside"))
        for dst, name in matrices:
            sp.dma_start(dst, a[name]).then_inc(self.eval_in, 16)

    def as_parts(self, act):
        act.wait_ge(self.eval_in, 16 * 4)
        for src, dst in ((self.evaluate_in, self.evaluate), (self.d_eval_in, self.d_eval)):
            act.activation(flat(dst), flat(src), ACT.Copy).then_inc(self.matrices_ready, 1)
        act.wait_ge(self.d_coef_done, 1)
        for r, first in enumerate(self.d_starts):
            act.activation(self.d_thrice[:, r, :, :, :], self.d_coef[:, :, DEG * first:DEG * first + FEAT]
                           .unsqueeze(2).broadcast_to([P, KT, 3, FEAT]), ACT.Copy).then_inc(self.d_laid_out, 1)

    def coefficients(self, pool):
        link = chained(pool, self.link)
        pool.wait_ge(self.table_in, 16 * 6)
        weighted(pool, link, self.term, self.d_coef[:, :, :].rearrange("p k (s d) -> p k s d", d=DEG),
                 lambda m: self.d_points[:, :, m:m + D_SEGS].unsqueeze(3).broadcast_to([P, KT, D_SEGS, DEG]),
                 lambda m: self.d_psi[:, m, :, :, :], 4, (KT, D_SEGS, DEG))
        pool.sem_inc(self.d_coef_done, 1)
        for w in NAMES:
            link(pool.memset(self.coef[w][:, :, MOM + WINDOWS:], 0.0))
            weighted(pool, link, self.term, self.coef[w][:, :, 0:MOM].rearrange("p m (s d) -> p m s d", d=DEG),
                     lambda m: self.points[w][:, :, m:m + SEGS].unsqueeze(3).broadcast_to([P, MT, SEGS, DEG]),
                     lambda m: self.psi[:, m, :, :, :], 4, (MT, SEGS, DEG))
            weighted(pool, link, self.term, self.coef[w][:, :, MOM:MOM + WINDOWS].unsqueeze(3),
                     lambda m: self.points[w][:, :, m:m + WINDOWS].unsqueeze(3),
                     lambda m: self.phi[:, m, :, :].unsqueeze(3), 5, (MT, WINDOWS, 1))
        pool.sem_inc(self.coef_done, 1)


def ffn(nc, a, out, ctx, sems, bank, h_all, ident, splines, norm2):
    def sb(name, shape, dt=F32, where=ctx):
        return where.enter_context(nc.sbuf_tensor(name, shape, dt))

    near_hi, near_lo = {}, {}
    for w in NAMES:
        near_hi[w], near_lo[w] = (sb(f"{w}_near_{part}", [P, INTER], F32R) for part in ("hi", "lo"))
    x = sb("x2", [P, BLOCK_TILES, HID])
    xt_hi = sb("x2t_hi", [P, KT, BLOCK], F32R)
    xt_lo = sb("x2t_lo", [P, KT, BLOCK], F32R)
    feat = sb("feat", [STACK, GROUPS, BLOCK], F32R)
    far = {w: sb(f"{w}_far", [STACK, INTER], F32R) for w in NAMES}
    basis_hi_in = raw(nc, "basis_hi_in", [P, GROUPS, KT, STACK])
    basis_hi = sb("basis_hi", [P, GROUPS, KT, STACK], F32R)
    basis_lo_in = raw(nc, "basis_lo_in", [P, GROUPS, KT, STACK])
    basis_lo = sb("basis_lo", [P, GROUPS, KT, STACK], F32R)
    down_hi = sb("down_hi", [P, MT, HID], F32R)
    down_lo = sb("down_lo", [P, MT, HID], F32R)
    W_BUFS = 6
    (xt_mm, xt_hi_done, xt_done, feat_mm, feat_hi, feat_done, gu_mm, silu_done, prod_done, act_hi_done, act_done,
     down_mm, out_ready, stored) = sems(
        "xt_mm2", "xt_hi_done2", "xt_done2", "feat_mm", "feat_hi", "feat_done", "gu_mm", "silu_done", "prod_done",
        "act_hi_done", "act_done", "down_mm", "out_ready", "stored")
    h_row, x_ready = norm2.h_row, norm2.x_ready
    LN_AT, BASIS_AT = 9, 14

    with ExitStack() as gen:
        w_f = sb("w_f", [P, W_BUFS, 512], where=gen)
        thrice = sb("thrice", [P, MT, 3, FEAT], where=gen)
        basis_in, laid_out, turn_mm, far_hi, far_lo, evaluated, copied, picked, hi_done, lo_vector, lo_pool = sems(
            "basis_in", "laid_out", "turn_mm", "far_hi", "far_lo", "evaluated", "copied", "picked", "w_hi", "lo_vector", "lo_pool")

        turns = [([splines.d_thrice[:, r, k, :, :] for k in range(KT)], splines.d_stack[:, r, :]) for r in range(GM)]
        jobs = [(m % GM, splines.d_stack[:, m % GM, :], splines.d_eval[:, m, :, :],
                 splines.d_side[:, m, :].bitcast(U8), down_hi[:, m, :], down_lo[:, m, :]) for m in range(MT)]
        for w in NAMES:
            for g in range(GROUPS):
                n = slice(g * INTER // GROUPS, (g + 1) * INTER // GROUPS)
                jobs.append((len(turns), far[w][:, n], splines.evaluate[:, g, :, :],
                             splines.side[:, n.start // 4:n.stop // 4].bitcast(U8), near_hi[w][:, n], near_lo[w][:, n]))
                turns.append(([thrice[:, g * GM + m, :, :] for m in range(GM)], far[w][:, n]))

        def schedule(turn, job):
            for t in range(GM):
                turn(t)
            for j in range(len(jobs)):
                if j % 2 == 0 and GM + j // 2 < len(turns):
                    turn(GM + j // 2)
                job(j)

        def rest_done(j):
            return (lo_vector, j // 3 + 1) if j % 3 == 2 else (lo_pool, j + 1 - (j + 1) // 3)

        def rest(engine, j):
            engine.wait_ge(hi_done, j + 1)
            engine.tensor_tensor(jobs[j][5], w_f[:, j % W_BUFS, :], jobs[j][4].bitcast(F32),
                                 ALU.subtract).then_inc(rest_done(j)[0], 1)

        block = gen.enter_context(nc.Block())

        @block.sync
        def _(sp):
            for dst, name in ((basis_hi_in, "c_basis_hi"), (basis_lo_in, "c_basis_lo")):
                sp.dma_start(flat(dst), a[name]).then_inc(basis_in, 16)

        @block.tensor
        def _(pe):
            def turn(t):
                if t < GM:
                    pe.wait_ge(splines.d_laid_out, t + 1)
                if t >= 2:
                    pe.wait_ge(far_lo, t - 1)
                if t >= GM:
                    pe.wait_ge(laid_out, (t - GM) // GROUPS + 1)
                for n, rows in enumerate(turns[t][0]):
                    mm = pe.transpose(bank[t % 2][0:STACK, n * P:(n + 1) * P],
                                      rows.rearrange("p c f -> p (c f)"), ident[:, :])
                mm.then_inc(turn_mm, 1)

            def job(j):
                t, coefs, matrices = jobs[j][0:3]
                pe.wait_ge(far_lo, t + 1)
                if j >= 3:
                    pe.wait_ge(picked, j - 2)
                for x in range(2):
                    mm = pe.matmul(bank[2 + 2 * (j % 3) + x][:, :], matrices[:, x, :], coefs, start=True, stop=True)
                mm.then_inc(evaluated, 1)

            pe.wait_ge(splines.matrices_ready, 2)
            schedule(turn, job)

        @block.scalar
        def _(act):
            def turn(t):
                act.wait_ge(turn_mm, t + 1)
                act.activation(turns[t][1], bank[t % 2][0:STACK, :], ACT.Copy).then_inc(far_hi, 1)
                if t == GM - 1:
                    lay_out("gate")

            def copy_hi(j):
                act.wait_ge(picked, j + 1)
                act.activation(jobs[j][4], w_f[:, j % W_BUFS, :], ACT.Copy).then_inc(hi_done, 1)

            def job(j):
                act.wait_ge(evaluated, j + 1)
                if j >= W_BUFS:
                    act.wait_ge(*rest_done(j - W_BUFS))
                act.activation(w_f[:, j % W_BUFS, :], bank[2 + 2 * (j % 3)][:, :], ACT.Copy).then_inc(copied, 1)
                if j > 0:
                    copy_hi(j - 1)
                if j == LN_AT - 2:
                    act.wait_ge(turn_mm, GM + GROUPS)
                    lay_out("up")

            def lay_out(w):
                act.activation(thrice[:, :, :, :], splines.coef[w][:, :, :].unsqueeze(2)
                               .broadcast_to([P, MT, 3, FEAT]), ACT.Copy).then_inc(laid_out, 1)

            act.wait_ge(splines.coef_done, 1)
            schedule(turn, job)
            copy_hi(len(jobs) - 1)

        @block.vector
        def _(dve):
            def turn(t):
                low = slice(2 * FEAT, STACK)
                dve.wait_ge(far_hi, t + 1)
                dve.tensor_tensor(turns[t][1][low, :], bank[t % 2][low, :], turns[t][1][low, :].bitcast(F32),
                                  ALU.subtract).then_inc(far_lo, 1)

            def job(j):
                dve.wait_ge(copied, j + 1)
                dve.copy_predicated(w_f[:, j % W_BUFS, :], jobs[j][3],
                                    bank[3 + 2 * (j % 3)][:, :]).then_inc(picked, 1)
                if j > 0 and (j - 1) % 3 == 2:
                    rest(dve, j - 1)
                if j == LN_AT:
                    dve.wait_ge(laid_out, len(NAMES))
                    norm2.normalise(dve, 0, x)
                if j == BASIS_AT:
                    dve.wait_ge(basis_in, 32)
                    for src, dst in ((basis_hi_in, basis_hi), (basis_lo_in, basis_lo)):
                        dve.tensor_copy(flat(dst), flat(src))

            dve.wait_ge(splines.eval_in, 16 * 4)
            schedule(turn, job)
            rest(dve, len(jobs) - 1)

        @block.gpsimd
        def _(pool):
            for j in range(len(jobs)):
                if j % 3 != 2:
                    rest(pool, j)

    act_f = sb("act_f", [P, 2, BLOCK])
    act_hi = sb("act_hi", [P, 2, BLOCK], F32R)
    act_lo = sb("act_lo", [P, 2, BLOCK], F32R)
    acc = bank[0:4]
    front = bank[4:8]

    block = ctx.enter_context(nc.Block())


    @block.tensor
    def _(pe):
        def turn(i, g):
            for t in range(BLOCK_TILES):
                mm = pe.transpose(front[g][:, t * P:(t + 1) * P], x[:, t, g * P:(g + 1) * P], ident[:, :])
            mm.then_inc(xt_mm, 1)

        def step(i, more):
            pe.wait_ge(xt_done, i * KT + KT)
            for g in range(GROUPS):
                for k in range(KT):
                    for n, (w, y) in enumerate(((basis_hi, xt_hi), (basis_hi, xt_lo), (basis_lo, xt_hi))):
                        mm = pe.matmul(front[g][0:STACK, :], w[:, g, k, :], y[:, k, :], start=(k == 0 and n == 0),
                                       stop=(k == KT - 1 and n == 2))
                mm.then_inc(feat_mm, 1)

            def gate_up(m):
                g = m // GM
                if m < 2:
                    pe.wait_ge(feat_done, i * GROUPS + 2 * m + 2)
                elif m % GM == 0:
                    pe.wait_ge(feat_done, i * GROUPS + g + 1)
                if m >= 2:
                    pe.wait_ge(prod_done, i * MT + m - 1)
                cols = slice(m * P, (m + 1) * P)
                for n, w in enumerate(NAMES):
                    o = front[2 * (m % 2) + n][:, :]
                    pe.matmul(o, near_hi[w][:, cols], xt_hi[:, g, :], start=True, stop=False)
                    pe.matmul(o, near_lo[w][:, cols], xt_hi[:, g, :], start=False, stop=False)
                    pe.matmul(o, near_hi[w][:, cols], xt_lo[:, g, :], start=False, stop=False)
                    mm = pe.matmul(o, far[w][:, cols], feat[:, g, :], start=False, stop=True)
                mm.then_inc(gu_mm, 1)

            def down(m):
                pe.wait_ge(act_done, i * MT + m + 1)
                for t in range(BLOCK_TILES):
                    tk = slice(t * P, (t + 1) * P)
                    first, last = m == 0, m == MT - 1
                    if first and not first_step(i):
                        pe.wait_ge(out_ready, i * BLOCK_TILES + t - BLOCK_TILES + 1)
                    pe.matmul(acc[t][:, :], act_hi[:, m % 2, tk], down_hi[:, m, :], start=first, stop=False)
                    pe.matmul(acc[t][:, :], act_lo[:, m % 2, tk], down_hi[:, m, :], start=False, stop=False)
                    mm = pe.matmul(acc[t][:, :], act_hi[:, m % 2, tk], down_lo[:, m, :], start=False, stop=last)
                mm.then_inc(down_mm, 1)

            for m in range(MT + 2):
                if m < MT:
                    gate_up(m)
                elif more:
                    n = m - MT
                    if n == 0:
                        pe.wait_ge(x_ready, (i + 1) * BLOCK_TILES + BLOCK_TILES)
                    pe.wait_ge(prod_done, i * MT + MT - 1 + n)
                    turn(i + 1, 2 * n)
                    turn(i + 1, 2 * n + 1)
                if m >= 2:
                    down(m - 2)

        pe.wait_ge(x_ready, BLOCK_TILES)
        for g in range(KT):
            turn(0, g)
        step(0, True)
        with pe.Fori(1, STEPS - 1) as i:
            step(i, True)
        step(STEPS - 1, False)

    @block.scalar
    def _(act):
        def turned(i, g):
            act.wait_ge(xt_mm, i * KT + g + 1)
            act.activation(xt_hi[:, g, :], front[g][:, :], ACT.Copy).then_inc(xt_hi_done, 1)

        def step(i, more):
            for g in range(GROUPS):
                act.wait_ge(feat_mm, i * GROUPS + g + 1)
                act.activation(feat[:, g, :], front[g][0:STACK, :], ACT.Copy).then_inc(feat_hi, 1)

            def copy_hi(m):
                act.wait_ge(prod_done, i * MT + m + 1)
                if m >= 2 or not first_step(i):
                    act.wait_ge(down_mm, i * MT + m - 1)
                act.activation(act_hi[:, m % 2, :], act_f[:, m % 2, :], ACT.Copy).then_inc(act_hi_done, 1)

            for m in range(MT):
                act.wait_ge(gu_mm, i * MT + m + 1)
                if m >= 2:
                    act.wait_ge(act_done, i * MT + m - 1)
                act.activation(act_f[:, m % 2, :], front[2 * (m % 2)][:, :], ACT.Silu).then_inc(silu_done, 1)
                if m > 0:
                    copy_hi(m - 1)
            copy_hi(MT - 1)
            if more:
                for g in range(KT):
                    turned(i + 1, g)

        for g in range(KT):
            turned(0, g)
        step(0, True)
        with act.Fori(1, STEPS - 1) as i:
            step(i, True)
        step(STEPS - 1, False)

    @block.gpsimd
    def _(pool):
        with pool.Fori(1, STEPS) as i:
            norm2.rstd_of(pool, i)

    @block.vector
    def _(dve):
        def turned(i, g):
            dve.wait_ge(xt_hi_done, i * KT + g + 1)
            dve.tensor_tensor(xt_lo[:, g, :], front[g][:, :], xt_hi[:, g, :].bitcast(F32),
                              ALU.subtract).then_inc(xt_done, 1)

        def step(i, more):
            for g in range(GROUPS):
                mid = slice(FEAT, 2 * FEAT)
                dve.wait_ge(feat_hi, i * GROUPS + g + 1)
                dve.tensor_tensor(feat[mid, g, :], front[g][mid, :], feat[mid, g, :].bitcast(F32),
                                  ALU.subtract).then_inc(feat_done, 1)

            def split_lo(m):
                dve.wait_ge(act_hi_done, i * MT + m + 1)
                dve.tensor_tensor(act_lo[:, m % 2, :], act_f[:, m % 2, :], act_hi[:, m % 2, :].bitcast(F32),
                                  ALU.subtract).then_inc(act_done, 1)

            for m in range(MT):
                dve.wait_ge(silu_done, i * MT + m + 1)
                dve.tensor_tensor(act_f[:, m % 2, :], act_f[:, m % 2, :], front[2 * (m % 2) + 1][:, :],
                                  ALU.mult).then_inc(prod_done, 1)
                if m > 0:
                    split_lo(m - 1)
                if more and m == MT // 2:
                    norm2.moments_of(dve, i + 1)
                if more and m == MT // 2 + 3:
                    norm2.normalise(dve, i + 1, x)
            split_lo(MT - 1)
            if more:
                for g in range(KT):
                    turned(i + 1, g)
            dve.wait_ge(down_mm, i * MT + MT)
            for t in range(BLOCK_TILES):
                dve.tensor_tensor(h_row(i, t), acc[t][:, :], h_row(i, t), ALU.add).then_inc(out_ready, 1)

        for g in range(KT):
            turned(0, g)
        step(0, True)
        with dve.Fori(1, STEPS - 1) as i:
            step(i, True)
        step(STEPS - 1, False)

    @block.sync
    def _(sp):
        rows = out.rearrange("b s d -> (b s) d")
        with sp.Fori(0, STEPS) as i:
            for t in range(BLOCK_TILES):
                sp.wait_ge(out_ready, i * BLOCK_TILES + t + 1)
                sp.dma_start(rows[bass.ds(i * BLOCK + t * P, P), :], h_row(i, t)).then_inc(stored, 16)
        sp.wait_ge(stored, 16 * TILES)



def kernel(x, L0_tok_embed_low, L0_tok_project_up, L0_attn_W_in, L0_attn_b_in, L0_attn_W_out, L0_attn_b_out,
           L0_ffn_gate_cp, L0_ffn_up_cp, L0_ffn_down_cp):
    import concourse.bacc as bacc
    from concourse.bass_utils import run_bass_kernel_spmd

    tables, gate_starts, down_starts, d_starts = _tables()
    b_in = np.asarray(L0_attn_b_in)
    arrays = {
        "tokens": np.ascontiguousarray(np.asarray(x).reshape(TILES, P).T).view(np.uint32),
        "embed": np.asarray(L0_tok_embed_low),
        "up_t": np.ascontiguousarray(np.asarray(L0_tok_project_up).T),
        "w_in_t": np.ascontiguousarray(np.asarray(L0_attn_W_in).T),
        "w_out_t": np.ascontiguousarray(np.asarray(L0_attn_W_out).T),
        "b_qk": np.ascontiguousarray(b_in[:2 * HID].reshape(2 * KT, P).T),
        "b_v": np.ascontiguousarray(b_in[2 * HID:].reshape(KT, P).T),
        "b_out": np.asarray(L0_attn_b_out).reshape(1, HID),
        "gate_points": _windows(np.asarray(L0_ffn_gate_cp), gate_starts, G_WIN, MT),
        "up_points": _windows(np.asarray(L0_ffn_up_cp), gate_starts, G_WIN, MT),
        "down_points": _windows(np.asarray(L0_ffn_down_cp), down_starts, D_WIN, KT),
        **tables,
    }
    nc = bacc.Bacc("TRN2", target_bir_lowering=False, num_devices=1)
    aps = {n: nc.dram_tensor(f"in_{n}", v.shape, mybir.dt.from_np(v.dtype), kind="ExternalInput").ap() for n, v in arrays.items()}
    out = nc.dram_tensor("out", (BATCH, SEQ, HID), F32, kind="ExternalOutput").ap()
    build(nc, aps, out, d_starts)
    return run_bass_kernel_spmd(nc, [{f"in_{n}": v for n, v in arrays.items()}], core_ids=[0]).results[0]["out"]
```

```python
from contextlib import ExitStack
from math import comb

import numpy as np

import concourse.bass as bass
from concourse import mybir

F32 = mybir.dt.float32
F32R = mybir.dt.float32r
U32 = mybir.dt.uint32
U8 = mybir.dt.uint8
ALU = mybir.AluOpType
ACT = mybir.ActivationFunctionType
AX = mybir.AxisListType

P = 128
HID = 512
INTER = 2048
BATCH, SEQ = 8, 256
TOKENS = BATCH * SEQ
RANK = 64
HEADS, HEAD_DIM = 16, 32
EPS = 1e-5
SCALE = float(HEAD_DIM) ** -0.5
MASKED = -1e30

BLOCK_TILES = 4
BLOCK = BLOCK_TILES * P
STEPS = TOKENS // BLOCK
TILES = TOKENS // P
KT = HID // P
MT = INTER // P
BLOCK_SEQS = BLOCK // SEQ
SEQ_TILES = SEQ // P
QUAD = P // HEAD_DIM
GROUPS_A = KT * BLOCK_SEQS

N_WEIGHTS = HID * INTER
N_CTRL = max(16, int(N_WEIGHTS / 128.9))
DEG = 4
WINDOWS = 4
GROUPS = 4
WIN = 32
PITCH = 129
SEGS = WINDOWS + 1
MOM = SEGS * DEG
FEAT = 32
STACK = 3 * FEAT
U_SCALE = 64.0
GM = MT // GROUPS
D_SEGS = 17
D_WIDE = FEAT // DEG
D_SCALE = 128.0
G_WIN = SEGS + 3
D_WIN = D_SEGS + 3



def _grid():
    t = np.linspace(0.0, N_CTRL - 1.0, N_WEIGHTS, dtype=np.float64)
    return np.clip(np.floor(t).astype(np.int64), 0, N_CTRL - 2), (N_CTRL - 1.0) / (N_WEIGHTS - 1)


_CR = 0.5 * np.array([[0, 2, 0, 0], [-1, 0, 1, 0], [2, -5, 4, -1], [-1, 3, -3, 1]], np.float64)


def _psi(center, scale):
    out = np.zeros((4,) + center.shape + (DEG,))
    for d in range(DEG):
        for e in range(d, DEG):
            out[..., d] += np.multiply.outer(_CR[e], comb(e, d) * center ** (e - d) * scale ** d)
    return out


def _split(a):
    a = np.ascontiguousarray(a, np.float32)
    bits = a.view(np.uint32)
    hi = ((bits + 0x7FF + ((bits >> 12) & 1)) & np.uint32(0xFFFFF000)).view(np.float32)
    return hi, a - hi


def _stack(a):
    hi, lo = _split(np.concatenate([a, np.zeros((FEAT - len(a),) + a.shape[1:])]).reshape(FEAT, -1))
    return np.concatenate([hi, lo, hi])


def _tables():
    interval, step = _grid()
    rows = interval.reshape(INTER, HID)
    first = rows[:, 0]
    ends = np.array([[np.searchsorted(r, r[0] + 1 + c) for c in range(WINDOWS)] for r in rows])
    start = PITCH * np.arange(WINDOWS)[None] + WIN * np.arange(GROUPS)[:, None]
    fits = ((ends[:, None] >= start) & (ends[:, None] <= start + WIN + 1)) | (
        (ends[:, None] >= HID) & (start + WIN + 1 >= HID))
    fits = fits.all(2)
    group = [[] for _ in range(GROUPS)]
    for i in sorted(range(INTER), key=lambda i: (fits[i].sum(), int(np.argmax(fits[i])))):
        options = np.flatnonzero(fits[i])
        group[next(g for g in options if len(group[g]) < INTER // GROUPS)].append(i)
    assert all(len(g) == INTER // GROUPS for g in group)
    order = np.concatenate([np.array(sorted(g)) for g in group])
    tile = order.reshape(MT, P)

    def center(g, s):
        return PITCH * s + WIN * g - 48

    where = np.array([[PITCH * c + WIN * g + j for c in range(WINDOWS) for j in range(WIN)] for g in range(GROUPS)])
    spare = where >= HID
    where = np.where(spare, (where - HID + 1) * PITCH - 1, where)

    psi = np.zeros((4, INTER, SEGS, DEG))
    phi = np.zeros((5, INTER, WINDOWS))
    for n, i in enumerate(order):
        g = n // (INTER // GROUPS)
        s = np.arange(SEGS)
        f0 = (i * HID + center(g, s)) * step - (first[i] + s)
        psi[:, n] = _psi(f0, U_SCALE * step)
        for c in range(WINDOWS):
            h = start[g, c] + WIN
            if h < HID and rows[i, h] == first[i] + c:
                f = (i * HID + h) * step - (first[i] + c)
                phi[0:4, n, c] += _CR.T @ (f ** np.arange(4))
                phi[1:5, n, c] -= _CR.T @ ((f - 1) ** np.arange(4))

    moments = np.zeros((P, GROUPS, KT, FEAT))
    for g in range(GROUPS):
        for t in range(KT):
            for r in range(P):
                h = where[t, r]
                if t == g and not spare[t, r]:
                    continue
                s = int((h >= start[g] + WIN).sum())
                moments[r, g, t, DEG * s:DEG * s + DEG] = ((h - center(g, s)) / U_SCALE) ** np.arange(DEG)
                for c in range(WINDOWS):
                    if h == start[g, c] + WIN:
                        moments[r, g, t, MOM + c] = 1.0
    moments = np.concatenate([moments] * 3, axis=3)

    evaluate = np.zeros((MOM, GROUPS, 2, P))
    side = np.zeros((P, INTER), np.uint8)
    for g in range(GROUPS):
        for r in range(P):
            if spare[g, r]:
                continue
            c, h = r // WIN, where[g, r]
            for x in range(2):
                u = (h - center(g, c + x)) / U_SCALE
                evaluate[DEG * (c + x):DEG * (c + x + 1), g, x, r] = u ** np.arange(DEG)
            n = slice(g * INTER // GROUPS, (g + 1) * INTER // GROUPS)
            side[r, n] = rows[order[n], h] - first[order[n]] - c
    assert side.max() == 1

    d_first = interval.reshape(HID, INTER)[:, 0]
    s = np.arange(D_SEGS)
    f0 = (np.arange(HID)[:, None] * INTER + PITCH * s) * step - (d_first[:, None] + s)
    d_psi = _psi(f0, D_SCALE * step)
    d_eval = np.zeros((FEAT, MT, 2, P))
    d_side = np.zeros((P, MT, HID), np.uint8)
    low = np.floor(np.arange(INTER) * step).astype(np.int64)
    kind = low[tile].reshape(GROUPS, GM, P)
    d_starts = [min(int(kind[:, r].min()), D_SEGS - D_WIDE) for r in range(GM)]
    assert all(kind[:, r].max() + 1 < d_starts[r] + D_WIDE for r in range(GM))
    for m in range(MT):
        for r in range(P):
            i = tile[m, r]
            for x in range(2):
                k = low[i] + x
                at = DEG * (k - d_starts[m % GM])
                d_eval[at:at + DEG, m, x, r] = ((i - PITCH * k) / D_SCALE) ** np.arange(DEG)
            d_side[r, m] = interval.reshape(HID, INTER)[:, i] - d_first - low[i]
    assert d_side.max() == 1

    def by_partition(a, lead):
        a = a.reshape(a.shape[:lead] + (-1, P) + a.shape[lead + 1:])
        return np.moveaxis(a, lead + 1, 0).reshape(P, -1)

    causal = np.where(np.arange(P)[None] > np.arange(P)[:, None], MASKED, 0.0)
    f32 = {
        "c_psi": by_partition(psi, 1), "c_phi": by_partition(phi, 1), "c_dpsi": by_partition(d_psi, 1),
        "c_mask": np.tile(causal, (1, QUAD)), "c_ident": np.eye(P),
    }
    tables = {k: np.ascontiguousarray(v, np.float32) for k, v in f32.items()}
    tables["c_basis_hi"], tables["c_basis_lo"] = _split(moments.reshape(P, -1))
    tables["c_evaluate"], tables["c_deval"] = _stack(evaluate), _stack(d_eval)
    tables["c_side"] = side.view(np.uint32)
    tables["c_dside"] = d_side.reshape(P, -1).view(np.uint32)
    return tables, first[order], d_first, d_starts


def _windows(points, starts, width, tiles):
    padded = np.concatenate([points[:1], points, np.repeat(points[-1:], D_WIN)])
    rows = np.stack([padded[s:s + width] for s in starts])
    return np.ascontiguousarray(rows.reshape(tiles, P, width).transpose(1, 0, 2).reshape(P, -1))



def build(nc, a, out, d_starts):
    with ExitStack() as top:
        banks = top.enter_context(nc.psum_tensor("banks", [P, 8, 512], F32))
        bank = [banks[:, n, :] for n in range(8)]

        def sems(*names):
            return [top.enter_context(nc.semaphore(n)) for n in names]

        h_all = top.enter_context(nc.sbuf_tensor("h_all", [P, TILES, HID], F32))
        ident = top.enter_context(nc.sbuf_tensor("ident", [P, P], F32))
        norm2 = SecondNorm(nc, top, sems, h_all)
        splines = Splines(nc, a, sems, d_starts)
        with ExitStack() as ctx:
            attention(nc, a, ctx, sems, banks, bank, h_all, ident, splines, norm2)
        with ExitStack() as ctx:
            ffn(nc, a, out, ctx, sems, bank, h_all, ident, splines, norm2)


def chained(engine, sem):
    count = [0]

    def link(instruction):
        count[0] += 1
        instruction.then_inc(sem, 1)
        engine.wait_ge(sem, count[0])
    return link


def apart(engine, tick):
    engine.sem_inc(tick, 1)


def attention(nc, a, ctx, sems, banks, bank, h_all, ident, splines, norm2):
    def sb(name, shape, dt=F32, where=ctx):
        return where.enter_context(nc.sbuf_tensor(name, shape, dt))

    win_hi = sb("win_hi", [P, KT, 3 * HID], F32R)
    win_in = raw(nc, "win_in", [P, KT, 3 * HID])
    win_lo = sb("win_lo", [P, KT, 3 * HID], F32R)
    xt_hi = sb("xt_hi", [P, KT, BLOCK], F32R)
    xt_lo = sb("xt_lo", [P, KT, BLOCK], F32R)
    assert 4 * 2 * KT * (3 * HID + BLOCK) >= splines.size
    wout_hi = sb("wout_hi", [P, KT, HID], F32R)
    wout_in = raw(nc, "wout_in", [P, KT, HID])
    wout_lo = sb("wout_lo", [P, KT, HID], F32R)
    up_hi = sb("up_hi", [P, HID], F32R)
    up_in = raw(nc, "up_in", [P, HID])
    up_lo = sb("up_lo", [P, HID], F32R)
    late = TILES * RANK // HID
    low_all = h_all[:, TILES - late:, :].rearrange("p a (b r) -> p (a b) r", r=RANK)
    tok = sb("tok", [P, TILES], U32)
    bias_qk = sb("bias_qk", [P, 2 * KT])
    bias_v = sb("bias_v", [P, KT])
    bias_out = sb("bias_out", [P, HID])
    mask_in = raw(nc, "mask_in", [P, QUAD * P])
    mask = sb("mask", [P, QUAD * P], F32R)
    ident_r = sb("ident_r", [P, P], F32R)

    tok_in, ident_in, mask_loaded, bias_in, split_hi, split_lo, mask_ready, gathered_0, gathered_1, gathered_rest = sems(
        "tok_in", "ident_in", "mask_loaded", "bias_in", "split_hi", "split_lo", "mask_ready", "gathered_0",
        "gathered_1", "gathered_rest")

    def third(t, n):
        return t[:, :, n * HID:(n + 1) * HID]

    UP, WQ, WK, WV, WOUT = range(5)
    weight_in = sems("up_loaded", "wq_loaded", "wk_loaded", "wv_loaded", "wout_loaded")
    weights = [(up_in[:, :], up_hi[:, :], up_lo[:, :])] \
        + [(third(win_in, n), third(win_hi, n), third(win_lo, n)) for n in range(3)] \
        + [(wout_in[:, :, :], wout_hi[:, :, :], wout_lo[:, :, :])]

    low2 = sb("low2", [P, BLOCK_TILES, 2, RANK])
    low_t = sb("low_t", [P, BLOCK], F32R)
    x = sb("x", [P, BLOCK_TILES, HID])
    q_hi = sb("q_hi", [P, 2, BLOCK], F32R)
    q_lo = sb("q_lo", [P, 2, BLOCK], F32R)
    k_hi = sb("k_hi", [P, BLOCK_TILES, QUAD, P], F32R)
    k_lo = sb("k_lo", [P, BLOCK_TILES, QUAD, P], F32R)
    v = sb("v", [P, BLOCK_TILES, HID])
    p = sb("p", [P, 2, 3, QUAD, P])
    pt = sb("pt", [P, 2, 3, BLOCK])
    at_hi = sb("at_hi", [P, KT, BLOCK], F32R)
    at_lo = sb("at_lo", [P, KT, BLOCK], F32R)
    row_max = sb("row_max", [P, 2, 2, QUAD])
    neg_max = sb("neg_max", [P, 2, 2, QUAD])
    sums = sb("sums", [P, 2, 2, QUAD])
    recips = sb("recips", [P, 2, 2, QUAD])
    stats = sb("stats", [P, BLOCK_TILES, 6])
    mean_var = sb("mean_var", [P, BLOCK_TILES, 2])
    var_eps = sb("var_eps", [P, BLOCK_TILES])
    minus_half = sb("minus_half", [P, BLOCK_TILES])
    rstd = sb("rstd", [P, BLOCK_TILES])

    (low2_ready, low_mm, low_hi, low_ready, h_mm, h_copied, h_kept, stat_ready, rstd_ready, x_ready, xt_mm, xt_hi_done,
     xt_done, proj_mm, proj_hi, proj_done, k_ready, sc_mm, max_read, max_ready, p_ready, recip_ready, p_normal, pt_mm,
     pt_done, pv_mm, at_hi_done, at_done, out_mm, out_done, keys_clear, dve_a, pool_a, dve_tick, pool_tick) = sems(
        "low2_ready", "low_mm", "low_hi", "low_ready", "h_mm", "h_copied", "h_kept", "stat_ready", "rstd_ready",
        "x_ready", "xt_mm", "xt_hi_done", "xt_done", "proj_mm", "proj_hi", "proj_done", "k_ready", "sc_mm", "max_read",
        "max_ready", "p_ready", "recip_ready", "p_normal", "pt_mm", "pt_done", "pv_mm", "at_hi_done",
        "at_done", "out_mm", "out_done", "keys_clear", "dve_a", "pool_a", "dve_tick", "pool_tick")

    score_banks = banks[:, 0:3, :]
    turn_bank = [bank[3], bank[4]]
    o_banks = banks[:, 5:7, :]
    spare = bank[7]
    out_bank = [bank[0], bank[1], bank[3], bank[4]]
    ORDER = (("q", 0, bank[7]), ("k", 0, bank[7]), ("v", 0, bank[5]), ("v", 1, bank[6]), ("v", 2, bank[5]),
             ("q", 1, bank[7]), ("k", 1, bank[7]), ("v", 3, bank[6]), ("q", 2, bank[7]), ("k", 2, bank[7]),
             ("q", 3, bank[7]), ("k", 3, bank[7]))
    JOBS = len(ORDER)
    PLACE = {(what, n): j for j, (what, n, _) in enumerate(ORDER)}
    WITH_GROUP = [PLACE[("q", 1)], PLACE[("k", 1)], PLACE[("q", 2)], PLACE[("k", 2)], PLACE[("q", 3)], PLACE[("k", 3)]]
    BLOCKS = ((0, 0), (1, 0), (1, 1))

    def token_bank(i, n):
        return bank[n] if first_step(i) else spare

    def split3(pe, psum_out, hi_t, lo_t, hi, lo, first, last):
        pe.matmul(psum_out, hi_t, hi, start=first, stop=False)
        pe.matmul(psum_out, lo_t, hi, start=False, stop=False)
        return pe.matmul(psum_out, hi_t, lo, start=False, stop=last)

    block = ctx.enter_context(nc.Block())

    HIS = KT * (1 + 2 * QUAD)
    LN_AT = 3
    XT_AT = 6

    @block.tensor
    def _(pe):
        def weight_ready(w):
            pe.wait_ge(split_lo, w + 1)

        def low_turn(i):
            pe.wait_ge(low2_ready, i + 1)
            for t in range(BLOCK_TILES):
                mm = pe.transpose(spare[:, t * P:(t + 1) * P], low2[:, t, :, :].rearrange("p a r -> p (a r)"),
                                  ident[:, :])
            mm.then_inc(low_mm, 1)

        def embed(i, t):
            o = token_bank(i, t)
            if t == 0:
                pe.wait_ge(low_ready, i + 1)
            elif not first_step(i):
                pe.wait_ge(h_copied, i * BLOCK_TILES + t)
            tk = slice(t * P, (t + 1) * P)
            pe.matmul(o[:, :], low_t[:, tk], up_hi[:, :], start=True, stop=False)
            pe.matmul(o[:, :], low_t[0:RANK, tk], up_lo[0:RANK, :], start=False, stop=True).then_inc(h_mm, 1)

        def turn_tokens(i, k):
            if k == 0:
                pe.wait_ge(x_ready, i * BLOCK_TILES + BLOCK_TILES)
            elif not first_step(i):
                pe.wait_ge(xt_done, i * KT + k)
            for t in range(BLOCK_TILES):
                mm = pe.transpose(token_bank(i, k)[:, t * P:(t + 1) * P], x[:, t, k * P:(k + 1) * P], ident[:, :])
            mm.then_inc(xt_mm, 1)

        def project(i, j):
            what, m, o = ORDER[j]
            if j == 0:
                pe.wait_ge(xt_done, i * KT + KT)
            for k in range(KT):
                if what == "v":
                    tk, cols = slice(m * P, (m + 1) * P), slice(2 * HID, 3 * HID)
                    mm = split3(pe, o[:, :], xt_hi[:, k, tk], xt_lo[:, k, tk],
                                win_hi[:, k, cols], win_lo[:, k, cols], k == 0, k == KT - 1)
                else:
                    at = (what == "k") * HID + m * P
                    cols = slice(at, at + P)
                    mm = split3(pe, o[:, :], win_hi[:, k, cols], win_lo[:, k, cols],
                                xt_hi[:, k, :], xt_lo[:, k, :], k == 0, k == KT - 1)
            mm.then_inc(proj_mm, 1)

        def tile_read(i, what, n):
            pe.wait_ge(proj_done, i * JOBS + PLACE[(what, n)] + 1)

        def scores(i, g):
            m, sq = divmod(g, BLOCK_SEQS)
            if sq == 0:
                tile_read(i, "q", m)
                pe.wait_ge(k_ready, i * KT + m + 1)
            else:
                tile_read(i, "k", m)
            if g > 0:
                pe.wait_ge(p_ready, i * GROUPS_A + g)
            for n, (q, k) in enumerate(BLOCKS):
                o = score_banks[:, n, :]
                tq = slice(sq * SEQ + q * P, sq * SEQ + (q + 1) * P)
                if q == k:
                    pe.matmul(o, ident_r[:, :], mask[:, :], start=True, stop=False)
                tk = sq * SEQ_TILES + k
                mm = split3(pe, o, q_hi[:, m % 2, tq], q_lo[:, m % 2, tq],
                            k_hi[:, tk, :, :].rearrange("p h k -> p (h k)"),
                            k_lo[:, tk, :, :].rearrange("p h k -> p (h k)"), q != k, True)
                if n != 1:
                    mm.then_inc(sc_mm, 1)

        def turn(i, g):
            pe.wait_ge(p_normal, i * GROUPS_A + g + 1)
            for n in range(3):
                c = 3 * g + n
                if c >= 2:
                    pe.wait_ge(pt_done, i * 3 * GROUPS_A + c - 1)
                for hd in range(QUAD):
                    mm = pe.transpose(turn_bank[c % 2][:, hd * P:(hd + 1) * P], p[:, g % 2, n, hd, :], ident[:, :])
                mm.then_inc(pt_mm, 1)

        def values(i, g):
            m, sq = divmod(g, BLOCK_SEQS)
            cols = slice(m * P, (m + 1) * P)
            pe.wait_ge(pt_done, i * 3 * GROUPS_A + 3 * g + 3)
            if g > 0:
                pe.wait_ge(at_done, i * GROUPS_A + g)
            else:
                tile_read(i, "v", BLOCK_TILES - 1)
            for n, (q, k) in enumerate(BLOCKS):
                mm = pe.matmul(o_banks[:, q, :], v[:, sq * SEQ_TILES + k, cols], pt[:, g % 2, n, :],
                               start=k == 0, stop=q == k)
            mm.then_inc(pv_mm, 1)

        def project_out(i, t):
            if t == 0:
                pe.wait_ge(p_ready, i * GROUPS_A + GROUPS_A)
            if t % SEQ_TILES == 0:
                pe.wait_ge(at_done, i * GROUPS_A + GROUPS_A - BLOCK_SEQS + t // SEQ_TILES + 1)
            tk = slice(t * P, (t + 1) * P)
            for k in range(KT):
                mm = split3(pe, out_bank[t][:, :], at_hi[:, k, tk], at_lo[:, k, tk],
                            wout_hi[:, k, :], wout_lo[:, k, :], k == 0, k == KT - 1)
            mm.then_inc(out_mm, 1)

        def step(i, more):
            nxt = i + 1
            for g in range(GROUPS_A):
                if g == 0:
                    if not first_step(i):
                        project_out(i - 1, 2)
                    if more:
                        tile_read(i, "k", 0)
                        low_turn(nxt)
                    if first_step(i):
                        project(i, PLACE[("v", 0)])
                    else:
                        project_out(i - 1, 3)
                    if more:
                        embed(nxt, 0)
                    if not first_step(i):
                        project(i, PLACE[("v", 0)])
                    if more:
                        embed(nxt, 1)
                    project(i, PLACE[("v", 1)])
                    if more:
                        embed(nxt, 2)
                    tile_read(i, "v", 0)
                    project(i, PLACE[("v", 2)])
                    if more:
                        pe.wait_ge(h_copied, nxt * BLOCK_TILES + 3)
                    else:
                        tile_read(i, "k", 0)
                    project(i, PLACE[("q", 1)])
                else:
                    scores(i, g)
                    if g < len(WITH_GROUP):
                        before = ORDER[WITH_GROUP[g] - (2 if g == 2 else 1)]
                        tile_read(i, before[0], before[1])
                        if more and g == 3:
                            pe.wait_ge(h_copied, nxt * BLOCK_TILES + BLOCK_TILES)
                        project(i, WITH_GROUP[g])
                if g == 1 and not first_step(i):
                    pe.wait_ge(out_done, i * BLOCK_TILES)
                if g >= 1:
                    turn(i, g - 1)
                if g == 1:
                    tile_read(i, "v", 1)
                    project(i, PLACE[("v", 3)])
                if more and g >= XT_AT:
                    if g == XT_AT:
                        tile_read(i, "k", KT - 1)
                    turn_tokens(nxt, 2 * (g - XT_AT))
                if g >= 2:
                    values(i, g - 2)
                if more and g == 2:
                    tile_read(i, "q", 2)
                    embed(nxt, 3)
                if more and g >= XT_AT:
                    turn_tokens(nxt, 2 * (g - XT_AT) + 1)
            values(i, GROUPS_A - 2)
            if more:
                project(nxt, PLACE[("q", 0)])
            turn(i, GROUPS_A - 1)
            if first_step(i):
                weight_ready(WOUT)
            project_out(i, 0)
            if more:
                tile_read(nxt, "q", 0)
                project(nxt, PLACE[("k", 0)])
            project_out(i, 1)
            values(i, GROUPS_A - 1)
            if more:
                pe.wait_ge(out_done, i * BLOCK_TILES + 2)
                scores(nxt, 0)
            else:
                project_out(i, 2)
                project_out(i, 3)

        pe.wait_ge(ident_in, 16)
        low_turn(0)
        weight_ready(UP)
        for t in range(BLOCK_TILES):
            embed(0, t)
        for k in range(KT):
            turn_tokens(0, k)
        weight_ready(WK)
        project(0, PLACE[("q", 0)])
        tile_read(0, "q", 0)
        project(0, PLACE[("k", 0)])
        pe.wait_ge(mask_ready, 2)
        scores(0, 0)
        weight_ready(WV)
        step(0, True)
        with pe.Fori(1, STEPS - 1) as i:
            step(i, True)
        step(STEPS - 1, False)

    def head_keys(t, r, sq):
        return t[r * HEAD_DIM:(r + 1) * HEAD_DIM, sq * SEQ_TILES:(sq + 1) * SEQ_TILES, r, :]

    def copies(m, sq, r):
        return m * (1 + 2 * QUAD) + 1 + sq * QUAD + r + 1

    def by_tile(ap):
        return ap.rearrange("p (t k) -> p t k", k=P)

    @block.scalar
    def _(act):
        def weight_hi(w):
            act.wait_ge(weight_in[w], 32 if w == UP else 16)
            src, hi, _ = weights[w]
            act.activation(hi, src, ACT.Copy).then_inc(split_hi, 1)

        def low(i):
            act.wait_ge(low_mm, i + 1)
            act.activation(low_t[:, :], spare[:, :], ACT.Copy).then_inc(low_hi, 1)

        def embedded(i, t):
            act.wait_ge(h_mm, i * BLOCK_TILES + t + 1)
            act.activation(x[:, t, :], token_bank(i, t)[:, :], ACT.Copy).then_inc(h_copied, 1)

        def tokens_hi(i, k):
            act.wait_ge(xt_mm, i * KT + k + 1)
            act.activation(xt_hi[:, k, :], token_bank(i, k)[:, :], ACT.Copy).then_inc(xt_hi_done, 1)

        def queries(i, m):
            j = PLACE[("q", m)]
            act.wait_ge(proj_mm, i * JOBS + j + 1)
            act.activation(q_hi[:, m % 2, :], ORDER[j][2][:, :], ACT.Identity,
                           bias=bias_qk[:, m:m + 1]).then_inc(proj_hi, 1)

        def keys(i, m, sq):
            j = PLACE[("k", m)]
            act.wait_ge(proj_mm, i * JOBS + j + 1)
            if sq > 0:
                act.wait_ge(k_ready, i * KT + m + 1)
            for r in range(QUAD):
                rows = slice(r * HEAD_DIM, (r + 1) * HEAD_DIM)
                act.activation(head_keys(k_hi, r, sq), by_tile(ORDER[j][2][rows, sq * SEQ:(sq + 1) * SEQ]),
                               ACT.Identity, bias=bias_qk[rows, KT + m:KT + m + 1]).then_inc(proj_hi, 1)

        def exponentials(i, g):
            act.wait_ge(max_ready, i * GROUPS_A + g + 1)
            for hd in range(QUAD):
                for q in range(SEQ_TILES):
                    blocks = slice(q, 2 * q + 1)
                    e = act.activation(p[:, g % 2, blocks, hd, :], score_banks[:, blocks, hd * P:(hd + 1) * P],
                                       ACT.Exp, bias=neg_max[:, g % 2, q, hd:hd + 1], scale=SCALE,
                                       accum_out=sums[:, g % 2, q, hd:hd + 1])
            e.then_inc(p_ready, 1)

        def attended(i, g):
            m, sq = divmod(g, BLOCK_SEQS)
            act.wait_ge(pv_mm, i * GROUPS_A + g + 1)
            for r in range(QUAD):
                rows = slice(r * HEAD_DIM, (r + 1) * HEAD_DIM)
                act.activation(by_tile(at_hi[rows, m, sq * SEQ:(sq + 1) * SEQ]), o_banks[rows, :, r * P:(r + 1) * P],
                               ACT.Identity, bias=bias_v[rows, m:m + 1]).then_inc(at_hi_done, 1)

        def step(i, more):
            nxt = i + 1
            for g in range(GROUPS_A):
                exponentials(i, g)
                if more and g == 0:
                    low(nxt)
                    for t in range(BLOCK_TILES - 1):
                        embedded(nxt, t)
                if first_step(i) and g == 1:
                    weight_hi(WOUT)
                if g < len(WITH_GROUP):
                    if g % 2 == 0:
                        queries(i, 1 + g // 2)
                    else:
                        keys(i, 1 + g // 2, 0)
                if more and g >= XT_AT:
                    tokens_hi(nxt, 2 * (g - XT_AT))
                if g >= 2:
                    attended(i, g - 2)
                if g < len(WITH_GROUP) and g % 2 == 1:
                    keys(i, 1 + g // 2, 1)
                if more and g == 2:
                    embedded(nxt, 3)
                if more and g >= XT_AT:
                    tokens_hi(nxt, 2 * (g - XT_AT) + 1)
            attended(i, GROUPS_A - 2)
            if more:
                queries(nxt, 0)
                keys(nxt, 0, 0)
                keys(nxt, 0, 1)
            else:
                splines.as_parts(act)
            attended(i, GROUPS_A - 1)

        weight_hi(UP)
        weight_hi(WQ)
        low(0)
        for t in range(BLOCK_TILES):
            embedded(0, t)
        weight_hi(WK)
        for k in range(KT):
            tokens_hi(0, k)
        weight_hi(WV)
        act.wait_ge(bias_in, 3 * 16)
        act.wait_ge(keys_clear, 2)
        act.wait_ge(mask_loaded, 16)
        act.wait_ge(ident_in, 16)
        act.activation(mask[:, :], mask_in[:, :], ACT.Copy).then_inc(mask_ready, 1)
        act.activation(ident_r[:, :], ident[:, :], ACT.Copy).then_inc(mask_ready, 1)
        queries(0, 0)
        keys(0, 0, 0)
        keys(0, 0, 1)
        step(0, True)
        with act.Fori(1, STEPS - 1) as i:
            step(i, True)
        step(STEPS - 1, False)
        splines.lay_out_down(act)

    @block.gpsimd
    def _(pool):
        def keep(i, tiles):
            for t in tiles:
                pool.wait_ge(h_copied, i * BLOCK_TILES + t + 1)
                pool.tensor_tensor(h_all[:, bass.ds(i * BLOCK_TILES + t, 1), :].rearrange("p a n -> p (a n)"),
                                   x[:, t, :], bias_out[:, :], ALU.add).then_inc(h_kept, 1)

        def inverse_deviation(i):
            pool.wait_ge(stat_ready, i + 1)
            apart(pool, pool_tick)
            pool.tensor_scalar(var_eps[:, :], mean_var[:, :, 1], EPS, None, ALU.add).then_inc(pool_a, 1)
            pool.wait_ge(pool_a, i + 1)
            pool.tensor_tensor(rstd[:, :], var_eps[:, :], minus_half[:, :], ALU.pow).then_inc(rstd_ready, 1)

        def step(i, more):
            for g in range(GROUPS_A):
                pool.wait_ge(recip_ready, i * GROUPS_A + g + 1)
                for n in range(3):
                    part = p[:, g % 2, n, :, :]
                    ins = pool.tensor_tensor(part, part, recips[:, g % 2, min(n, 1), :].unsqueeze(2)
                                             .broadcast_to([P, QUAD, P]), ALU.mult)
                ins.then_inc(p_normal, 1)
                if more and g == LN_AT - 1:
                    keep(i + 1, range(BLOCK_TILES - 1))
                if not more and g == GROUPS_A - 2:
                    splines.down_coefficients(pool)
                if more and g == LN_AT:
                    inverse_deviation(i + 1)
                    keep(i + 1, range(BLOCK_TILES - 1, BLOCK_TILES))

        def gather(tiles, done):
            for n in tiles:
                pool.indirect_dma_start(
                    out=low_all[:, n, :], out_offset=None, in_=a["embed"],
                    in_offset=bass.IndirectOffsetOnAxis(ap=tok[:, n:n + 1], axis=0)).then_inc(done, 16)

        pool.wait_ge(tok_in, 16)
        gather(range(BLOCK_TILES), gathered_0)
        pool.memset(minus_half[:, :], -0.5)
        pool.wait_ge(bias_in, 3 * 16)
        keep(0, range(BLOCK_TILES - 1))
        inverse_deviation(0)
        keep(0, range(BLOCK_TILES - 1, BLOCK_TILES))
        gather(range(BLOCK_TILES, 2 * BLOCK_TILES), gathered_1)
        gather(range(2 * BLOCK_TILES, TILES), gathered_rest)
        step(0, True)
        with pool.Fori(1, STEPS - 1) as i:
            step(i, True)
        step(STEPS - 1, False)
        splines.coefficients(pool)
        norm2.rstd_of(pool, 0)

    @block.vector
    def _(dve):
        def weight_lo(w):
            dve.wait_ge(split_hi, w + 1)
            src, hi, lo = weights[w]
            dve.tensor_tensor(lo, src, hi.bitcast(F32), ALU.subtract).then_inc(split_lo, 1)

        def look_up(i):
            if first_step(i):
                dve.wait_ge(gathered_0, 16 * BLOCK_TILES)
            elif isinstance(i, int):
                dve.wait_ge(gathered_1, 16 * BLOCK_TILES)
            else:
                dve.wait_ge(gathered_rest, 16 * (TILES - 2 * BLOCK_TILES))
            dve.tensor_copy(low2[:, :, :, :], low_all[:, bass.ds(i * BLOCK_TILES, BLOCK_TILES), :].unsqueeze(2)
                            .broadcast_to([P, BLOCK_TILES, 2, RANK])).then_inc(low2_ready, 1)

        def low(i):
            dve.wait_ge(low_hi, i + 1)
            dve.tensor_tensor(low_t[RANK:, :], spare[RANK:, :], low_t[RANK:, :].bitcast(F32),
                              ALU.subtract).then_inc(low_ready, 1)

        def moment_of(i, t):
            dve.wait_ge(h_copied, i * BLOCK_TILES + t + 1)
            dve.bn_stats(stats[:, t, :], x[:, t, :]).then_inc(dve_a, 1)

        def moments_of(i):
            for t in range(BLOCK_TILES):
                dve.wait_ge(dve_a, i * BLOCK_TILES + t + 1)
                apart(dve, dve_tick)
                st = dve.bn_aggr(mean_var[:, t, :], stats[:, t, :])
            st.then_inc(stat_ready, 1)

        def normalise(i):
            dve.wait_ge(rstd_ready, i + 1)
            for t in range(BLOCK_TILES):
                dve.wait_ge(h_kept, i * BLOCK_TILES + t + 1)
                dve.tensor_scalar(x[:, t, :], x[:, t, :], mean_var[:, t, 0:1], rstd[:, t:t + 1], ALU.subtract,
                                  ALU.mult).then_inc(x_ready, 1)

        def tokens_lo(i, k):
            dve.wait_ge(xt_hi_done, i * KT + k + 1)
            dve.tensor_tensor(xt_lo[:, k, :], token_bank(i, k)[:, :], xt_hi[:, k, :].bitcast(F32),
                              ALU.subtract).then_inc(xt_done, 1)

        def v_tile(i, t):
            j = PLACE[("v", t)]
            dve.wait_ge(proj_mm, i * JOBS + j + 1)
            dve.tensor_copy(v[:, t, :], ORDER[j][2][:, :]).then_inc(proj_done, 1)

        def queries(i, m):
            dve.wait_ge(proj_hi, i * HIS + m * (1 + 2 * QUAD) + 1)
            dve.scalar_tensor_tensor(out=q_lo[:, m % 2, :], in0=ORDER[PLACE[("q", m)]][2][:, :],
                                     scalar=bias_qk[:, m:m + 1], in1=q_hi[:, m % 2, :].bitcast(F32), op0=ALU.add,
                                     op1=ALU.subtract).then_inc(proj_done, 1)

        def keys(i, m, sq):
            for r in range(QUAD):
                rows = slice(r * HEAD_DIM, (r + 1) * HEAD_DIM)
                dve.wait_ge(proj_hi, i * HIS + copies(m, sq, r))
                ins = dve.scalar_tensor_tensor(
                    out=head_keys(k_lo, r, sq), in0=by_tile(ORDER[PLACE[("k", m)]][2][rows, sq * SEQ:(sq + 1) * SEQ]),
                    scalar=bias_qk[rows, KT + m:KT + m + 1], in1=head_keys(k_hi, r, sq).bitcast(F32), op0=ALU.add,
                    op1=ALU.subtract)
            ins.then_inc(k_ready if sq == 0 else proj_done, 1)

        def maxima(i, g):
            for q in range(SEQ_TILES):
                dve.wait_ge(sc_mm, i * 2 * GROUPS_A + 2 * g + q + 1)
                src = score_banks[:, q:2 * q + 1, :].rearrange("p b (h k) -> p h b k", h=QUAD)
                dve.tensor_reduce(row_max[:, g % 2, q, :], src, AX.XY, ALU.max).then_inc(max_read, 1)
            dve.wait_ge(max_read, i * 2 * GROUPS_A + 2 * g + 2)
            dve.tensor_scalar(neg_max[:, g % 2, :, :], row_max[:, g % 2, :, :], -SCALE, None,
                              ALU.mult).then_inc(max_ready, 1)

        def over_sums(i, g):
            dve.wait_ge(p_ready, i * GROUPS_A + g + 1)
            dve.reciprocal(recips[:, g % 2, :, :], sums[:, g % 2, :, :]).then_inc(recip_ready, 1)

        def turned(i, g):
            for n in range(3):
                c = 3 * g + n
                dve.wait_ge(pt_mm, i * 3 * GROUPS_A + c + 1)
                dve.tensor_copy(pt[:, g % 2, n, :], turn_bank[c % 2][:, :]).then_inc(pt_done, 1)

        def attended(i, g):
            m, sq = divmod(g, BLOCK_SEQS)
            for r in range(QUAD):
                rows = slice(r * HEAD_DIM, (r + 1) * HEAD_DIM)
                own = slice(sq * SEQ, (sq + 1) * SEQ)
                dve.wait_ge(at_hi_done, (i * GROUPS_A + g) * QUAD + r + 1)
                ins = dve.scalar_tensor_tensor(
                    out=by_tile(at_lo[rows, m, own]), in0=o_banks[rows, :, r * P:(r + 1) * P],
                    scalar=bias_v[rows, m:m + 1], in1=by_tile(at_hi[rows, m, own]).bitcast(F32),
                    op0=ALU.add, op1=ALU.subtract)
            ins.then_inc(at_done, 1)

        def add_out(i, t):
            dve.wait_ge(out_mm, i * BLOCK_TILES + t + 1)
            row = h_all[:, bass.ds(i * BLOCK_TILES + t, 1), :].rearrange("p a n -> p (a n)")
            dve.tensor_tensor(row, out_bank[t][:, :], row, ALU.add).then_inc(out_done, 1)

        def step(i, more):
            nxt = i + 1
            if more:
                look_up(nxt)
            if not first_step(i):
                add_out(i - 1, 2)
            over_sums(i, 0)
            if more:
                low(nxt)
            if not first_step(i):
                add_out(i - 1, 3)
            for t in range(BLOCK_TILES - 1):
                v_tile(i, t)
                if more:
                    moment_of(nxt, t)
            for g in range(GROUPS_A):
                if g > 0:
                    maxima(i, g)
                    turned(i, g - 1)
                    if more and g == LN_AT + 1:
                        normalise(nxt)
                if g > 0:
                    over_sums(i, g)
                if g < len(WITH_GROUP):
                    if g % 2 == 0:
                        queries(i, 1 + g // 2)
                    else:
                        keys(i, 1 + g // 2, 0)
                if more and g >= XT_AT:
                    tokens_lo(nxt, 2 * (g - XT_AT))
                if g >= 2:
                    attended(i, g - 2)
                if g < len(WITH_GROUP) and g % 2 == 1:
                    keys(i, 1 + g // 2, 1)
                if g == 1:
                    v_tile(i, 3)
                if first_step(i) and g == 2:
                    weight_lo(WOUT)
                if more and g == LN_AT:
                    moment_of(nxt, BLOCK_TILES - 1)
                    moments_of(nxt)
                if more and g >= XT_AT:
                    tokens_lo(nxt, 2 * (g - XT_AT) + 1)
            attended(i, GROUPS_A - 2)
            turned(i, GROUPS_A - 1)
            if more:
                queries(nxt, 0)
            else:
                norm2.moments_of(dve, 0)
            add_out(i, 0)
            if more:
                keys(nxt, 0, 0)
                keys(nxt, 0, 1)
            add_out(i, 1)
            attended(i, GROUPS_A - 1)
            if more:
                maxima(nxt, 0)
            else:
                add_out(i, 2)
                add_out(i, 3)

        for part in (k_hi, k_lo):
            dve.memset(flat(part).bitcast(F32), 0.0).then_inc(keys_clear, 1)
        look_up(0)
        weight_lo(UP)
        low(0)
        weight_lo(WQ)
        for t in range(BLOCK_TILES):
            moment_of(0, t)
        moments_of(0)
        normalise(0)
        weight_lo(WK)
        for k in range(KT):
            tokens_lo(0, k)
        weight_lo(WV)
        dve.wait_ge(bias_in, 3 * 16)
        dve.wait_ge(keys_clear, 2)
        queries(0, 0)
        keys(0, 0, 0)
        keys(0, 0, 1)
        maxima(0, 0)
        step(0, True)
        with dve.Fori(1, STEPS - 1) as i:
            step(i, True)
        step(STEPS - 1, False)

    @block.sync
    def _(sp):
        sp.dma_start(tok[:, :], a["tokens"]).then_inc(tok_in, 16)
        sp.dma_start(ident[:, :], a["c_ident"]).then_inc(ident_in, 16)
        for half in range(2):
            sp.dma_start(up_in[half * RANK:(half + 1) * RANK, :], a["up_t"]).then_inc(weight_in[UP], 16)
        sp.dma_start(bias_out[:, :], a["b_out"].broadcast_to([P, HID])).then_inc(bias_in, 16)
        sp.dma_start(bias_qk[:, :], a["b_qk"]).then_inc(bias_in, 16)
        sp.dma_start(bias_v[:, :], a["b_v"]).then_inc(bias_in, 16)
        w_in = a["w_in_t"].rearrange("(k p) n -> p k n", p=P)
        for n, w in enumerate((WQ, WK, WV)):
            if w == WK:
                sp.wait_ge(gathered_0, 16 * BLOCK_TILES)
            sp.dma_start(third(win_in, n), third(w_in, n)).then_inc(weight_in[w], 16)
        sp.dma_start(mask_in[:, :], a["c_mask"]).then_inc(mask_loaded, 16)
        sp.dma_start(wout_in[:, :, :], a["w_out_t"].rearrange("(k p) n -> p k n", p=P)).then_inc(weight_in[WOUT], 16)
        sp.wait_ge(proj_done, STEPS * JOBS)
        splines.load(sp)


def first_step(i):
    return isinstance(i, int) and i == 0


def raw(nc, name, shape):
    with nc.sbuf_tensor(name, shape, F32) as t:
        return t


def flat(t):
    names = " ".join("abcd"[:len(t.shape) - 1])
    return t[(slice(None),) * len(t.shape)].rearrange(f"p {names} -> p ({names})")


def weighted(engine, link, term, dst, points_of, table_of, taps, shape):
    t = term[:, 0:int(np.prod(shape))].rearrange("p (a b c) -> p a b c", a=shape[0], b=shape[1])
    link(engine.tensor_tensor(dst, points_of(0), table_of(0), ALU.mult))
    for m in range(1, taps):
        link(engine.tensor_tensor(t, points_of(m), table_of(m), ALU.mult))
        link(engine.tensor_tensor(dst, dst, t, ALU.add))


class SecondNorm:

    def __init__(self, nc, ctx, sems, h_all):
        def sb(name, shape):
            return ctx.enter_context(nc.sbuf_tensor(name, shape, F32))

        self.h_all = h_all
        self.stats = sb("stats2", [P, BLOCK_TILES, 6])
        self.mean_var = sb("mean_var2", [P, BLOCK_TILES, 2])
        self.var_eps = sb("var_eps2", [P, BLOCK_TILES])
        self.minus_half = sb("minus_half2", [P, BLOCK_TILES])
        self.rstd = sb("rstd2", [P, BLOCK_TILES])
        self.stat_ready, self.rstd_ready, self.x_ready, self.dve_a, self.pool_a, self.dve_tick, self.pool_tick = sems(
            "stat_ready2", "rstd_ready2", "x_ready2", "dve_a2", "pool_a2", "dve_tick2", "pool_tick2")

    def h_row(self, i, t):
        return self.h_all[:, bass.ds(i * BLOCK_TILES + t, 1), :].rearrange("p a n -> p (a n)")

    def moments_of(self, dve, i):
        for t in range(BLOCK_TILES):
            dve.bn_stats(self.stats[:, t, :], self.h_row(i, t)).then_inc(self.dve_a, 1)
        for t in range(BLOCK_TILES):
            dve.wait_ge(self.dve_a, i * BLOCK_TILES + t + 1)
            apart(dve, self.dve_tick)
            ins = dve.bn_aggr(self.mean_var[:, t, :], self.stats[:, t, :])
        ins.then_inc(self.stat_ready, 1)

    def rstd_of(self, pool, i):
        if first_step(i):
            pool.memset(self.minus_half[:, :], -0.5)
        pool.wait_ge(self.stat_ready, i + 1)
        apart(pool, self.pool_tick)
        pool.tensor_scalar(self.var_eps[:, :], self.mean_var[:, :, 1], EPS, None, ALU.add).then_inc(self.pool_a, 1)
        pool.wait_ge(self.pool_a, i + 1)
        pool.tensor_tensor(self.rstd[:, :], self.var_eps[:, :], self.minus_half[:, :],
                           ALU.pow).then_inc(self.rstd_ready, 1)

    def normalise(self, dve, i, x, tiles=range(BLOCK_TILES)):
        dve.wait_ge(self.rstd_ready, i + 1)
        whole = (WINDOWS - 1) * PITCH
        late = HID - whole - (GROUPS - 1) * WIN
        for t in tiles:
            row = self.h_row(i, t)
            by_window = x[:, t, :].rearrange("p (g c j) -> p c g j", g=GROUPS, c=WINDOWS)
            pieces = (
                (by_window[:, 0:WINDOWS - 1, :, :],
                 row[:, 0:whole].rearrange("p (c w) -> p c w", w=PITCH)[:, :, 0:P]
                 .rearrange("p c (g j) -> p c g j", j=WIN)),
                (by_window[:, WINDOWS - 1, 0:GROUPS - 1, :],
                 row[:, whole:whole + (GROUPS - 1) * WIN].rearrange("p (g j) -> p g j", j=WIN)),
                (x[:, t, HID - WIN:HID - WIN + late], row[:, HID - late:HID]),
                (x[:, t, HID - WIN + late:HID], row[:, 0:whole].rearrange("p (c w) -> p c w", w=PITCH)[:, :, PITCH - 1]),
            )
            for dst, src in pieces:
                ins = dve.tensor_scalar(dst, src, self.mean_var[:, t, 0:1], self.rstd[:, t:t + 1], ALU.subtract,
                                        ALU.mult)
            ins.then_inc(self.x_ready, 1)


NAMES = ("gate", "up")


class Splines:

    def __init__(self, nc, a, sems, d_starts):
        self.size = 0
        with ExitStack() as ctx:
            def sb(name, shape, dt=F32):
                self.size += 4 * int(np.prod(shape[1:]))
                return ctx.enter_context(nc.sbuf_tensor(name, shape, dt))

            def twice(name, shape):
                loaded = raw(nc, name + "_in", shape)
                return loaded, sb(name, shape, F32R)

            self.d_side = sb("d_side", [P, MT, HID // 4], U32)
            self.psi = sb("psi", [P, 4, MT, SEGS, DEG])
            self.phi = sb("phi", [P, 5, MT, WINDOWS])
            self.points = {w: sb(f"{w}_points", [P, MT, G_WIN]) for w in NAMES}
            self.d_eval_in, self.d_eval = twice("d_eval", [STACK, MT, 2, P])
            self.d_psi = sb("d_psi", [P, 4, KT, D_SEGS, DEG])
            assert 4 * 4 * INTER <= self.size
            self.d_points = sb("d_points", [P, KT, D_WIN])
            self.d_coef = sb("d_coef", [P, KT, D_SEGS * DEG])
            self.term = sb("term", [P, MT * MOM])
            self.coef = {w: sb(f"{w}_coef", [P, MT, FEAT]) for w in NAMES}
            assert 4 * (4 * INTER + BLOCK_TILES * HID) <= self.size
            self.d_thrice = sb("d_thrice", [P, GM, KT, 3, FEAT])
            self.d_stack = sb("d_stack", [STACK, GM, HID], F32R)
            self.gate_thrice = sb("gate_thrice", [P, MT, 3, FEAT])
        self.a, self.d_starts = a, d_starts
        (self.table_in, self.eval_in, self.matrices_ready, self.d_coef_done, self.d_laid_out, self.coef_done,
         self.laid_out, self.down_link, self.link) = sems(
            "table_in", "eval_in", "matrices_ready", "d_coef_done", "d_laid_out", "coef_done", "laid_out",
            "down_link", "link")

    def load(self, sp):
        a = self.a
        tables = ((self.d_psi, "c_dpsi"), (self.d_points, "down_points"), (self.psi, "c_psi"), (self.phi, "c_phi"),
                  (self.points["gate"], "gate_points"), (self.points["up"], "up_points"))
        for dst, name in tables:
            sp.dma_start(flat(dst), a[name]).then_inc(self.table_in, 16)
        matrices = ((flat(self.d_eval_in), "c_deval"), (flat(self.d_side), "c_dside"))
        for dst, name in matrices:
            sp.dma_start(dst, a[name]).then_inc(self.eval_in, 16)

    def as_parts(self, act):
        act.wait_ge(self.eval_in, 16 * 2)
        act.activation(flat(self.d_eval), flat(self.d_eval_in), ACT.Copy).then_inc(self.matrices_ready, 1)

    def lay_out_down(self, act):
        act.wait_ge(self.d_coef_done, 1)
        for r, first in enumerate(self.d_starts):
            act.activation(self.d_thrice[:, r, :, :, :], self.d_coef[:, :, DEG * first:DEG * first + FEAT]
                           .unsqueeze(2).broadcast_to([P, KT, 3, FEAT]), ACT.Copy).then_inc(self.d_laid_out, 1)
        self.lay_out(act, "gate", self.gate_thrice)

    def lay_out(self, act, w, thrice):
        act.wait_ge(self.coef_done, NAMES.index(w) + 1)
        act.activation(thrice[:, :, :, :], self.coef[w][:, :, :].unsqueeze(2).broadcast_to([P, MT, 3, FEAT]),
                       ACT.Copy).then_inc(self.laid_out, 1)

    def down_coefficients(self, pool):
        link = chained(pool, self.down_link)
        pool.wait_ge(self.table_in, 16 * 6)
        weighted(pool, link, self.term, self.d_coef[:, :, :].rearrange("p k (s d) -> p k s d", d=DEG),
                 lambda m: self.d_points[:, :, m:m + D_SEGS].unsqueeze(3).broadcast_to([P, KT, D_SEGS, DEG]),
                 lambda m: self.d_psi[:, m, :, :, :], 4, (KT, D_SEGS, DEG))
        pool.sem_inc(self.d_coef_done, 1)

    def coefficients(self, pool):
        link = chained(pool, self.link)
        for w in NAMES:
            link(pool.memset(self.coef[w][:, :, MOM + WINDOWS:], 0.0))
            weighted(pool, link, self.term, self.coef[w][:, :, 0:MOM].rearrange("p m (s d) -> p m s d", d=DEG),
                     lambda m: self.points[w][:, :, m:m + SEGS].unsqueeze(3).broadcast_to([P, MT, SEGS, DEG]),
                     lambda m: self.psi[:, m, :, :, :], 4, (MT, SEGS, DEG))
            weighted(pool, link, self.term, self.coef[w][:, :, MOM:MOM + WINDOWS].unsqueeze(3),
                     lambda m: self.points[w][:, :, m:m + WINDOWS].unsqueeze(3),
                     lambda m: self.phi[:, m, :, :].unsqueeze(3), 5, (MT, WINDOWS, 1))
            pool.sem_inc(self.coef_done, 1)


def ffn(nc, a, out, ctx, sems, bank, h_all, ident, splines, norm2):
    def sb(name, shape, dt=F32, where=ctx):
        return where.enter_context(nc.sbuf_tensor(name, shape, dt))

    near_hi, near_lo = {}, {}
    for w in NAMES:
        near_hi[w], near_lo[w] = (sb(f"{w}_near_{part}", [P, INTER], F32R) for part in ("hi", "lo"))
    x = sb("x2", [P, BLOCK_TILES, HID])
    xt_hi = sb("x2t_hi", [P, KT, BLOCK], F32R)
    xt_lo = sb("x2t_lo", [P, KT, BLOCK], F32R)
    feat = sb("feat", [STACK, GROUPS, BLOCK], F32R)
    far = {w: sb(f"{w}_far", [STACK, INTER], F32R) for w in NAMES}
    basis_hi_in = raw(nc, "basis_hi_in", [P, GROUPS, KT, STACK])
    basis_hi = sb("basis_hi", [P, GROUPS, KT, STACK], F32R)
    basis_lo_in = raw(nc, "basis_lo_in", [P, GROUPS, KT, STACK])
    basis_lo = sb("basis_lo", [P, GROUPS, KT, STACK], F32R)
    down_hi = sb("down_hi", [P, MT, HID], F32R)
    down_lo = sb("down_lo", [P, MT, HID], F32R)
    W_BUFS = 3
    (xt_mm, xt_hi_done, xt_done, feat_mm, feat_hi, feat_done, gu_mm, silu_done, prod_done, act_hi_done, act_done,
     down_mm, out_ready, stored, basis_ready) = sems(
        "xt_mm2", "xt_hi_done2", "xt_done2", "feat_mm", "feat_hi", "feat_done", "gu_mm", "silu_done", "prod_done",
        "act_hi_done", "act_done", "down_mm", "out_ready", "stored",
        "basis_ready")
    h_row, x_ready = norm2.h_row, norm2.x_ready
    acc = bank[0:4]
    front = bank[4:8]

    def own_bank(i, g):
        return bank[g % 2] if first_step(i) else front[g]

    def turn_tokens(pe, i, g):
        if first_step(i) and g >= 2:
            pe.wait_ge(xt_done, g - 1)
        for t in range(BLOCK_TILES):
            mm = pe.transpose(own_bank(i, g)[:, t * P:(t + 1) * P], x[:, t, g * P:(g + 1) * P], ident[:, :])
        mm.then_inc(xt_mm, 1)

    def make_features(pe, i, g):
        if g == 0:
            pe.wait_ge(xt_done, i * KT + KT)
        if first_step(i) and g >= 2:
            pe.wait_ge(feat_done, g - 1)
        for k in range(KT):
            for n, (w, y) in enumerate(((basis_hi, xt_hi), (basis_hi, xt_lo), (basis_lo, xt_hi))):
                mm = pe.matmul(own_bank(i, g)[0:STACK, :], w[:, g, k, :], y[:, k, :], start=(k == 0 and n == 0),
                               stop=(k == KT - 1 and n == 2))
        mm.then_inc(feat_mm, 1)

    def tokens_hi(act, i, g):
        act.wait_ge(xt_mm, i * KT + g + 1)
        act.activation(xt_hi[:, g, :], own_bank(i, g)[:, :], ACT.Copy).then_inc(xt_hi_done, 1)

    def features_hi(act, i, g):
        act.wait_ge(feat_mm, i * GROUPS + g + 1)
        act.activation(feat[:, g, :], own_bank(i, g)[0:STACK, :], ACT.Copy).then_inc(feat_hi, 1)

    def tokens_lo(dve, i, g):
        dve.wait_ge(xt_hi_done, i * KT + g + 1)
        dve.tensor_tensor(xt_lo[:, g, :], own_bank(i, g)[:, :], xt_hi[:, g, :].bitcast(F32),
                          ALU.subtract).then_inc(xt_done, 1)

    def features_lo(dve, i, g):
        mid = slice(FEAT, 2 * FEAT)
        dve.wait_ge(feat_hi, i * GROUPS + g + 1)
        dve.tensor_tensor(feat[mid, g, :], own_bank(i, g)[mid, :], feat[mid, g, :].bitcast(F32),
                          ALU.subtract).then_inc(feat_done, 1)

    LN_AT, BASIS_AT = 9, (14, 16)

    with ExitStack() as gen:
        w_f = sb("w_f", [P, W_BUFS, 512], where=gen)
        evaluate_in = raw(nc, "evaluate_in", [STACK, GROUPS, 2, P])
        evaluate = sb("evaluate", [STACK, GROUPS, 2, P], F32R, where=gen)
        side = sb("side", [P, INTER // 4], U32, where=gen)
        thrice = {"gate": splines.gate_thrice, "up": sb("up_thrice", [P, MT, 3, FEAT], where=gen)}
        (basis_in, eval_in, eval_ready, turn_mm, far_hi, far_lo, evaluated, copied, picked, hi_done, lo_vector,
         lo_pool) = sems(
            "basis_in", "g_eval_in", "g_eval_ready", "turn_mm", "far_hi", "far_lo", "evaluated", "copied", "picked",
            "w_hi", "lo_vector", "lo_pool")

        turns = [([splines.d_thrice[:, r, k, :, :] for k in range(KT)], splines.d_stack[:, r, :]) for r in range(GM)]
        jobs = [(m % GM, splines.d_stack[:, m % GM, :], splines.d_eval[:, m, :, :],
                 splines.d_side[:, m, :].bitcast(U8), down_hi[:, m, :], down_lo[:, m, :]) for m in range(MT)]
        for w in NAMES:
            for g in range(GROUPS):
                n = slice(g * INTER // GROUPS, (g + 1) * INTER // GROUPS)
                jobs.append((len(turns), far[w][:, n], evaluate[:, g, :, :],
                             side[:, n.start // 4:n.stop // 4].bitcast(U8), near_hi[w][:, n], near_lo[w][:, n]))
                turns.append(([thrice[w][:, g * GM + m, :, :] for m in range(GM)], far[w][:, n]))

        def schedule(turn, job, turned, features):
            for t in range(GM):
                turn(t)
            for j in range(len(jobs)):
                if j % 2 == 0 and GM + j // 2 < len(turns):
                    turn(GM + j // 2)
                job(j)
                if MT <= j < MT + KT:
                    turned(0, j - MT)
                elif MT + KT <= j:
                    features(0, j - MT - KT)

        def turn_bank(t):
            return bank[(0, 1, 6, 7)[t]] if t < GM else bank[t % 2]

        def rest_done(j):
            return (lo_vector, j // 6 + 1) if j % 6 == 5 else (lo_pool, j + 1 - (j + 1) // 6)

        def rest(engine, j):
            engine.wait_ge(hi_done, j + 1)
            engine.tensor_tensor(jobs[j][5], w_f[:, j % W_BUFS, :], jobs[j][4].bitcast(F32),
                                 ALU.subtract).then_inc(rest_done(j)[0], 1)

        block = gen.enter_context(nc.Block())

        @block.sync
        def _(sp):
            sp.dma_start(flat(evaluate_in), a["c_evaluate"]).then_inc(eval_in, 16)
            sp.dma_start(side[:, :], a["c_side"]).then_inc(eval_in, 16)
            for dst, name in ((basis_hi_in, "c_basis_hi"), (basis_lo_in, "c_basis_lo")):
                sp.dma_start(flat(dst), a[name]).then_inc(basis_in, 16)

        @block.tensor
        def _(pe):
            def turn(t):
                if t < GM:
                    pe.wait_ge(splines.d_laid_out, t + 1)
                if t >= GM:
                    pe.wait_ge(far_lo, t - 1)
                if t >= GM:
                    pe.wait_ge(splines.laid_out, (t - GM) // GROUPS + 1)
                for n, rows in enumerate(turns[t][0]):
                    mm = pe.transpose(turn_bank(t)[0:STACK, n * P:(n + 1) * P],
                                      rows.rearrange("p c f -> p (c f)"), ident[:, :])
                mm.then_inc(turn_mm, 1)

            def job(j):
                t, coefs, matrices = jobs[j][0:3]
                pe.wait_ge(far_lo, t + 1)
                if j == MT:
                    pe.wait_ge(eval_ready, 1)
                if j == 2:
                    pe.wait_ge(far_lo, GM)
                if j >= 3:
                    pe.wait_ge(picked, j - 2)
                for x in range(2):
                    mm = pe.matmul(bank[2 + 2 * (j % 3) + x][:, :], matrices[:, x, :], coefs, start=True, stop=True)
                mm.then_inc(evaluated, 1)

            def turned(i, g):
                if g == 0:
                    pe.wait_ge(far_lo, len(turns))
                    pe.wait_ge(x_ready, BLOCK_TILES)
                turn_tokens(pe, i, g)

            def features(i, g):
                if g == 0:
                    pe.wait_ge(basis_ready, 2)
                make_features(pe, i, g)

            pe.wait_ge(splines.matrices_ready, 1)
            schedule(turn, job, turned, features)

        @block.scalar
        def _(act):
            def turn(t):
                act.wait_ge(turn_mm, t + 1)
                act.activation(turns[t][1], turn_bank(t)[0:STACK, :], ACT.Copy).then_inc(far_hi, 1)
                if t == GM - 1:
                    splines.lay_out(act, "up", thrice["up"])

            def copy_hi(j):
                act.wait_ge(picked, j + 1)
                act.activation(jobs[j][4], w_f[:, j % W_BUFS, :], ACT.Copy).then_inc(hi_done, 1)

            def job(j):
                act.wait_ge(evaluated, j + 1)
                if j >= W_BUFS:
                    act.wait_ge(*rest_done(j - W_BUFS))
                act.activation(w_f[:, j % W_BUFS, :], bank[2 + 2 * (j % 3)][:, :], ACT.Copy).then_inc(copied, 1)
                if j > 0:
                    copy_hi(j - 1)
                if j == MT - 2:
                    act.wait_ge(eval_in, 32)
                    act.activation(flat(evaluate), flat(evaluate_in), ACT.Copy).then_inc(eval_ready, 1)

            def turned(i, g):
                tokens_hi(act, i, g)

            def features(i, g):
                features_hi(act, i, g)

            schedule(turn, job, turned, features)
            copy_hi(len(jobs) - 1)

        @block.vector
        def _(dve):
            def turn(t):
                low = slice(2 * FEAT, STACK)
                dve.wait_ge(far_hi, t + 1)
                dve.tensor_tensor(turns[t][1][low, :], turn_bank(t)[low, :], turns[t][1][low, :].bitcast(F32),
                                  ALU.subtract).then_inc(far_lo, 1)

            def job(j):
                if j == MT:
                    dve.wait_ge(eval_in, 32)
                dve.wait_ge(copied, j + 1)
                dve.copy_predicated(w_f[:, j % W_BUFS, :], jobs[j][3],
                                    bank[3 + 2 * (j % 3)][:, :]).then_inc(picked, 1)
                if j > 0 and (j - 1) % 6 == 5:
                    rest(dve, j - 1)
                if j == LN_AT:
                    dve.wait_ge(splines.laid_out, len(NAMES))
                if LN_AT <= j < LN_AT + BLOCK_TILES:
                    norm2.normalise(dve, 0, x, [j - LN_AT])
                if j in BASIS_AT:
                    dve.wait_ge(basis_in, 32)
                    src, dst = ((basis_hi_in, basis_hi), (basis_lo_in, basis_lo))[BASIS_AT.index(j)]
                    dve.tensor_copy(flat(dst), flat(src)).then_inc(basis_ready, 1)

            dve.wait_ge(splines.eval_in, 16 * 2)
            def turned(i, g):
                tokens_lo(dve, i, g)

            def features(i, g):
                features_lo(dve, i, g)

            schedule(turn, job, turned, features)
            rest(dve, len(jobs) - 1)

        @block.gpsimd
        def _(pool):
            for j in range(len(jobs)):
                if j % 6 != 5:
                    rest(pool, j)

    act_f = sb("act_f", [P, 2, BLOCK])
    act_hi = sb("act_hi", [P, 2, BLOCK], F32R)
    act_lo = sb("act_lo", [P, 2, BLOCK], F32R)

    block = ctx.enter_context(nc.Block())


    @block.tensor
    def _(pe):
        def step(i, more):
            if not first_step(i):
                for g in range(GROUPS):
                    make_features(pe, i, g)

            def gate_up(m):
                g = m // GM
                if m < 2:
                    pe.wait_ge(feat_done, i * GROUPS + 2 * m + 2)
                elif m % GM == 0:
                    pe.wait_ge(feat_done, i * GROUPS + g + 1)
                if m >= 2:
                    pe.wait_ge(prod_done, i * MT + m - 1)
                cols = slice(m * P, (m + 1) * P)
                for n, w in enumerate(NAMES):
                    o = front[2 * (m % 2) + n][:, :]
                    pe.matmul(o, near_hi[w][:, cols], xt_hi[:, g, :], start=True, stop=False)
                    pe.matmul(o, near_lo[w][:, cols], xt_hi[:, g, :], start=False, stop=False)
                    pe.matmul(o, near_hi[w][:, cols], xt_lo[:, g, :], start=False, stop=False)
                    mm = pe.matmul(o, far[w][:, cols], feat[:, g, :], start=False, stop=True)
                mm.then_inc(gu_mm, 1)

            def down(m):
                pe.wait_ge(act_done, i * MT + m + 1)
                for t in range(BLOCK_TILES):
                    tk = slice(t * P, (t + 1) * P)
                    first, last = m == 0, m == MT - 1
                    if first and not first_step(i):
                        pe.wait_ge(out_ready, i * BLOCK_TILES + t - BLOCK_TILES + 1)
                    pe.matmul(acc[t][:, :], act_hi[:, m % 2, tk], down_hi[:, m, :], start=first, stop=False)
                    pe.matmul(acc[t][:, :], act_lo[:, m % 2, tk], down_hi[:, m, :], start=False, stop=False)
                    mm = pe.matmul(acc[t][:, :], act_hi[:, m % 2, tk], down_lo[:, m, :], start=False, stop=last)
                mm.then_inc(down_mm, 1)

            for m in range(MT + 2):
                if m < MT:
                    gate_up(m)
                elif more:
                    n = m - MT
                    if n == 0:
                        pe.wait_ge(x_ready, (i + 1) * BLOCK_TILES + BLOCK_TILES)
                    pe.wait_ge(prod_done, i * MT + MT - 1 + n)
                    turn_tokens(pe, i + 1, 2 * n)
                    turn_tokens(pe, i + 1, 2 * n + 1)
                if m >= 2:
                    down(m - 2)

        step(0, True)
        with pe.Fori(1, STEPS - 1) as i:
            step(i, True)
        step(STEPS - 1, False)

    @block.scalar
    def _(act):
        def step(i, more):
            if not first_step(i):
                for g in range(GROUPS):
                    features_hi(act, i, g)

            def copy_hi(m):
                act.wait_ge(prod_done, i * MT + m + 1)
                if m >= 2 or not first_step(i):
                    act.wait_ge(down_mm, i * MT + m - 1)
                act.activation(act_hi[:, m % 2, :], act_f[:, m % 2, :], ACT.Copy).then_inc(act_hi_done, 1)

            for m in range(MT):
                act.wait_ge(gu_mm, i * MT + m + 1)
                if m >= 2:
                    act.wait_ge(act_done, i * MT + m - 1)
                act.activation(act_f[:, m % 2, :], front[2 * (m % 2)][:, :], ACT.Silu).then_inc(silu_done, 1)
                if m > 0:
                    copy_hi(m - 1)
            copy_hi(MT - 1)
            if more:
                for g in range(KT):
                    tokens_hi(act, i + 1, g)

        step(0, True)
        with act.Fori(1, STEPS - 1) as i:
            step(i, True)
        step(STEPS - 1, False)

    @block.gpsimd
    def _(pool):
        with pool.Fori(1, STEPS) as i:
            norm2.rstd_of(pool, i)

    @block.vector
    def _(dve):
        def step(i, more):
            if not first_step(i):
                for g in range(GROUPS):
                    features_lo(dve, i, g)

            def split_lo(m):
                dve.wait_ge(act_hi_done, i * MT + m + 1)
                dve.tensor_tensor(act_lo[:, m % 2, :], act_f[:, m % 2, :], act_hi[:, m % 2, :].bitcast(F32),
                                  ALU.subtract).then_inc(act_done, 1)

            for m in range(MT):
                dve.wait_ge(silu_done, i * MT + m + 1)
                dve.tensor_tensor(act_f[:, m % 2, :], act_f[:, m % 2, :], front[2 * (m % 2) + 1][:, :],
                                  ALU.mult).then_inc(prod_done, 1)
                if m > 0:
                    split_lo(m - 1)
                if more and m == MT // 2:
                    norm2.moments_of(dve, i + 1)
                if more and m == MT // 2 + 3:
                    norm2.normalise(dve, i + 1, x)
            split_lo(MT - 1)
            if more:
                for g in range(KT):
                    tokens_lo(dve, i + 1, g)
            dve.wait_ge(down_mm, i * MT + MT)
            for t in range(BLOCK_TILES):
                dve.tensor_tensor(h_row(i, t), acc[t][:, :], h_row(i, t), ALU.add).then_inc(out_ready, 1)

        step(0, True)
        with dve.Fori(1, STEPS - 1) as i:
            step(i, True)
        step(STEPS - 1, False)

    @block.sync
    def _(sp):
        rows = out.rearrange("b s d -> (b s) d")
        with sp.Fori(0, STEPS) as i:
            for t in range(BLOCK_TILES):
                sp.wait_ge(out_ready, i * BLOCK_TILES + t + 1)
                sp.dma_start(rows[bass.ds(i * BLOCK + t * P, P), :], h_row(i, t)).then_inc(stored, 16)
        sp.wait_ge(stored, 16 * TILES)



def kernel(x, L0_tok_embed_low, L0_tok_project_up, L0_attn_W_in, L0_attn_b_in, L0_attn_W_out, L0_attn_b_out,
           L0_ffn_gate_cp, L0_ffn_up_cp, L0_ffn_down_cp):
    import concourse.bacc as bacc
    from concourse.bass_utils import run_bass_kernel_spmd

    tables, gate_starts, down_starts, d_starts = _tables()
    b_in = np.asarray(L0_attn_b_in)
    arrays = {
        "tokens": np.ascontiguousarray(np.asarray(x).reshape(TILES, P).T).view(np.uint32),
        "embed": np.asarray(L0_tok_embed_low),
        "up_t": np.ascontiguousarray(np.asarray(L0_tok_project_up).T),
        "w_in_t": np.ascontiguousarray(np.asarray(L0_attn_W_in).T),
        "w_out_t": np.ascontiguousarray(np.asarray(L0_attn_W_out).T),
        "b_qk": np.ascontiguousarray(b_in[:2 * HID].reshape(2 * KT, P).T),
        "b_v": np.ascontiguousarray(b_in[2 * HID:].reshape(KT, P).T),
        "b_out": np.asarray(L0_attn_b_out).reshape(1, HID),
        "gate_points": _windows(np.asarray(L0_ffn_gate_cp), gate_starts, G_WIN, MT),
        "up_points": _windows(np.asarray(L0_ffn_up_cp), gate_starts, G_WIN, MT),
        "down_points": _windows(np.asarray(L0_ffn_down_cp), down_starts, D_WIN, KT),
        **tables,
    }
    nc = bacc.Bacc("TRN2", target_bir_lowering=False, num_devices=1)
    aps = {n: nc.dram_tensor(f"in_{n}", v.shape, mybir.dt.from_np(v.dtype), kind="ExternalInput").ap()
           for n, v in arrays.items()}
    out = nc.dram_tensor("out", (BATCH, SEQ, HID), F32, kind="ExternalOutput").ap()
    build(nc, aps, out, d_starts)
    return run_bass_kernel_spmd(nc, [{f"in_{n}": v for n, v in arrays.items()}], core_ids=[0]).results[0]["out"]
```
